# Optimizing a Trainium2 kernel written in Bass

```python
import numpy as np
import jax
import jax.numpy as jnp

def _softmax(x, axis=-1):
    return jax.nn.softmax(x, axis=axis)

def _gelu(x):
    return jax.nn.gelu(x, approximate=True)

def _silu(x):
    return jax.nn.silu(x)

def _sigmoid(x):
    return jax.nn.sigmoid(x)

def _layernorm(x, axis=-1, eps=1e-05):
    m = jnp.mean(x, axis=axis, keepdims=True)
    v = jnp.var(x, axis=axis, keepdims=True)
    return (x - m) / jnp.sqrt(v + eps)

def _scatter_add(tgt, idx, src, axis=0):
    return tgt.at[idx].add(src)

def _segment_sum(src, seg, n):
    return jax.ops.segment_sum(src, seg, n)
kernel_name = 'mk_flamingo_gated_d2_seqx_r4_5d0475'

def setup_inputs(seed: int=0):
    np.random.seed(seed)
    _w = jnp.asarray

    def _rec_inputs():
        import jax
        import jax.numpy as jnp
        _rk = jax.random.key(seed)
        x = -0.0002928 + 1 * jax.random.normal(jax.random.fold_in(_rk, 1), (1, 2048, 256), jnp.float32)
        _lenS = 2048 - jax.random.randint(jax.random.fold_in(_rk, 7), (1,), 0, max(1, 2048 // 4) + 1, jnp.int32)
        _lenS2 = 1601 - jax.random.randint(jax.random.fold_in(_rk, 8), (1,), 0, max(1, 1601 // 4) + 1, jnp.int32)
        _ctx_1024P = jax.random.normal(jax.random.fold_in(_rk, 11), (1, 16, 256), jnp.float32)
        _ctx_1024c = jax.random.dirichlet(jax.random.fold_in(_rk, 511), 0.3 * jnp.ones((16,), jnp.float32), (1, 1601))
        _ctx_1024t = jnp.einsum('bsk,bkd->bsd', _ctx_1024c, _ctx_1024P)
        _ctx_1024t = _ctx_1024t * jax.lax.rsqrt(jnp.mean(jnp.square(_ctx_1024t)) + 1e-12) * 0.953939
        ctx_1024 = -1.39393e-06 + 0.999914 * (_ctx_1024t + 0.3 * jax.random.normal(jax.random.fold_in(_rk, 611), (1, 1601, 256), jnp.float32))
        _g = jax.random.normal(jax.random.fold_in(_rk, 9001), (2, 2), jnp.float32)
        _g = jnp.sign(_g) * jnp.maximum(jnp.abs(_g), 1.0) + (_g == 0) * 1.0
        g_xattn = _g[0]
        g_ffn = _g[1]
        return (x, ctx_1024, g_xattn, g_ffn)
    x, ctx_1024, g_xattn, g_ffn = _rec_inputs()

    def _L0_xattn_setup():
        import jax, jax.numpy as jnp
        import numpy as np
        B, S, SC, E, H = (2, 512, 512, 256, 16)
        D = E // H
        EPS = 1e-06

        def _layernorm(x, g, b):
            m = jnp.mean(x, axis=-1, keepdims=True)
            v = jnp.mean((x - m) ** 2, axis=-1, keepdims=True)
            return (x - m) / jnp.sqrt(v + EPS) * g + b

        def _mha(xk, xv, xq, Wk, Wv, Wq, Wo, bo, masked):
            K = jnp.einsum('bse,hed->bhsd', xk, Wk)
            V = jnp.einsum('bse,hed->bhsd', xv, Wv)
            Q = jnp.einsum('bqe,hed->bhqd', xq, Wq)
            scores = jnp.einsum('bhqd,bhkd->bhqk', Q, K)
            sk = xk.shape[1]
            if masked:
                causal = jnp.triu(jnp.ones((xq.shape[1], sk), dtype=bool), k=1)
                scores = jnp.where(causal, -jnp.inf, scores)
            att = jax.nn.softmax(scores / jnp.sqrt(jnp.asarray(sk, scores.dtype)), axis=-1)
            out = jnp.einsum('bhqk,bhkd->bhqd', att, V)
            out = out.transpose(0, 2, 1, 3).reshape(out.shape[0], out.shape[2], -1)
            return jax.nn.relu(out @ Wo + bo)
        key = jax.random.key(seed)
        ks = jax.random.split(key, 16)
        w = lambda k, shape: jax.random.normal(k, shape, jnp.float32) * 0.02
        return {'inputs': jax.random.normal(ks[0], (B, S, E), jnp.float32), 'context_seq': jax.random.normal(ks[1], (B, SC, E), jnp.float32), 'Wk1': w(ks[2], (H, E, D)), 'Wv1': w(ks[3], (H, E, D)), 'Wq1': w(ks[4], (H, E, D)), 'Wo1': w(ks[5], (E, E)), 'bo1': jnp.zeros((E,), jnp.float32), 'Wk2': w(ks[6], (H, E, D)), 'Wv2': w(ks[7], (H, E, D)), 'Wq2': w(ks[8], (H, E, D)), 'Wo2': w(ks[9], (E, E)), 'bo2': jnp.zeros((E,), jnp.float32), 'Wf': w(ks[10], (E, E)), 'bf': jnp.zeros((E,), jnp.float32), 'g1': jnp.ones((E,), jnp.float32), 'b1': jnp.zeros((E,), jnp.float32), 'g2': jnp.ones((E,), jnp.float32), 'b2': jnp.zeros((E,), jnp.float32), 'g3': jnp.ones((E,), jnp.float32), 'b3': jnp.zeros((E,), jnp.float32)}
    _L0_xattn_all = _L0_xattn_setup()
    _L0_xattn_in = {k: v for k, v in _L0_xattn_all.items() if k in ('Wk1', 'Wv1', 'Wq1', 'Wo1', 'bo1', 'Wk2', 'Wv2', 'Wq2', 'Wo2', 'bo2', 'Wf', 'bf', 'g1', 'b1', 'g2', 'b2', 'g3', 'b3')}
    del _L0_xattn_all

    def _L0_ffn_setup():
        import jax, jax.numpy as jnp
        import numpy as np
        EPS = 1e-05

        def _ln(x, g, b):
            mu = jnp.mean(x, axis=-1, keepdims=True)
            var = jnp.mean(jnp.square(x - mu), axis=-1, keepdims=True)
            return (x - mu) * jax.lax.rsqrt(var + EPS) * g + b

        def _forward(x, index_b, index_t, sw1, sb1, sw2, sb2, sw3, sb3, s_ln_g, s_ln_b, sg_w, sg_b, eg_w, eg_b, exp_bias, ew1, eb1, ew2, eb2, ew3, eb3, sel_ln_g, sel_ln_b):
            x1 = jnp.einsum('btd,hd->bth', x, sw1) + sb1
            x2 = jnp.einsum('btd,hd->bth', x, sw2) + sb2
            sh = _ln(jax.nn.silu(x1) * x2, s_ln_g, s_ln_b)
            shared_out = jnp.einsum('bth,dh->btd', sh, sw3) + sb3
            x_moe = x[index_b, index_t]
            shared_scores = jax.nn.sigmoid(x_moe @ sg_w.T + sg_b)
            expert_scores = jax.nn.sigmoid(x_moe @ eg_w.T + eg_b)
            top1_idx = jnp.argmax(expert_scores + exp_bias, axis=-1)
            top1_score = jnp.take_along_axis(expert_scores, top1_idx[:, None], axis=-1)
            weights = jax.nn.softmax(jnp.concatenate([shared_scores, top1_score], axis=-1), axis=-1)
            shared_w, expert_w = (weights[:, 0], weights[:, 1])
            shared_moe_out = shared_out[index_b, index_t] * shared_w[:, None]
            h1 = jnp.einsum('md,ehd->meh', x_moe, ew1) + eb1
            h2 = jnp.einsum('md,ehd->meh', x_moe, ew2) + eb2
            z = _ln(jax.nn.silu(h1) * h2, sel_ln_g, sel_ln_b)
            out_all = jnp.einsum('meh,edh->med', z, ew3) + eb3
            expert_out = jnp.take_along_axis(out_all, top1_idx[:, None, None], axis=1)[:, 0]
            expert_moe_out = expert_out * expert_w[:, None]
            final_out = shared_out.at[index_b, index_t].set(shared_moe_out + expert_moe_out)
            return final_out
        B, T, D, E, H, M = (2, 512, 256, 8, 128, 512)
        key = jax.random.key(seed)
        ks = jax.random.split(key, 24)
        s = 0.02
        inp = {}
        inp['x'] = jax.random.normal(ks[0], (B, T, D), jnp.float32)
        flat = jnp.arange(M, dtype=jnp.int32) * 2
        inp['index_b'] = flat // T
        inp['index_t'] = flat % T
        inp['sw1'] = jax.random.normal(ks[1], (H, D), jnp.float32) * s
        inp['sb1'] = jnp.zeros((H,), jnp.float32)
        inp['sw2'] = jax.random.normal(ks[2], (H, D), jnp.float32) * s
        inp['sb2'] = jnp.zeros((H,), jnp.float32)
        inp['sw3'] = jax.random.normal(ks[3], (D, H), jnp.float32) * s
        inp['sb3'] = jnp.zeros((D,), jnp.float32)
        inp['s_ln_g'] = jnp.ones((H,), jnp.float32)
        inp['s_ln_b'] = jnp.zeros((H,), jnp.float32)
        inp['sg_w'] = jax.random.normal(ks[4], (1, D), jnp.float32) * s
        inp['sg_b'] = jnp.zeros((1,), jnp.float32)
        inp['eg_w'] = jax.random.normal(ks[5], (E, D), jnp.float32) * s
        inp['eg_b'] = jnp.zeros((E,), jnp.float32)
        inp['exp_bias'] = jnp.zeros((E,), jnp.float32)
        inp['ew1'] = jax.random.normal(ks[6], (E, H, D), jnp.float32) * s
        inp['eb1'] = jnp.zeros((E, H), jnp.float32)
        inp['ew2'] = jax.random.normal(ks[7], (E, H, D), jnp.float32) * s
        inp['eb2'] = jnp.zeros((E, H), jnp.float32)
        inp['ew3'] = jax.random.normal(ks[8], (E, D, H), jnp.float32) * s
        inp['eb3'] = jnp.zeros((E, D), jnp.float32)
        inp['sel_ln_g'] = jnp.ones((H,), jnp.float32)
        inp['sel_ln_b'] = jnp.zeros((H,), jnp.float32)
        return inp
    _L0_ffn_all = _L0_ffn_setup()
    _L0_ffn_in = {k: v for k, v in _L0_ffn_all.items() if k in ('index_b', 'index_t', 'sw1', 'sb1', 'sw2', 'sb2', 'sw3', 'sb3', 's_ln_g', 's_ln_b', 'sg_w', 'sg_b', 'eg_w', 'eg_b', 'exp_bias', 'ew1', 'eb1', 'ew2', 'eb2', 'ew3', 'eb3', 'sel_ln_g', 'sel_ln_b')}
    del _L0_ffn_all

    def _L1_xattn_setup():
        import jax, jax.numpy as jnp
        import numpy as np
        EMB = 256
        HEADS = 16
        HEAD_DIM = EMB // HEADS
        key = jax.random.key(seed)
        ks = jax.random.split(key, 11)
        B, S = (4, 512)
        scale = 1.0 / np.sqrt(EMB)
        inp = {'query': jax.random.normal(ks[0], (B, S, EMB), jnp.float32), 'key': jax.random.normal(ks[1], (B, S, EMB), jnp.float32), 'value': jax.random.normal(ks[2], (B, S, EMB), jnp.float32), 'Wq': jax.random.normal(ks[3], (EMB, EMB), jnp.float32) * scale, 'bq': jnp.zeros((EMB,), jnp.float32), 'Wk': jax.random.normal(ks[4], (EMB, EMB), jnp.float32) * scale, 'bk': jnp.zeros((EMB,), jnp.float32), 'Wv': jax.random.normal(ks[5], (EMB, EMB), jnp.float32) * scale, 'bv': jnp.zeros((EMB,), jnp.float32), 'Wo': jax.random.normal(ks[6], (EMB, EMB), jnp.float32) * scale, 'bo': jnp.zeros((EMB,), jnp.float32)}
        return inp
    _L1_xattn_all = _L1_xattn_setup()
    _L1_xattn_in = {k: v for k, v in _L1_xattn_all.items() if k in ('Wq', 'bq', 'Wk', 'bk', 'Wv', 'bv', 'Wo', 'bo')}
    del _L1_xattn_all

    def _L1_ffn_setup():
        import jax, jax.numpy as jnp
        import numpy as np
        DIM = 256
        HIDDEN = 768
        SCALE = 1.0 / 127.0

        def _dequant(w_int, dtype):
            return w_int.astype(dtype) * jnp.asarray(SCALE, dtype)
        key = jax.random.key(seed)
        k_x, k_g, k_u, k_d = jax.random.split(key, 4)
        x = jax.random.normal(k_x, (4, 512, DIM), dtype=jnp.float32)
        w_gate = jax.random.randint(k_g, (HIDDEN, DIM), -127, 128, dtype=jnp.int32)
        w_up = jax.random.randint(k_u, (HIDDEN, DIM), -127, 128, dtype=jnp.int32)
        w_down = jax.random.randint(k_d, (DIM, HIDDEN), -127, 128, dtype=jnp.int32)
        return {'x': x, 'w_gate': w_gate, 'w_up': w_up, 'w_down': w_down}
    _L1_ffn_all = _L1_ffn_setup()
    _L1_ffn_in = {k: v for k, v in _L1_ffn_all.items() if k in ('w_gate', 'w_up', 'w_down')}
    del _L1_ffn_all
    return {'x': x, 'ctx_1024': ctx_1024, 'g_xattn': g_xattn, 'g_ffn': g_ffn, 'L0_xattn_Wk1': _L0_xattn_in['Wk1'], 'L0_xattn_Wv1': _L0_xattn_in['Wv1'], 'L0_xattn_Wq1': _L0_xattn_in['Wq1'], 'L0_xattn_Wo1': _L0_xattn_in['Wo1'], 'L0_xattn_bo1': _L0_xattn_in['bo1'], 'L0_xattn_Wk2': _L0_xattn_in['Wk2'], 'L0_xattn_Wv2': _L0_xattn_in['Wv2'], 'L0_xattn_Wq2': _L0_xattn_in['Wq2'], 'L0_xattn_Wo2': _L0_xattn_in['Wo2'], 'L0_xattn_bo2': _L0_xattn_in['bo2'], 'L0_xattn_Wf': _L0_xattn_in['Wf'], 'L0_xattn_bf': _L0_xattn_in['bf'], 'L0_xattn_g1': _L0_xattn_in['g1'], 'L0_xattn_b1': _L0_xattn_in['b1'], 'L0_xattn_g2': _L0_xattn_in['g2'], 'L0_xattn_b2': _L0_xattn_in['b2'], 'L0_xattn_g3': _L0_xattn_in['g3'], 'L0_xattn_b3': _L0_xattn_in['b3'], 'L0_ffn_index_b': _L0_ffn_in['index_b'], 'L0_ffn_index_t': _L0_ffn_in['index_t'], 'L0_ffn_sw1': _L0_ffn_in['sw1'], 'L0_ffn_sb1': _L0_ffn_in['sb1'], 'L0_ffn_sw2': _L0_ffn_in['sw2'], 'L0_ffn_sb2': _L0_ffn_in['sb2'], 'L0_ffn_sw3': _L0_ffn_in['sw3'], 'L0_ffn_sb3': _L0_ffn_in['sb3'], 'L0_ffn_s_ln_g': _L0_ffn_in['s_ln_g'], 'L0_ffn_s_ln_b': _L0_ffn_in['s_ln_b'], 'L0_ffn_sg_w': _L0_ffn_in['sg_w'], 'L0_ffn_sg_b': _L0_ffn_in['sg_b'], 'L0_ffn_eg_w': _L0_ffn_in['eg_w'], 'L0_ffn_eg_b': _L0_ffn_in['eg_b'], 'L0_ffn_exp_bias': _L0_ffn_in['exp_bias'], 'L0_ffn_ew1': _L0_ffn_in['ew1'], 'L0_ffn_eb1': _L0_ffn_in['eb1'], 'L0_ffn_ew2': _L0_ffn_in['ew2'], 'L0_ffn_eb2': _L0_ffn_in['eb2'], 'L0_ffn_ew3': _L0_ffn_in['ew3'], 'L0_ffn_eb3': _L0_ffn_in['eb3'], 'L0_ffn_sel_ln_g': _L0_ffn_in['sel_ln_g'], 'L0_ffn_sel_ln_b': _L0_ffn_in['sel_ln_b'], 'L1_xattn_Wq': _L1_xattn_in['Wq'], 'L1_xattn_bq': _L1_xattn_in['bq'], 'L1_xattn_Wk': _L1_xattn_in['Wk'], 'L1_xattn_bk': _L1_xattn_in['bk'], 'L1_xattn_Wv': _L1_xattn_in['Wv'], 'L1_xattn_bv': _L1_xattn_in['bv'], 'L1_xattn_Wo': _L1_xattn_in['Wo'], 'L1_xattn_bo': _L1_xattn_in['bo'], 'L1_ffn_w_gate': _L1_ffn_in['w_gate'], 'L1_ffn_w_up': _L1_ffn_in['w_up'], 'L1_ffn_w_down': _L1_ffn_in['w_down']}

def reference(x, ctx_1024, g_xattn, g_ffn, L0_xattn_Wk1, L0_xattn_Wv1, L0_xattn_Wq1, L0_xattn_Wo1, L0_xattn_bo1, L0_xattn_Wk2, L0_xattn_Wv2, L0_xattn_Wq2, L0_xattn_Wo2, L0_xattn_bo2, L0_xattn_Wf, L0_xattn_bf, L0_xattn_g1, L0_xattn_b1, L0_xattn_g2, L0_xattn_b2, L0_xattn_g3, L0_xattn_b3, L0_ffn_index_b, L0_ffn_index_t, L0_ffn_sw1, L0_ffn_sb1, L0_ffn_sw2, L0_ffn_sb2, L0_ffn_sw3, L0_ffn_sb3, L0_ffn_s_ln_g, L0_ffn_s_ln_b, L0_ffn_sg_w, L0_ffn_sg_b, L0_ffn_eg_w, L0_ffn_eg_b, L0_ffn_exp_bias, L0_ffn_ew1, L0_ffn_eb1, L0_ffn_ew2, L0_ffn_eb2, L0_ffn_ew3, L0_ffn_eb3, L0_ffn_sel_ln_g, L0_ffn_sel_ln_b, L1_xattn_Wq, L1_xattn_bq, L1_xattn_Wk, L1_xattn_bk, L1_xattn_Wv, L1_xattn_bv, L1_xattn_Wo, L1_xattn_bo, L1_ffn_w_gate, L1_ffn_w_up, L1_ffn_w_down):
    import jax
    import jax.numpy as jnp

    def _L0_xattn_ref(inputs, context_seq, Wk1, Wv1, Wq1, Wo1, bo1, Wk2, Wv2, Wq2, Wo2, bo2, Wf, bf, g1, b1, g2, b2, g3, b3):
        import jax, jax.numpy as jnp
        import numpy as np
        B, S, SC, E, H = (2, 512, 512, 256, 16)
        D = E // H
        EPS = 1e-06

        def _layernorm(x, g, b):
            m = jnp.mean(x, axis=-1, keepdims=True)
            v = jnp.mean((x - m) ** 2, axis=-1, keepdims=True)
            return (x - m) / jnp.sqrt(v + EPS) * g + b

        def _mha(xk, xv, xq, Wk, Wv, Wq, Wo, bo, masked):
            K = jnp.einsum('bse,hed->bhsd', xk, Wk)
            V = jnp.einsum('bse,hed->bhsd', xv, Wv)
            Q = jnp.einsum('bqe,hed->bhqd', xq, Wq)
            scores = jnp.einsum('bhqd,bhkd->bhqk', Q, K)
            sk = xk.shape[1]
            if masked:
                causal = jnp.triu(jnp.ones((xq.shape[1], sk), dtype=bool), k=1)
                scores = jnp.where(causal, -jnp.inf, scores)
            att = jax.nn.softmax(scores / jnp.sqrt(jnp.asarray(sk, scores.dtype)), axis=-1)
            out = jnp.einsum('bhqk,bhkd->bhqd', att, V)
            out = out.transpose(0, 2, 1, 3).reshape(out.shape[0], out.shape[2], -1)
            return jax.nn.relu(out @ Wo + bo)
        a = _mha(inputs, inputs, inputs, Wk1, Wv1, Wq1, Wo1, bo1, masked=True)
        a = _layernorm(inputs + a, g1, b1)
        c = _mha(context_seq, context_seq, a, Wk2, Wv2, Wq2, Wo2, bo2, masked=False)
        c = _layernorm(c + c, g2, b2)
        f = jax.nn.relu(c @ Wf + bf)
        return _layernorm(c + f, g3, b3)

    def _L0_ffn_ref(x, index_b, index_t, sw1, sb1, sw2, sb2, sw3, sb3, s_ln_g, s_ln_b, sg_w, sg_b, eg_w, eg_b, exp_bias, ew1, eb1, ew2, eb2, ew3, eb3, sel_ln_g, sel_ln_b):
        import jax, jax.numpy as jnp
        import numpy as np
        EPS = 1e-05

        def _ln(x, g, b):
            mu = jnp.mean(x, axis=-1, keepdims=True)
            var = jnp.mean(jnp.square(x - mu), axis=-1, keepdims=True)
            return (x - mu) * jax.lax.rsqrt(var + EPS) * g + b

        def _forward(x, index_b, index_t, sw1, sb1, sw2, sb2, sw3, sb3, s_ln_g, s_ln_b, sg_w, sg_b, eg_w, eg_b, exp_bias, ew1, eb1, ew2, eb2, ew3, eb3, sel_ln_g, sel_ln_b):
            x1 = jnp.einsum('btd,hd->bth', x, sw1) + sb1
            x2 = jnp.einsum('btd,hd->bth', x, sw2) + sb2
            sh = _ln(jax.nn.silu(x1) * x2, s_ln_g, s_ln_b)
            shared_out = jnp.einsum('bth,dh->btd', sh, sw3) + sb3
            x_moe = x[index_b, index_t]
            shared_scores = jax.nn.sigmoid(x_moe @ sg_w.T + sg_b)
            expert_scores = jax.nn.sigmoid(x_moe @ eg_w.T + eg_b)
            top1_idx = jnp.argmax(expert_scores + exp_bias, axis=-1)
            top1_score = jnp.take_along_axis(expert_scores, top1_idx[:, None], axis=-1)
            weights = jax.nn.softmax(jnp.concatenate([shared_scores, top1_score], axis=-1), axis=-1)
            shared_w, expert_w = (weights[:, 0], weights[:, 1])
            shared_moe_out = shared_out[index_b, index_t] * shared_w[:, None]
            h1 = jnp.einsum('md,ehd->meh', x_moe, ew1) + eb1
            h2 = jnp.einsum('md,ehd->meh', x_moe, ew2) + eb2
            z = _ln(jax.nn.silu(h1) * h2, sel_ln_g, sel_ln_b)
            out_all = jnp.einsum('meh,edh->med', z, ew3) + eb3
            expert_out = jnp.take_along_axis(out_all, top1_idx[:, None, None], axis=1)[:, 0]
            expert_moe_out = expert_out * expert_w[:, None]
            final_out = shared_out.at[index_b, index_t].set(shared_moe_out + expert_moe_out)
            return final_out
        return _forward(x, index_b, index_t, sw1, sb1, sw2, sb2, sw3, sb3, s_ln_g, s_ln_b, sg_w, sg_b, eg_w, eg_b, exp_bias, ew1, eb1, ew2, eb2, ew3, eb3, sel_ln_g, sel_ln_b)

    def _L1_xattn_ref(query, key, value, Wq, bq, Wk, bk, Wv, bv, Wo, bo):
        import jax, jax.numpy as jnp
        import numpy as np
        EMB = 256
        HEADS = 16
        HEAD_DIM = EMB // HEADS
        B, S, E = query.shape
        H, D = (HEADS, HEAD_DIM)

        def split_heads(x):
            return x.reshape(B, -1, H, D).transpose(0, 2, 1, 3)
        Q = split_heads(query @ Wq + bq)
        K = split_heads(key @ Wk + bk)
        V = split_heads(value @ Wv + bv)
        scores = jnp.einsum('bhqd,bhkd->bhqk', Q, K) / jnp.sqrt(jnp.float32(D))
        attn = jax.nn.softmax(scores, axis=-1)
        out = jnp.einsum('bhqk,bhkd->bhqd', attn, V)
        out = out.transpose(0, 2, 1, 3).reshape(B, S, E)
        return out @ Wo + bo

    def _L1_ffn_ref(x, w_gate, w_up, w_down):
        import jax, jax.numpy as jnp
        import numpy as np
        DIM = 256
        HIDDEN = 768
        SCALE = 1.0 / 127.0

        def _dequant(w_int, dtype):
            return w_int.astype(dtype) * jnp.asarray(SCALE, dtype)
        wg = _dequant(w_gate, x.dtype)
        wu = _dequant(w_up, x.dtype)
        wd = _dequant(w_down, x.dtype)
        gate = jnp.einsum('bsd,hd->bsh', x, wg)
        up = jnp.einsum('bsd,hd->bsh', x, wu)
        h = jax.nn.silu(gate) * up
        return jnp.einsum('bsh,dh->bsd', h, wd)
    x = x + jnp.tanh(g_xattn[0]) * _L0_xattn_ref(_layernorm(x, axis=-1), ctx_1024, L0_xattn_Wk1, L0_xattn_Wv1, L0_xattn_Wq1, L0_xattn_Wo1, L0_xattn_bo1, L0_xattn_Wk2, L0_xattn_Wv2, L0_xattn_Wq2, L0_xattn_Wo2, L0_xattn_bo2, L0_xattn_Wf, L0_xattn_bf, L0_xattn_g1, L0_xattn_b1, L0_xattn_g2, L0_xattn_b2, L0_xattn_g3, L0_xattn_b3)
    x = x + jnp.tanh(g_ffn[0]) * _L0_ffn_ref(_layernorm(x, axis=-1), L0_ffn_index_b, L0_ffn_index_t, L0_ffn_sw1, L0_ffn_sb1, L0_ffn_sw2, L0_ffn_sb2, L0_ffn_sw3, L0_ffn_sb3, L0_ffn_s_ln_g, L0_ffn_s_ln_b, L0_ffn_sg_w, L0_ffn_sg_b, L0_ffn_eg_w, L0_ffn_eg_b, L0_ffn_exp_bias, L0_ffn_ew1, L0_ffn_eb1, L0_ffn_ew2, L0_ffn_eb2, L0_ffn_ew3, L0_ffn_eb3, L0_ffn_sel_ln_g, L0_ffn_sel_ln_b)
    x = x + jnp.tanh(g_xattn[1]) * _L1_xattn_ref(_layernorm(x, axis=-1), ctx_1024, ctx_1024, L1_xattn_Wq, L1_xattn_bq, L1_xattn_Wk, L1_xattn_bk, L1_xattn_Wv, L1_xattn_bv, L1_xattn_Wo, L1_xattn_bo)
    x = x + jnp.tanh(g_ffn[1]) * _L1_ffn_ref(_layernorm(x, axis=-1), L1_ffn_w_gate, L1_ffn_w_up, L1_ffn_w_down)
    return x

_drawn_inputs = setup_inputs


def setup_inputs(seed=0):
    import zlib

    import numpy as np

    out = dict(_drawn_inputs(seed))
    spreads = {'g_ffn': (-1.0, 0.2),
     'L0_xattn_bo1': (0.0, 0.8),
     'L0_xattn_bo2': (0.0, 0.1),
     'L0_xattn_bf': (0.0, 0.1),
     'L0_xattn_g1': (1.0, 0.6),
     'L0_xattn_b1': (0.0, 0.8),
     'L0_xattn_g2': (1.0, 0.2),
     'L0_xattn_b2': (0.0, 0.1),
     'L0_xattn_g3': (1.0, 0.2),
     'L0_xattn_b3': (0.0, 0.1),
     'L0_ffn_sb1': (0.0, 0.1),
     'L0_ffn_sb2': (0.0, 0.1),
     'L0_ffn_sb3': (0.0, 0.1),
     'L0_ffn_s_ln_g': (1.0, 0.2),
     'L0_ffn_s_ln_b': (0.0, 0.438),
     'L0_ffn_eg_b': (0.0, 0.8),
     'L0_ffn_exp_bias': (0.0, 0.1),
     'L0_ffn_eb1': (0.0, 0.732),
     'L0_ffn_eb2': (0.0, 0.681),
     'L0_ffn_eb3': (0.0, 0.556),
     'L0_ffn_sel_ln_g': (1.0, 0.6),
     'L0_ffn_sel_ln_b': (0.0, 0.8),
     'L1_xattn_bq': (0.0, 0.452),
     'L1_xattn_bk': (0.0, 0.8),
     'L1_xattn_bv': (0.0, 0.1),
     'L1_xattn_bo': (0.0, 0.1)}
    factors = {'L0_xattn_Wk1': 8.0,
     'L0_xattn_Wv1': 8.0,
     'L0_xattn_Wq1': 8.0,
     'L0_xattn_Wo1': 8.0,
     'L0_xattn_Wk2': 8.0,
     'L0_xattn_Wq2': 8.0,
     'L0_ffn_sg_w': 8.0,
     'L0_ffn_eg_w': 7.682}
    for name, (base, spread) in spreads.items():
        noise = np.random.default_rng([zlib.crc32(name.encode()), seed]).standard_normal(out[name].shape)
        drawn = base * np.exp(spread * noise) if base else spread * noise
        out[name] = jnp.asarray(drawn.astype(out[name].dtype))
    for name, factor in factors.items():
        out[name] = (out[name] * factor).astype(out[name].dtype)
    return out
```

```python
from contextlib import ExitStack

import concourse.bass as bass
from concourse import mybir

F32 = mybir.dt.float32
BF16 = mybir.dt.bfloat16
I32 = mybir.dt.int32
ALU = mybir.AluOpType
ACT = mybir.ActivationFunctionType
AX = mybir.AxisListType
ds = bass.ds

P = 128
S = 2048
E = 256
H = 16
D = E // H
CTX = 1601
CH = 512
NC = S // CH
R = CH // P
NG = H // 4
HF = 128
NE = 8
M = 512
FF = 768
QROWS = 6 * D
MASKED = -3.0e38

Q_PARTS = (0, 0, 1, 1, 0, 2)
K_PARTS = (0, 1, 0, 1, 2, 0)


class Chain:

    def __init__(self, eng, sem):
        self.eng, self.sem, self.base, self.k, self.it = eng, sem, 0, 0, None

    def loop(self, it, per):
        self.base, self.k, self.it, self.per = self.base + self.k, 0, it, per

    def end(self, times):
        assert self.k == self.per, (self.k, self.per)
        self.base, self.k, self.it = self.base + times * self.per, 0, None

    def link(self, ins):
        self.note(ins)
        self.join()

    def note(self, ins):
        self.k += 1
        ins.then_inc(self.sem, 1)

    def join(self):
        at = self.base + self.k
        self.eng.wait_ge(self.sem, at if self.it is None else self.it * self.per + at)


def steps_of(causal):
    out = []
    for qc in range(NC):
        kts = range(R * qc + R) if causal else range(-(-CTX // P))
        for kt in kts:
            c0 = max(0, kt - R * qc) * P if causal else 0
            kn = P if causal else min(P, CTX - kt * P)
            out.append((qc, kt, c0, kn, kt == kts[-1]))
    return out


def build(nc, A, out):
    ctx = ExitStack()
    with ctx:
        def sb(name, shape, dt=F32):
            return ctx.enter_context(nc.sbuf_tensor(name, shape, dt))

        sems = {}

        def sem(name):
            if name not in sems:
                sems[name] = ctx.enter_context(nc.semaphore(name))
            return sems[name]

        x_sb = sb("x_sb", [P, S // P, E])
        xmean = sb("xmean", [P, S // P])
        xrstd = sb("xrstd", [P, S // P])
        o_sb = sb("o_sb", [P, S // P, E])
        hb = sb("hb", [P, R, E])
        xT = sb("xT", [P, 2, CH])
        z = sb("z", [P, R, E])
        z2 = sb("z2", [P, R, E])
        st = sb("st", [P, R, 6])
        mv = sb("mv", [P, R, 2])
        ve = sb("ve", [P, R])
        rs = sb("rs", [P, R])
        mhalf = sb("mhalf", [P, R])
        identf = sb("identf", [P, P])
        identb = sb("identb", [P, P], BF16)
        mask_kq = sb("mask_kq", [P, P], BF16)
        mask_qk = sb("mask_qk", [P, P], BF16)
        accS = sb("accS", [P, 2, CH])
        rec = sb("rec", [P, R * 4])
        mx = sb("mx", [P, 4 * S // P])
        mneg = sb("mneg", [4 * S // P, P])
        mres = sb("mres", [4 * S // P, P])
        mparts = sb("mparts", [4 * S // P, 3, P], BF16)
        wt = {n: sb(n, [P, 2, E]) for n in ("wq1", "wk1", "wv1", "wo1", "wq2", "wk2", "wv2", "wo2", "wf",
                                            "wq3", "wk3", "wv3", "wo3", "sw12")}
        sw3 = sb("sw3", [P, E])
        gate_w = sb("gate_w", [P, 2, 16])
        bias_col = {n: sb(n, [P, 2]) for n in ("bq3", "bk3")}
        rows = {}
        for n, w in (("bo1", E), ("g1", E), ("b1", E), ("bo2", E), ("g2", E), ("b2", E), ("bf", E), ("g3", E),
                     ("b3", E), ("bv3", E), ("bo3", E), ("sb12", E), ("sb3", E), ("slg", HF), ("slb", HF),
                     ("elg", HF), ("elb", HF), ("gateb", 16), ("expb", NE)):
            rows[n] = sb("row_" + n, [P, w])
        tg = sb("tg", [P, 4])
        iota8 = sb("iota8", [P, NE])
        tok_id = sb("tok_id", [P, S // P])
        routed = sb("routed", [P, S // P])
        sc = sb("sc", [P, R, 16])
        sel = sb("sel", [P, R, NE])
        oh = sb("oh", [P, R, NE])
        small = sb("small", [P, 8, R])
        ohT = sb("ohT", [NE, R, P])

        arena = sb("arena", [P, 26624])

        def region(at, shape, dt=F32):
            n = 1
            for d in shape:
                n *= d
            words = n if dt != BF16 else n // 2
            v = arena[:, at:at + words]
            if dt != F32:
                v = v.bitcast(dt)
            if len(shape) == 2:
                v = v.rearrange("p (a b) -> p a b", b=shape[1])
            elif len(shape) == 3:
                v = v.rearrange("p (a b c) -> p a b c", b=shape[1], c=shape[2])
            return v

        stackQ = [region(4096 * h, (4, S), BF16) for h in range(2)]
        stackK = [region(8192 + 4096 * h, (4, S), BF16) for h in range(2)]
        probs = [region(16384 + 1024 * n, (2, CH)) for n in range(6)]
        vg = [region(22528 + 2048 * h, (S // P, 4, 32)) for h in range(2)]
        pt = region(16384, (2, CH))
        pr = region(17408, (2, CH))
        parts = [region(18432 + 512 * n, (2, CH), BF16) for n in range(3)]
        vst = region(19968, (R, H, 32))
        ew12 = region(0, (2, 2 * NE * HF))
        ew3 = region(4096, (NE * E,))
        eb = region(6144, (2 * HF + E,))
        eo = region(6656, (R, E))
        midx = region(7680, (M,))
        bsel = region(19968, (R, 2 * HF + E))
        shr = region(22016, (R, E))
        hs = region(23040, (R, 2 * HF))
        mtmp = region(24064, (M,))
        mtmp2 = region(24576, (M,))
        midx_i = region(25088, (2, M), I32)
        sg = region(26112, (R, HF))
        wgu = region(0, (2, 2, FF))
        wd = region(3072, (FF // P, E))
        hT = region(4608, (FF // P, CH))
        sgT = region(7680, (2, CH))
        wint = region(8704, (2, 2, FF), I32)
        dint = region(11776, (FF // P, E), I32)

        ps = ctx.enter_context(nc.psum_tensor("ps", [P, 8, 512], F32))

        scr_qk = {}
        for n in ("q1", "k1", "q2", "k2", "q3", "k3"):
            scr_qk[n] = nc.dram_tensor("scr_" + n, [3, E, S], BF16, kind="Internal").ap()
        scr_v = {n: nc.dram_tensor("scr_" + n, [S, H * 32], F32, kind="Internal").ap() for n in ("v1", "v2", "v3")}
        scr_m = nc.dram_tensor("scr_m", [3, 3, NG, 4 * S], BF16, kind="Internal").ap()

        weights_early = []

        def w2(name, src):
            weights_early.append((wt[name][:, :, :], src.rearrange("(c p) n -> p c n", p=P)))

        for n in ("wq1", "wk1", "wv1", "wo1", "wq2", "wk2", "wv2", "wo2", "wf", "wq3", "wk3", "wv3", "wo3", "sw12"):
            w2(n, A[n])
        weights_early.append((sw3[:, :], A["sw3"]))
        weights_early.append((gate_w[:, :, 0:NE + 1], A["gate_w"].rearrange("(c p) n -> p c n", p=P)))
        for n in ("bq3", "bk3"):
            weights_early.append((bias_col[n][:, :], A[n]))
        for n in rows:
            w = A[n].shape[0]
            weights_early.append((rows[n][:, 0:w], A[n].partition_broadcast(P)))
        weights_early.append((tg[:, :], A["gates"].partition_broadcast(P)))

        weights_in = sem("weights_in")
        x_in = sem("x_in")
        W_ALL = 16 * len(weights_early)

        dma_jobs = {}
        NORM = dict(A=1)

        SPLITS = {"A": (0, 2), "C": (8, 2), "B1": (16, 1), "B2": (20, 1)}
        VSTORES = {"A": (0, 1), "C": (4, 2)}
        LNS = {"A": (0, 1), "B1": (4, 1), "B2": (8, 6), "B3": (32, 1)}

        def split_n(p, c, k):
            base, per = SPLITS[p]
            return c * per + (base + k)

        def v_n(p, c, k):
            base, per = VSTORES[p]
            return c * per + (base + k)

        def ln_n(p, c, k):
            base, per = LNS[p]
            return c * per + (base + k)

        proj_t, part_hi, part_rest, part_mid, part_lo, parts_out = (
            sem(n) for n in ("proj_t", "part_hi", "part_rest", "part_mid", "part_lo", "parts_out"))
        v_staged, v_out = sem("v_staged"), sem("v_out")
        ln_var, ln_rstd = sem("ln_var"), sem("ln_rstd")
        consts = sem("consts")
        N_CONST = 13

        def apart(eng):
            eng.nop(nofuse=True)

        block = ctx.enter_context(nc.Block())

        TR = {"A": 1, "C": 1, "B1": 2, "B2": 7, "B3": 2}

        @block.sync
        def _(sp):
            for t in range(NC):
                sp.dma_start(x_sb[:, 4 * t:4 * t + 4, :],
                             A["x"][0, t * CH:(t + 1) * CH, :].rearrange("(r p) e -> p r e", p=P)).then_inc(x_in, 16)
            for dst, src in weights_early:
                sp.dma_start(dst, src).then_inc(weights_in, 16)

            def store_parts(p, c, k, name):
                n = split_n(p, c, k)
                dst = [scr_qk[name][i, :, ds(c * CH, CH)].rearrange("(o p) q -> p o q", p=P) for i in range(3)]
                sp.wait_ge(part_hi, n + 1)
                apart(sp)
                sp.dma_start(dst[0], parts[0]).then_inc(parts_out, 16)
                sp.wait_ge(part_lo, n + 1)
                apart(sp)
                sp.dma_start(dst[1], parts[1]).then_inc(parts_out, 16)
                apart(sp)
                sp.dma_start(dst[2], parts[2]).then_inc(parts_out, 16)

            def store_v(p, c, k, name):
                sp.wait_ge(v_staged, v_n(p, c, k) + 1)
                apart(sp)
                sp.dma_start(scr_v[name][ds(c * CH, CH), :].rearrange("(r p) n -> p r n", p=P),
                             vst.rearrange("p r h d -> p r (h d)")).then_inc(v_out, 16)

            with sp.Fori(0, NC) as c:
                store_parts("A", c, 0, "k1")
                store_parts("A", c, 1, "q1")
                store_v("A", c, 0, "v1")

            ctx_in = sem("ctx_in")
            with sp.Fori(0, 3) as c:
                sp.wait_ge(sem("tr_C"), c)
                apart(sp)
                sp.dma_start(hb[:, :, :], A["ctx"][0, ds(c * CH, CH), :].rearrange("(r p) e -> p r e", p=P))\
                  .then_inc(ctx_in, 16)
                store_parts("C", c, 0, "k2")
                store_parts("C", c, 1, "k3")
                store_v("C", c, 0, "v2")
                store_v("C", c, 1, "v3")
            sp.wait_ge(sem("ctx_pad"), 1)
            sp.dma_start(hb[0:CTX - 3 * CH, 0, :], A["ctx"][0, 3 * CH:CTX, :]).then_inc(ctx_in, 16)
            store_parts("C", 3, 0, "k2")
            store_parts("C", 3, 1, "k3")
            store_v("C", 3, 0, "v2")
            store_v("C", 3, 1, "v3")

            def attention_loads(a, parts_needed, v_needed):
                sp.wait_ge(parts_out, parts_needed)
                sp.wait_ge(v_out, v_needed)
                with sp.Fori(0, NG // 2) as i:
                    for half in range(2):
                        g = i * 2 + half
                        sp.wait_ge(sem(f"acc_T{half}_{a}"), i * 4)
                        apart(sp)
                        for blk in range(6):
                            for stack, parts_of, nm in ((stackQ, Q_PARTS, "q"), (stackK, K_PARTS, "k")):
                                sp.dma_start(stack[half][D * blk:D * blk + D, :, :],
                                             scr_qk[f"{nm}{a}"][parts_of[blk], ds(g * 64, 64), :]
                                             .rearrange("(h d) q -> d h q", d=D))\
                                  .then_inc(sem(f"stacks_in{half}_{a}"), 16)
                        sp.dma_start(vg[half].rearrange("p k h d -> p k (h d)"),
                                     scr_v[f"v{a}"][:, ds(g * 128, 128)].rearrange("(k p) n -> p k n", p=P))\
                          .then_inc(sem(f"v_in{half}_{a}"), 16)

            attention_loads(1, 48 * 16, 16 * 12)
            with sp.Fori(0, NC) as c:
                store_parts("B1", c, 0, "q2")
            attention_loads(2, 48 * 20, 16 * 12)
            sp.wait_ge(sem("normed_2"), 16)
            ew_in = sem("ew_in")
            sp.dma_start(ew12, A["ew12"].rearrange("(c p) n -> p c n", p=P)).then_inc(ew_in, 16)
            sp.dma_start(ew3, A["ew3"]).then_inc(ew_in, 16)
            sp.dma_start(eb[0:NE, :], A["eb"]).then_inc(ew_in, 16)
            sp.dma_start(midx_i[:, 0, :], A["index_b"].partition_broadcast(P)).then_inc(ew_in, 16)
            sp.dma_start(midx_i[:, 1, :], A["index_t"].partition_broadcast(P)).then_inc(ew_in, 16)
            with sp.Fori(0, NC) as c:
                store_parts("B2", c, 0, "q3")
            attention_loads(3, 48 * 24, 16 * 12)
            sp.wait_ge(sem("normed_3"), 16)
            fw_in = sem("fw_in")
            sp.dma_start(wint[:, 0, :, :], A["w_gate"].rearrange("(c p) n -> p c n", p=P)).then_inc(fw_in, 16)
            sp.dma_start(wint[:, 1, :, :], A["w_up"].rearrange("(c p) n -> p c n", p=P)).then_inc(fw_in, 16)
            sp.dma_start(dint, A["w_down"].rearrange("(c p) n -> p c n", p=P)).then_inc(fw_in, 16)
            with sp.Fori(0, NC) as c:
                sp.wait_ge(sem("sixseven_B3"), c * 2 + 2)
                apart(sp)
                sp.dma_start(out[0, ds(c * CH, CH), :].rearrange("(r p) e -> p r e", p=P),
                             x_sb[:, ds(c * 4, 4), :]).then_inc(sem("out_done"), 16)
            sp.wait_ge(sem("out_done"), 16 * NC)

        @block.gpsimd
        def _(pool):
            pool.memset(identf[:, :], 0.0).then_inc(consts, 1)
            pool.memset(identb[:, :], 0.0).then_inc(consts, 1)
            pool.memset(mask_kq[:, :], 0.0).then_inc(consts, 1)
            pool.memset(mask_qk[:, :], 0.0).then_inc(consts, 1)
            pool.wait_ge(consts, 4)
            pool.affine_select(out=identf[:, :], in_=identf[:, :], compare_op=ALU.not_equal, fill=1.0, base=0,
                               pattern=[[-1, P]], channel_multiplier=1).then_inc(consts, 1)
            pool.affine_select(out=identb[:, :], in_=identb[:, :], compare_op=ALU.not_equal, fill=1.0, base=0,
                               pattern=[[-1, P]], channel_multiplier=1).then_inc(consts, 1)
            pool.affine_select(out=mask_kq[:, :], in_=mask_kq[:, :], compare_op=ALU.is_ge, fill=MASKED, base=0,
                               pattern=[[1, P]], channel_multiplier=-1).then_inc(consts, 1)
            pool.affine_select(out=mask_qk[:, :], in_=mask_qk[:, :], compare_op=ALU.is_ge, fill=MASKED, base=0,
                               pattern=[[-1, P]], channel_multiplier=1).then_inc(consts, 1)
            pool.memset(mhalf[:, :], -0.5).then_inc(consts, 1)
            pool.memset(vst, 0.0).then_inc(consts, 1)
            pool.wait_ge(consts, 10)
            pool.memset(vst[:, :, :, D:D + 1], 1.0).then_inc(consts, 1)
            pool.iota(iota8[:, :], [[1, NE]], base=-NE, channel_multiplier=0,
                      allow_small_or_imprecise_dtypes=True).then_inc(consts, 1)
            pool.iota(tok_id[:, :], [[P, S // P]], base=1, channel_multiplier=1,
                      allow_small_or_imprecise_dtypes=True).then_inc(consts, 1)

            def rstd(p, c, k):
                n = ln_n(p, c, k)
                pool.wait_ge(ln_var, n + 1)
                pool.tensor_tensor(rs[:, :], ve[:, :], mhalf[:, :], ALU.pow).then_inc(ln_rstd, 1)

            def split(p, c, k):
                n = split_n(p, c, k)
                pool.wait_ge(part_rest, n + 1)
                pool.wait_ge(parts_out, n * 48)
                apart(pool)
                pool.tensor_copy(parts[1], pr).then_inc(part_mid, 1)
                pool.wait_ge(part_mid, n + 1)
                pool.tensor_tensor(parts[2], pr, parts[1], ALU.subtract).then_inc(part_lo, 1)

            with pool.Fori(0, NC) as c:
                rstd("A", c, 0)
                split("A", c, 0)
                split("A", c, 1)
            with pool.Fori(0, 3) as c:
                split("C", c, 0)
                split("C", c, 1)
            pool.wait_ge(sem("tr_C"), 3)
            pool.memset(hb[:, :, :], 0.0).then_inc(sem("ctx_pad"), 1)
            split("C", 3, 0)
            split("C", 3, 1)

            def take_o(a, p, c):
                pool.wait_ge(sem(f"tr_{p}"), c * TR[p])
                apart(pool)
                pool.tensor_copy(hb[:, :, :], o_sb[:, ds(c * 4, 4), :]).then_inc(sem(f"o_taken_{p}"), 1)

            pool.wait_ge(sem("normed_1"), 16)
            with pool.Fori(0, NC) as c:
                take_o(1, "B1", c)
                rstd("B1", c, 0)
                split("B1", c, 0)
            pool.wait_ge(sem("normed_2"), 16)
            with pool.Fori(0, NC) as c:
                take_o(2, "B2", c)
                for k in range(6):
                    rstd("B2", c, k)
                split("B2", c, 0)
            pool.wait_ge(sem("normed_3"), 16)
            with pool.Fori(0, NC) as c:
                take_o(3, "B3", c)
                rstd("B3", c, 0)

        @block.scalar
        def _(act):
            def evac_T(p, c, k, mm_before, hT_dst=None):
                act.wait_ge(sem(f"tr_{p}"), c * TR[p] + k + 1)
                act.wait_ge(sem(f"mm_{p}"), mm_before)
                act.activation(xT[:, :, :], ps[:, 0:2, :], ACT.Copy).then_inc(sem(f"xT_{p}"), 1)

            def take_proj(p, c, k, bank, mm_at, bias=None):
                n = split_n(p, c, k)
                act.wait_ge(sem(f"mm_{p}"), mm_at)
                act.wait_ge(part_rest, n)
                if bias is None:
                    act.activation(pt, ps[:, bank:bank + 2, :], ACT.Copy).then_inc(proj_t, 1)
                else:
                    act.activation(pt[:, 0, :], ps[:, bank, :], ACT.Identity, bias=bias[:, 0:1])
                    act.activation(pt[:, 1, :], ps[:, bank + 1, :], ACT.Identity, bias=bias[:, 1:2])\
                       .then_inc(proj_t, 1)

            act.wait_ge(weights_in, W_ALL)
            act.activation(tg[:, :], tg[:, :], ACT.Tanh).then_inc(sem("tanh_done"), 1)
            with act.Fori(0, NC) as c:
                evac_T("A", c, 0, c * 3)
                take_proj("A", c, 0, 2, c * 3 + 1)
                take_proj("A", c, 1, 4, c * 3 + 2)
            with act.Fori(0, NC) as c:
                evac_T("C", c, 0, c * 4)
                take_proj("C", c, 0, 2, c * 4 + 1)
                take_proj("C", c, 1, 4, c * 4 + 2, bias_col["bk3"])

            def attend(a, causal, scale):
                steps = steps_of(causal)
                T = len(steps)
                with act.Fori(0, NG // 2) as i:
                    for half in range(2):
                        g = i * 2 + half
                        act.wait_ge(sem(f"max_split_{a}"), g + 1)
                        for part in range(3):
                            act.dma_start(scr_m[a - 1, part, ds(g, 1), :].rearrange("o (w q) -> (o w) q", q=P),
                                          mparts[:, part, :]).then_inc(sem(f"max_out_{a}"), 16)
                        act.wait_ge(sem(f"max_out_{a}"), g * 48 + 48)
                        act.dma_start(stackQ[half][QROWS:QROWS + 3, :, :].rearrange("p h q -> p (h q)"),
                                      scr_m[a - 1, :, ds(g, 1), :].rearrange("t o n -> t (o n)"))\
                           .then_inc(sem(f"max_in{half}_{a}"), 16)
                        for t, (qc, kt, c0, kn, _) in enumerate(steps):
                            for pair in range(2):
                                n = 2 * t + pair
                                act.wait_ge(sem(f"scores_{a}"), g * (2 * T) + (n + 1))
                                if t >= 3:
                                    act.wait_ge(sem(f"pv_{a}"), g * T + (t - 2))
                                b = 2 * (n % 3)
                                act.activation(probs[n % 6][0:kn, :, c0:CH], ps[0:kn, b:b + 2, c0:CH], ACT.Exp,
                                               scale=scale).then_inc(sem(f"exp_{a}"), 1)

            attend(1, True, float(S) ** -0.5)
            with act.Fori(0, NC) as c:
                evac_T("B1", c, 0, c * 2)
                evac_T("B1", c, 1, c * 2 + 1)
                take_proj("B1", c, 0, 2, c * 2 + 2)
            attend(2, False, float(CTX) ** -0.5)
            MM2 = 14
            with act.Fori(0, NC) as c:
                m = c * MM2
                evac_T("B2", c, 0, m)
                evac_T("B2", c, 1, m + 1)
                evac_T("B2", c, 2, m + 2)
                act.wait_ge(sem("sixseven_B2"), c * 4 + 3)
                act.activation(sg[:, :, :], z[:, :, 0:HF], ACT.Silu).then_inc(sem("silu_2"), 1)
                act.wait_ge(sem("gate_in"), c + 1)
                act.activation(sc[:, :, 0:NE + 1], sc[:, :, 0:NE + 1], ACT.Sigmoid).then_inc(sem("sig_2"), 1)
                act.wait_ge(sem("tr_B2"), c * 7 + 4)
                act.activation(z2[:, :, :].rearrange("p r e -> p (r e)")[:, 0:CH], ps[:, 0, :], ACT.Copy)\
                   .then_inc(sem("xT_B2"), 1)
                act.wait_ge(sem("gate_diff"), c + 1)
                act.activation(small[:, 3, :], small[:, 2, :], ACT.Sigmoid).then_inc(sem("sig_2"), 1)
                act.activation(small[:, 4, :], small[:, 2, :], ACT.Sigmoid, scale=-1.0).then_inc(sem("sig_2"), 1)
                act.wait_ge(sem("tr_B2"), c * 7 + 5)
                act.activation(ohT[:, :, :].rearrange("e r p -> e (r p)"), ps[0:NE, 0, :], ACT.Copy)\
                   .then_inc(sem("xT_B2"), 1)
                act.wait_ge(sem("expert_out"), c * 4)
                for r in range(R):
                    act.wait_ge(sem("mm_B2"), m + (6 + 2 * r))
                    act.activation(bsel[:, r, :], ps[:, 5, :], ACT.Copy).then_inc(sem("bsel_2"), 1)
                act.wait_ge(sem("picked"), c * 4 + 4)
                act.activation(sg[:, :, :], hs[:, :, 0:HF], ACT.Silu).then_inc(sem("silu_2"), 1)
                act.wait_ge(sem("tr_B2"), c * 7 + 6)
                act.wait_ge(sem("mm_B2"), m + 5)
                act.activation(z2[:, :, :].rearrange("p r e -> p (r e)")[:, 0:CH], ps[:, 0, :], ACT.Copy)\
                   .then_inc(sem("xT_B2"), 1)
                evac_T("B2", c, 6, m + 13)
                take_proj("B2", c, 0, 2, m + 14, bias_col["bq3"])
            attend(3, False, float(D) ** -0.5)
            with act.Fori(0, NC) as c:
                m = c * 8
                evac_T("B3", c, 0, m)
                evac_T("B3", c, 1, m + 1)
                for f in range(FF // P):
                    act.wait_ge(sem("mm_B3"), m + 2 + f)
                    if f >= 2:
                        act.wait_ge(sem("up_done"), c * 6 + (f - 1))
                    else:
                        act.wait_ge(sem("up_done"), c * 6)
                    act.activation(sgT[:, f % 2, :], ps[:, 2 + 2 * (f % 2), :], ACT.Silu).then_inc(sem("silu_3"), 1)

        @block.tensor
        def _(pe):
            pe.wait_ge(weights_in, W_ALL)
            pe.wait_ge(consts, N_CONST)

            def transposes(p, c, k, src, ready, value, free_at=None):
                pe.wait_ge(ready, value)
                pe.wait_ge(sem(f"xT_{p}"), c * XT[p] + k)
                for cc in range(2):
                    for r in range(R):
                        last = pe.transpose(ps[:, cc, r * P:(r + 1) * P], src[:, r, cc * P:(cc + 1) * P], identf[:, :])
                last.then_inc(sem(f"tr_{p}"), 1)

            XT = TR

            def feature_major(p, w, bank, xt_at, n_out=2, free=None):
                pe.wait_ge(sem(f"xT_{p}"), xt_at)
                if free is not None:
                    pe.wait_ge(*free)
                for oc in range(n_out):
                    for cc in range(2):
                        last = pe.matmul(ps[:, bank + oc, :], w[:, cc, oc * P:(oc + 1) * P], xT[:, cc, :],
                                         start=(cc == 0), stop=(cc == 1))
                last.then_inc(sem(f"mm_{p}"), 1)

            def token_major(p, w, bank, xt_at, free=None):
                pe.wait_ge(sem(f"xT_{p}"), xt_at)
                if free is not None:
                    pe.wait_ge(*free)
                for r in range(R):
                    for cc in range(2):
                        last = pe.matmul(ps[:, bank + r // 2, (r % 2) * E:(r % 2) * E + E],
                                         xT[:, cc, r * P:(r + 1) * P], w[:, cc, :], start=(cc == 0), stop=(cc == 1))
                last.then_inc(sem(f"mm_{p}"), 1)

            with pe.Fori(0, NC) as c:
                transposes("A", c, 0, hb, sem("hb_A"), c + 1)
                feature_major("A", wt["wk1"], 2, c + 1, free=(proj_t, c * 2))
                feature_major("A", wt["wq1"], 4, c + 1, free=(proj_t, c * 2))
                token_major("A", wt["wv1"], 6, c + 1, free=(v_staged, c))
            with pe.Fori(0, NC) as c:
                transposes("C", c, 0, hb, sem("ctx_in"), c * 16 + 16)
                feature_major("C", wt["wk2"], 2, c + 1, free=(proj_t, c * 2 + 8))
                feature_major("C", wt["wk3"], 4, c + 1, free=(proj_t, c * 2 + 8))
                token_major("C", wt["wv2"], 6, c + 1, free=(v_staged, c * 2 + 4))
                token_major("C", wt["wv3"], 6, c + 1, free=(v_staged, c * 2 + 5))

            def attend(a, causal, before):
                steps = steps_of(causal)
                T = len(steps)
                keys = S if causal else CTX
                scores, exps, pv = sem(f"scores_{a}"), sem(f"exp_{a}"), sem(f"pv_{a}")
                for s, v in before:
                    pe.wait_ge(s, v)
                with pe.Fori(0, NG // 2) as i:
                    for half in range(2):
                        g = i * 2 + half
                        sq, sk = stackQ[half], stackK[half]
                        pe.wait_ge(sem(f"stacks_in{half}_{a}"), i * 192 + 192)
                        pe.wait_ge(exps, g * (2 * T))
                        pe.wait_ge(sem(f"normed_{a}"), g * 4)
                        for w in range(4 * S // P):
                            j, qt = w // (S // P), w % (S // P)
                            if w >= 2:
                                pe.wait_ge(sem(f"maxima_{a}"), g * 64 + (w - 1))
                            nk = (qt + 1) * P if causal else keys
                            b0 = 4 * (w % 2)
                            for k0 in range(0, nk, CH):
                                n = min(CH, nk - k0)
                                masked = causal and k0 + n == nk
                                last = pe.matmul(ps[:, b0 + k0 // CH, 0:n], sq[0:QROWS, j, qt * P:(qt + 1) * P],
                                                 sk[0:QROWS, j, k0:k0 + n], start=True, stop=not masked)
                            if causal:
                                last = pe.matmul(ps[:, b0 + k0 // CH, n - P:n], identb[:, :], mask_qk[:, :],
                                                 start=False, stop=True)
                            last.then_inc(sem(f"rows_{a}"), 1)
                        pe.wait_ge(sem(f"maxima_{a}"), g * 64 + 64)
                        apart(pe)
                        pe.transpose(ps[0:64, 0, 0:P], mx[:, :], identf[:, :]).then_inc(sem(f"max_T_{a}"), 1)
                        pe.wait_ge(sem(f"max_in{half}_{a}"), i * 16 + 16)
                        pe.wait_ge(sem(f"v_in{half}_{a}"), i * 16 + 16)

                        def values(t):
                            qc, kt, c0, kn, last_kt = steps[t]
                            pe.wait_ge(exps, g * (2 * T) + (2 * t + 2))
                            if kt == 0 and qc >= 2:
                                pe.wait_ge(sem(f"normed_{a}"), g * 4 + (qc - 1))
                            for j in range(4):
                                mm = pe.matmul(ps[32 * j:32 * j + 32, 6 + qc % 2, c0:CH], vg[half][0:kn, kt, j, :],
                                               probs[(2 * t + j // 2) % 6][0:kn, j % 2, c0:CH],
                                               start=(kt == 0), stop=last_kt, tile_position=(0, 32 * j))
                            mm.then_inc(pv, 1)

                        def turn(qc):
                            pe.wait_ge(sem(f"acc_out_{a}"), g * 4 + (qc + 1))
                            for r in range(R):
                                mm = pe.transpose(ps[:, 6 + qc % 2, r * P:(r + 1) * P],
                                                  accS[:, qc % 2, r * P:(r + 1) * P], identf[:, :])
                            mm.then_inc(sem(f"acc_T{half}_{a}"), 1)

                        for t, (qc, kt, c0, kn, _) in enumerate(steps):
                            diag = causal and kt >= R * qc
                            for pair in range(2):
                                n = 2 * t + pair
                                b = 2 * (n % 3)
                                if n >= 3:
                                    pe.wait_ge(exps, g * (2 * T) + (n - 2))
                                for jj in range(2):
                                    j = 2 * pair + jj
                                    mm = pe.matmul(ps[0:kn, b + jj, c0:CH], sk[0:QROWS + 3, j, kt * P:kt * P + kn],
                                                   sq[0:QROWS + 3, j, qc * CH + c0:(qc + 1) * CH],
                                                   start=True, stop=not diag)
                                    if diag:
                                        mm = pe.matmul(ps[:, b + jj, c0:c0 + P], identb[:, :], mask_kq[:, :],
                                                       start=False, stop=True)
                                mm.then_inc(scores, 1)
                            if t >= 1:
                                values(t - 1)
                            if kt == 2 and qc >= 1:
                                turn(qc - 1)
                        values(T - 1)
                        turn(NC - 1)

            attend(1, True, ((proj_t, 16), (v_staged, 12)))

            def o_proj(p, w, c, per_tr, per_mm):
                transposes(p, c, 0, hb, sem(f"o_taken_{p}"), c + 1)
                token_major(p, w, 6, c * per_tr + 1, free=(sem(f"sixseven_{p}"), c * SIX[p]))

            SIX = {"B1": 1, "B2": 4, "B3": 2}
            pe.wait_ge(sem("normed_1"), 16)
            with pe.Fori(0, NC) as c:
                o_proj("B1", wt["wo1"], c, 2, 2)
                transposes("B1", c, 1, hb, sem("hb_B1"), c + 1)
                feature_major("B1", wt["wq2"], 2, c * 2 + 2, free=(proj_t, c + 16))
            attend(2, False, ((proj_t, 20), (sem("sixseven_B1"), 4)))
            pe.wait_ge(sem("normed_2"), 16)
            with pe.Fori(0, NC) as c:
                xt = c * 7
                six = sem("sixseven_B2")
                o_proj("B2", wt["wo2"], c, 7, 14)
                transposes("B2", c, 1, hb, sem("hb_B2"), c * 3 + 1)
                token_major("B2", wt["wf"], 6, xt + 2, free=(six, c * 4 + 1))
                transposes("B2", c, 2, hb, sem("hb_B2"), c * 3 + 2)
                pe.wait_ge(sem("gate_in"), c)
                pe.wait_ge(sem("xT_B2"), xt + 3)
                pe.wait_ge(sem("bsel_2"), c * 4)
                for r in range(R):
                    for cc in range(2):
                        mm = pe.matmul(ps[:, 5, r * 16:r * 16 + NE + 1], xT[:, cc, r * P:(r + 1) * P],
                                       gate_w[:, cc, 0:NE + 1], start=(cc == 0), stop=(cc == 1))
                mm.then_inc(sem("mm_B2"), 1)
                token_major("B2", wt["sw12"], 6, xt + 3, free=(six, c * 4 + 2))
                pe.wait_ge(sem("hidden_2"), c * 2 + 1)
                for r in range(R):
                    mm = pe.transpose(ps[:, 0, r * P:(r + 1) * P], z[:, r, 0:HF], identf[:, :])
                mm.then_inc(sem("tr_B2"), 1)
                pe.wait_ge(sem("xT_B2"), xt + 4)
                pe.wait_ge(six, c * 4 + 3)
                for r in range(R):
                    mm = pe.matmul(ps[:, 6 + r // 2, (r % 2) * E:(r % 2) * E + E],
                                   z2[:, :, :].rearrange("p r e -> p (r e)")[:, r * P:(r + 1) * P], sw3[:, :],
                                   start=True, stop=True)
                mm.then_inc(sem("mm_B2"), 1)
                pe.wait_ge(sem("onehot"), c + 1)
                for r in range(R):
                    mm = pe.transpose(ps[0:NE, 0, r * P:(r + 1) * P], oh[:, r, :], identf[:, :])
                mm.then_inc(sem("tr_B2"), 1)
                pe.wait_ge(sem("xT_B2"), xt + 5)
                pe.wait_ge(sem("ew_in"), 80)
                pe.wait_ge(proj_t, c + 20)
                for r in range(R):
                    pe.wait_ge(sem("bsel_2"), c * 4 + r)
                    pe.matmul(ps[:, 5, :], ohT[:, r, :], eb[0:NE, :], start=True, stop=True)\
                      .then_inc(sem("mm_B2"), 1)
                    pe.wait_ge(sem("picked"), c * 4 + r)
                    for n in range(4):
                        for cc in range(2):
                            mm = pe.matmul(ps[:, 1 + n, :], xT[:, cc, r * P:(r + 1) * P],
                                           ew12[:, cc, n * 512:(n + 1) * 512], start=(cc == 0), stop=(cc == 1))
                    mm.then_inc(sem("mm_B2"), 1)
                pe.wait_ge(sem("hidden_2"), c * 2 + 2)
                for r in range(R):
                    mm = pe.transpose(ps[:, 0, r * P:(r + 1) * P], z[:, r, 0:HF], identf[:, :])
                mm.then_inc(sem("tr_B2"), 1)
                pe.wait_ge(sem("xT_B2"), xt + 6)
                pe.wait_ge(sem("picked"), c * 4 + 4)
                for r in range(R):
                    pe.wait_ge(sem("expert_out"), c * 4 + r)
                    for n in range(4):
                        mm = pe.matmul(ps[:, 1 + n, :],
                                       z2[:, :, :].rearrange("p r e -> p (r e)")[:, r * P:(r + 1) * P],
                                       ew3[:, n * 512:(n + 1) * 512], start=True, stop=True)
                    mm.then_inc(sem("down_2"), 1)
                pe.wait_ge(sem("expert_out"), c * 4 + 4)
                transposes("B2", c, 6, hb, sem("hb_B2"), c * 3 + 3)
                feature_major("B2", wt["wq3"], 2, xt + 7, free=(proj_t, c + 20))
            attend(3, False, ((proj_t, 24), (sem("sixseven_B2"), 16)))
            pe.wait_ge(sem("normed_3"), 16)
            with pe.Fori(0, NC) as c:
                o_proj("B3", wt["wo3"], c, 2, 8)
                transposes("B3", c, 1, hb, sem("hb_B3"), c + 1)
                pe.wait_ge(sem("xT_B3"), c * 2 + 2)
                pe.wait_ge(sem("fw_ready"), 3)
                for f in range(FF // P):
                    b = 2 + 2 * (f % 2)
                    pe.wait_ge(sem("up_done"), c * 6 + max(0, f - 1))
                    for u in range(2):
                        for cc in range(2):
                            mm = pe.matmul(ps[:, b + u, :], wgu[:, u, cc, f * P:(f + 1) * P], xT[:, cc, :],
                                           start=(cc == 0), stop=(cc == 1))
                    mm.then_inc(sem("mm_B3"), 1)
                pe.wait_ge(sem("up_done"), c * 6 + 6)
                pe.wait_ge(sem("sixseven_B3"), c * 2 + 1)
                for r in range(R):
                    for f in range(FF // P):
                        mm = pe.matmul(ps[:, 6 + r // 2, (r % 2) * E:(r % 2) * E + E], hT[:, f, r * P:(r + 1) * P],
                                       wd[:, f, :], start=(f == 0), stop=(f == FF // P - 1))
                mm.then_inc(sem("mm_B3"), 1)

        @block.vector
        def _(dve):
            ch = Chain(dve, sem("vector_chain"))
            link, note, join = ch.link, ch.note, ch.join

            def layernorm(p, c, k, src, dst, eps, g=None, b=None, signal=None):
                w = src.shape[-1]
                apart(dve)
                for r in range(R):
                    note(dve.bn_stats(st[:, r, :], src[:, r, :]))
                join()
                apart(dve)
                for r in range(R):
                    note(dve.bn_aggr(mv[:, r, :], st[:, r, :]))
                join()
                dve.tensor_scalar(ve[:, :], mv[:, :, 1], eps, None, ALU.add).then_inc(ln_var, 1)
                dve.wait_ge(ln_rstd, ln_n(p, c, k) + 1)
                for r in range(R):
                    ins = dve.tensor_scalar(dst[:, r, :], src[:, r, :], mv[:, r, 0:1], rs[:, r:r + 1],
                                            ALU.subtract, ALU.mult)
                    if g is None and r == R - 1 and signal is not None:
                        ins.then_inc(signal, 1)
                    else:
                        note(ins)
                if g is not None:
                    join()
                    link(dve.tensor_tensor(dst, dst, wide(g, w), ALU.mult))
                    ins = dve.tensor_tensor(dst, dst, wide(b, w), ALU.add)
                    if signal is not None:
                        ins.then_inc(signal, 1)
                    else:
                        link(ins)
                elif signal is None:
                    join()

            def wide(row, w):
                return row[:, 0:w].unsqueeze(1).to_broadcast([P, R, w])

            def chunk6():
                return ps[:, 6:8, :].rearrange("p b (r e) -> p (b r) e", e=E)

            def split(p, c, k):
                n = split_n(p, c, k)
                dve.wait_ge(proj_t, n + 1)
                dve.wait_ge(parts_out, n * 48)
                dve.tensor_copy(parts[0], pt).then_inc(part_hi, 1)
                dve.wait_ge(part_hi, n + 1)
                dve.wait_ge(part_lo, n)
                dve.tensor_tensor(pr, pt, parts[0], ALU.subtract).then_inc(part_rest, 1)

            def stage_v(p, c, k, mm_at, bias=None):
                dve.wait_ge(sem(f"mm_{p}"), mm_at)
                dve.wait_ge(v_out, v_n(p, c, k) * 16)
                src = chunk6().rearrange("p r (h d) -> p r h d", d=D)
                if bias is None:
                    dve.tensor_copy(vst[:, :, :, 0:D], src).then_inc(v_staged, 1)
                else:
                    link(dve.tensor_tensor(z[:, :, :], chunk6(), wide(bias, E), ALU.add))
                    dve.tensor_copy(vst[:, :, :, 0:D], z[:, :, :].rearrange("p r (h d) -> p r h d", d=D))\
                       .then_inc(v_staged, 1)

            for half in range(2):
                link(dve.memset(stackK[half][QROWS:QROWS + 3, :, :], 1.0))
            dve.wait_ge(consts, N_CONST)
            dve.wait_ge(x_in, 64)
            with dve.Fori(0, NC) as c:
                ch.loop(c, 13)
                dve.wait_ge(sem("tr_A"), c)
                layernorm("A", c, 0, x_sb[:, ds(c * 4, 4), :], hb[:, :, :], 1e-5, signal=sem("hb_A"))
                note(dve.tensor_copy(xmean[:, ds(c * 4, 4)], mv[:, :, 0]))
                note(dve.tensor_copy(xrstd[:, ds(c * 4, 4)], rs[:, :]))
                split("A", c, 0)
                split("A", c, 1)
                stage_v("A", c, 0, c * 3 + 3)
            ch.end(NC)
            with dve.Fori(0, NC) as c:
                ch.loop(c, 1)
                split("C", c, 0)
                split("C", c, 1)
                stage_v("C", c, 0, c * 4 + 3)
                stage_v("C", c, 1, c * 4 + 4, rows["bv3"])
            ch.end(NC)

            def attend(a, causal):
                steps = steps_of(causal)
                T = len(steps)
                keys = S if causal else CTX
                ends = [max(t for t, s in enumerate(steps) if s[0] == qc) + 1 for qc in range(NC)]
                with dve.Fori(0, NG // 2) as i:
                    ch.loop(i, 16)
                    for half in range(2):
                        g = i * 2 + half
                        dve.wait_ge(sem(f"max_T_{a}"), g)
                        for w in range(4 * S // P):
                            nk = (w % (S // P) + 1) * P if causal else keys
                            dve.wait_ge(sem(f"rows_{a}"), g * 64 + (w + 1))
                            b0 = 4 * (w % 2)
                            dve.tensor_reduce(mx[:, w:w + 1],
                                              ps[:, b0:b0 + 4, :].rearrange("p b n -> p (b n)")[:, 0:nk],
                                              AX.X, ALU.max).then_inc(sem(f"maxima_{a}"), 1)
                        dve.wait_ge(sem(f"max_T_{a}"), g + 1)
                        dve.wait_ge(sem(f"max_out_{a}"), g * 48)
                        link(dve.tensor_scalar(mneg[:, :], ps[0:64, 0, 0:P], -1.0, None, ALU.mult))
                        link(dve.tensor_copy(mparts[:, 0, :], mneg[:, :]))
                        link(dve.tensor_tensor(mres[:, :], mneg[:, :], mparts[:, 0, :], ALU.subtract))
                        link(dve.tensor_copy(mparts[:, 1, :], mres[:, :]))
                        dve.tensor_tensor(mparts[:, 2, :], mres[:, :], mparts[:, 1, :], ALU.subtract)\
                           .then_inc(sem(f"max_split_{a}"), 1)
                        for qc in range(NC):
                            b = 6 + qc % 2
                            dve.wait_ge(sem(f"pv_{a}"), g * T + ends[qc])
                            if qc >= 2:
                                dve.wait_ge(sem(f"acc_T{half}_{a}"), i * 4 + (qc - 1))
                            dve.tensor_copy(accS[:, qc % 2, :], ps[:, b, :]).then_inc(sem(f"acc_out_{a}"), 1)
                            dve.wait_ge(sem(f"acc_T{half}_{a}"), i * 4 + (qc + 1))
                            acc = ps[:, b, :].rearrange("p (r j d) -> p r j d", r=R, d=32)
                            link(dve.reciprocal(rec[:, :].rearrange("p (r j) -> p r j", r=R), acc[:, :, :, D]))
                            dve.tensor_tensor(
                                o_sb[:, 4 * qc:4 * qc + 4, ds(g * 64, 64)].rearrange("p r (j d) -> p r j d", d=D),
                                acc[:, :, :, 0:D],
                                rec[:, :].rearrange("p (r j) -> p r j", r=R).unsqueeze(3).to_broadcast([P, R, 4, D]),
                                ALU.mult).then_inc(sem(f"normed_{a}"), 1)
                ch.end(NG // 2)

            attend(1, True)
            dve.wait_ge(weights_in, W_ALL)
            dve.wait_ge(sem("tanh_done"), 1)
            with dve.Fori(0, NC) as c:
                ch.loop(c, 18)
                dve.wait_ge(sem("mm_B1"), c * 2 + 1)
                dve.tensor_tensor(z[:, :, :], chunk6(), wide(rows["bo1"], E), ALU.add).then_inc(sem("sixseven_B1"), 1)
                dve.wait_ge(sem("sixseven_B1"), c + 1)
                dve.wait_ge(sem("tr_B1"), c * 2 + 1)
                for r in range(R):
                    note(dve.tensor_scalar(hb[:, r, :], x_sb[:, ds(c * 4 + r, 1), :].rearrange("p o e -> p (o e)"),
                                           xmean[:, ds(c * 4 + r, 1)], xrstd[:, ds(c * 4 + r, 1)],
                                           ALU.subtract, ALU.mult))
                join()
                link(dve.scalar_tensor_tensor(out=z2[:, :, :], in0=z[:, :, :], scalar=0.0, in1=hb[:, :, :],
                                              op0=ALU.max, op1=ALU.add))
                layernorm("B1", c, 0, z2[:, :, :], hb[:, :, :], 1e-6, rows["g1"], rows["b1"], signal=sem("hb_B1"))
                split("B1", c, 0)
            ch.end(NC)
            attend(2, False)

            dve.wait_ge(sem("ew_in"), 80)
            link(dve.tensor_copy(midx, midx_i[:, 1, :]))
            link(dve.tensor_scalar(mtmp, midx, 0.0, float(S), ALU.is_lt, ALU.mult))
            link(dve.tensor_tensor(midx, midx, mtmp, ALU.add))
            link(dve.tensor_copy(mtmp2, midx_i[:, 0, :]))
            link(dve.tensor_scalar(mtmp, mtmp2, 0.0, None, ALU.is_equal))
            link(dve.tensor_scalar(mtmp2, mtmp2, -1.0, None, ALU.is_equal))
            link(dve.tensor_tensor(mtmp, mtmp, mtmp2, ALU.add))
            link(dve.scalar_tensor_tensor(out=midx, in0=midx, scalar=1.0, in1=mtmp, op0=ALU.add, op1=ALU.mult))
            for t in range(S // P):
                link(dve.tensor_scalar(mtmp, midx, tok_id[:, t:t + 1], None, ALU.is_equal))
                link(dve.tensor_reduce(routed[:, t:t + 1], mtmp, AX.X, ALU.max))

            six = sem("sixseven_B2")
            mm, tr = sem("mm_B2"), sem("tr_B2")
            with dve.Fori(0, NC) as c:
                ch.loop(c, 155)
                m = c * 14
                xc = x_sb[:, ds(c * 4, 4), :]
                hid = z[:, :, 0:HF]
                dve.wait_ge(mm, m + 1)
                dve.tensor_tensor(z[:, :, :], chunk6(), wide(rows["bo2"], E), ALU.add).then_inc(six, 1)
                dve.wait_ge(six, c * 4 + 1)
                link(dve.tensor_scalar(z[:, :, :], z[:, :, :], 0.0, None, ALU.max))
                dve.wait_ge(tr, c * 7 + 1)
                layernorm("B2", c, 0, z[:, :, :], hb[:, :, :], 0.25e-6, rows["g2"], rows["b2"], signal=sem("hb_B2"))
                dve.wait_ge(mm, m + 2)
                dve.tensor_tensor(z[:, :, :], chunk6(), wide(rows["bf"], E), ALU.add).then_inc(six, 1)
                dve.wait_ge(six, c * 4 + 2)
                link(dve.scalar_tensor_tensor(out=z2[:, :, :], in0=z[:, :, :], scalar=0.0, in1=hb[:, :, :],
                                              op0=ALU.max, op1=ALU.add))
                layernorm("B2", c, 1, z2[:, :, :], z2[:, :, :], 1e-6, rows["g3"], rows["b3"])
                link(dve.scalar_tensor_tensor(out=xc, in0=z2[:, :, :], scalar=tg[:, 0:1], in1=xc,
                                              op0=ALU.mult, op1=ALU.add))
                dve.wait_ge(tr, c * 7 + 2)
                layernorm("B2", c, 2, xc, hb[:, :, :], 1e-5, signal=sem("hb_B2"))
                dve.wait_ge(mm, m + 3)
                logits = ps[:, 5, 0:R * 16].rearrange("p (r n) -> p r n", r=R)[:, :, 0:NE + 1]
                dve.tensor_tensor(sc[:, :, 0:NE + 1], logits, wide(rows["gateb"], NE + 1), ALU.add)\
                   .then_inc(sem("gate_in"), 1)
                dve.wait_ge(mm, m + 4)
                dve.tensor_tensor(z[:, :, :], chunk6(), wide(rows["sb12"], E), ALU.add).then_inc(six, 1)
                dve.wait_ge(sem("silu_2"), c * 2 + 1)
                link(dve.tensor_tensor(hid, sg[:, :, :], z[:, :, HF:E], ALU.mult))
                layernorm("B2", c, 3, hid, hid, 1e-5, rows["slg"], rows["slb"], signal=sem("hidden_2"))
                dve.wait_ge(mm, m + 5)
                dve.tensor_tensor(shr, chunk6(), wide(rows["sb3"], E), ALU.add).then_inc(six, 1)
                dve.wait_ge(sem("sig_2"), c * 3 + 1)
                io = iota8[:, :].unsqueeze(1).to_broadcast([P, R, NE])
                link(dve.tensor_tensor(sel[:, :, :], sc[:, :, 0:NE], wide(rows["expb"], NE), ALU.add))
                link(dve.tensor_reduce(small[:, 0, :], sel[:, :, :], AX.X, ALU.max))
                link(dve.tensor_tensor(oh[:, :, :], sel[:, :, :],
                                       small[:, 0, :].unsqueeze(2).to_broadcast([P, R, NE]), ALU.is_ge))
                link(dve.tensor_tensor(sel[:, :, :], oh[:, :, :], io, ALU.mult))
                link(dve.tensor_reduce(small[:, 1, :], sel[:, :, :], AX.X, ALU.min))
                dve.tensor_tensor(oh[:, :, :], io, small[:, 1, :].unsqueeze(2).to_broadcast([P, R, NE]),
                                  ALU.is_equal).then_inc(sem("onehot"), 1)
                dve.wait_ge(sem("onehot"), c + 1)
                link(dve.tensor_tensor(sel[:, :, :], oh[:, :, :], sc[:, :, 0:NE], ALU.mult))
                link(dve.tensor_reduce(small[:, 5, :], sel[:, :, :], AX.X, ALU.add))
                dve.tensor_tensor(small[:, 2, :], sc[:, :, NE], small[:, 5, :], ALU.subtract)\
                   .then_inc(sem("gate_diff"), 1)
                dve.wait_ge(sem("sig_2"), c * 3 + 3)
                rt = routed[:, ds(c * 4, 4)]
                link(dve.scalar_tensor_tensor(out=small[:, 6, :], in0=small[:, 3, :], scalar=-1.0, in1=rt,
                                              op0=ALU.add, op1=ALU.mult))
                link(dve.tensor_scalar(small[:, 6, :], small[:, 6, :], 1.0, None, ALU.add))
                link(dve.tensor_tensor(small[:, 7, :], small[:, 4, :], rt, ALU.mult))
                up = ps[:, 1:5, :].rearrange("p (u b) (e h) -> p u (b e) h", u=2, h=HF)
                for r in range(R):
                    dve.wait_ge(sem("bsel_2"), c * 4 + (r + 1))
                    dve.wait_ge(mm, m + (7 + 2 * r))
                    acc = hs[:, r, :].rearrange("p (u h) -> p u h", u=2)
                    for e in range(NE):
                        start = bsel[:, r, 0:2 * HF].rearrange("p (u h) -> p u h", u=2)
                        ins = dve.scalar_tensor_tensor(out=acc, in0=up[:, :, e, :], scalar=oh[:, r, e:e + 1],
                                                       in1=acc if e else start, op0=ALU.mult, op1=ALU.add)
                        if e < NE - 1:
                            link(ins)
                    ins.then_inc(sem("picked"), 1)
                dve.wait_ge(sem("silu_2"), c * 2 + 2)
                dve.wait_ge(tr, c * 7 + 4)
                link(dve.tensor_tensor(hid, sg[:, :, :], hs[:, :, HF:2 * HF], ALU.mult))
                layernorm("B2", c, 4, hid, hid, 1e-5, rows["elg"], rows["elb"], signal=sem("hidden_2"))
                down = ps[:, 1:5, :].rearrange("p b (e n) -> p (b e) n", n=E)
                for r in range(R):
                    dve.wait_ge(sem("down_2"), c * 4 + (r + 1))
                    for e in range(NE):
                        ins = dve.scalar_tensor_tensor(out=eo[:, r, :], in0=down[:, e, :], scalar=oh[:, r, e:e + 1],
                                                       in1=eo[:, r, :] if e else bsel[:, r, 2 * HF:2 * HF + E],
                                                       op0=ALU.mult, op1=ALU.add)
                        if e < NE - 1:
                            link(ins)
                    ins.then_inc(sem("expert_out"), 1)
                dve.wait_ge(sem("expert_out"), c * 4 + 4)
                for r in range(R):
                    note(dve.tensor_scalar(eo[:, r, :], eo[:, r, :], small[:, 7, r:r + 1], None, ALU.mult))
                join()
                for r in range(R):
                    note(dve.scalar_tensor_tensor(out=eo[:, r, :], in0=shr[:, r, :], scalar=small[:, 6, r:r + 1],
                                                  in1=eo[:, r, :], op0=ALU.mult, op1=ALU.add))
                join()
                link(dve.scalar_tensor_tensor(out=xc, in0=eo, scalar=tg[:, 2:3], in1=xc, op0=ALU.mult, op1=ALU.add))
                dve.wait_ge(tr, c * 7 + 3)
                layernorm("B2", c, 5, xc, hb[:, :, :], 1e-5, signal=sem("hb_B2"))
                split("B2", c, 0)
            ch.end(NC)
            attend(3, False)
            dve.wait_ge(sem("fw_in"), 48)
            for u in range(2):
                dve.tensor_scalar(wgu[:, u, :, :], wint[:, u, :, :], 1.0 / 127.0, None, ALU.mult)\
                   .then_inc(sem("fw_ready"), 1)
            dve.tensor_scalar(wd, dint, 1.0 / 127.0, None, ALU.mult).then_inc(sem("fw_ready"), 1)
            six3 = sem("sixseven_B3")
            with dve.Fori(0, NC) as c:
                ch.loop(c, 12)
                m = c * 8
                xc = x_sb[:, ds(c * 4, 4), :]
                dve.wait_ge(sem("mm_B3"), m + 1)
                dve.tensor_tensor(z[:, :, :], chunk6(), wide(rows["bo3"], E), ALU.add).then_inc(six3, 1)
                dve.wait_ge(six3, c * 2 + 1)
                link(dve.scalar_tensor_tensor(out=xc, in0=z[:, :, :], scalar=tg[:, 1:2], in1=xc,
                                              op0=ALU.mult, op1=ALU.add))
                dve.wait_ge(sem("tr_B3"), c * 2 + 1)
                layernorm("B3", c, 0, xc, hb[:, :, :], 1e-5, signal=sem("hb_B3"))
                for f in range(FF // P):
                    dve.wait_ge(sem("mm_B3"), m + (2 + f))
                    dve.wait_ge(sem("silu_3"), c * 6 + (f + 1))
                    dve.tensor_tensor(hT[:, f, :], sgT[:, f % 2, :], ps[:, 3 + 2 * (f % 2), :], ALU.mult)\
                       .then_inc(sem("up_done"), 1)
                dve.wait_ge(sem("mm_B3"), m + 8)
                dve.scalar_tensor_tensor(out=xc, in0=chunk6(), scalar=tg[:, 3:4], in1=xc, op0=ALU.mult, op1=ALU.add)\
                   .then_inc(six3, 1)
            ch.end(NC)


_NAMES = {
    "wk1": "L0_xattn_Wk1", "wv1": "L0_xattn_Wv1", "wq1": "L0_xattn_Wq1", "wk2": "L0_xattn_Wk2",
    "wv2": "L0_xattn_Wv2", "wq2": "L0_xattn_Wq2", "wo1": "L0_xattn_Wo1", "wo2": "L0_xattn_Wo2",
    "wf": "L0_xattn_Wf", "bo1": "L0_xattn_bo1", "bo2": "L0_xattn_bo2", "bf": "L0_xattn_bf",
    "g1": "L0_xattn_g1", "b1": "L0_xattn_b1", "g2": "L0_xattn_g2", "b2": "L0_xattn_b2", "g3": "L0_xattn_g3",
    "b3": "L0_xattn_b3", "sb3": "L0_ffn_sb3", "slg": "L0_ffn_s_ln_g", "slb": "L0_ffn_s_ln_b",
    "elg": "L0_ffn_sel_ln_g", "elb": "L0_ffn_sel_ln_b", "expb": "L0_ffn_exp_bias",
    "index_b": "L0_ffn_index_b", "index_t": "L0_ffn_index_t",
    "wq3": "L1_xattn_Wq", "bq3": "L1_xattn_bq", "wk3": "L1_xattn_Wk", "bk3": "L1_xattn_bk",
    "wv3": "L1_xattn_Wv", "bv3": "L1_xattn_bv", "wo3": "L1_xattn_Wo", "bo3": "L1_xattn_bo",
    "x": "x", "ctx": "ctx_1024",
}


def lay_out(inputs):
    import numpy as np
    a = {k: np.asarray(inputs[v]) for k, v in _NAMES.items()}
    for n in ("wk1", "wv1", "wq1", "wk2", "wv2", "wq2"):
        a[n] = a[n].transpose(1, 0, 2).reshape(E, E)
    for n in ("bq3", "bk3"):
        a[n] = a[n].reshape(2, P).T
    f = {k: np.asarray(inputs["L0_ffn_" + k]) for k in
         ("sw1", "sw2", "sw3", "sb1", "sb2", "sg_w", "sg_b", "eg_w", "eg_b", "ew1", "ew2", "ew3", "eb1", "eb2", "eb3")}
    a["sw12"] = np.concatenate([f["sw1"].T, f["sw2"].T], axis=1)
    a["sb12"] = np.concatenate([f["sb1"], f["sb2"]])
    a["sw3"] = f["sw3"].T
    a["gate_w"] = np.concatenate([f["eg_w"].T, f["sg_w"].T], axis=1)
    a["gateb"] = np.concatenate([f["eg_b"], f["sg_b"]])
    a["ew12"] = np.concatenate([f["ew1"].reshape(NE * HF, E).T, f["ew2"].reshape(NE * HF, E).T], axis=1)
    a["ew3"] = f["ew3"].transpose(2, 0, 1).reshape(HF, NE * E)
    a["eb"] = np.concatenate([f["eb1"], f["eb2"], f["eb3"]], axis=1)
    a["gates"] = np.concatenate([np.asarray(inputs["g_xattn"]), np.asarray(inputs["g_ffn"])])
    a["w_gate"] = np.asarray(inputs["L1_ffn_w_gate"]).T
    a["w_up"] = np.asarray(inputs["L1_ffn_w_up"]).T
    a["w_down"] = np.asarray(inputs["L1_ffn_w_down"]).T
    return {k: np.ascontiguousarray(v) for k, v in a.items()}


def kernel(**inputs):
    import concourse.bacc as _bacc
    from concourse import mybir as _mybir
    from concourse.bass_utils import run_bass_kernel_spmd as _run

    nc = _bacc.Bacc("TRN2", target_bir_lowering=False, num_devices=1)
    arrays, A = {}, {}
    for name, a in lay_out(inputs).items():
        arrays[f"in_{name}"] = a
        A[name] = nc.dram_tensor(f"in_{name}", a.shape, _mybir.dt.from_np(a.dtype), kind="ExternalInput").ap()
    out = nc.dram_tensor("out_0", (1, S, E), _mybir.dt.float32, kind="ExternalOutput").ap()
    build(nc, A, out)
    r = _run(nc, [arrays], core_ids=[0])
    return r.results[0]["out_0"]
```

```python
from contextlib import ExitStack

import concourse.bass as bass
from concourse import mybir

F32 = mybir.dt.float32
BF16 = mybir.dt.bfloat16
I32 = mybir.dt.int32
ALU = mybir.AluOpType
ACT = mybir.ActivationFunctionType
AX = mybir.AxisListType
ds = bass.ds

P = 128
S = 2048
E = 256
H = 16
D = E // H
CTX = 1601
CH = 512
NC = S // CH
R = CH // P
NG = H // 4
HF = 128
NE = 8
M = 512
FF = 768
QROWS = 6 * D
MASKED = -3.0e38
START = 2

Q_PARTS = (0, 0, 1, 1, 0, 2)
K_PARTS = (0, 1, 0, 1, 2, 0)


PASSES = ("A", "C", "B1", "B2_0", "B2_1", "MOE", "B2", "B3")
SIGNALS = {
    "tensor": [f"{n}_{p}" for n in ("tr", "mm") for p in PASSES]
    + [f"{n}_{a}" for n in ("ring_full", "scores", "pv") for a in (1, 2, 3)] + ["scattered"],
    "scalar": ["proj_t", "tanh_done", "gates_out", "silu_moe", "silu_3", "bias_moe", "onehot_t"]
    + [f"{n}_{u}" for n in ("relu", "silu", "shared") for u in (0, 1)]
    + [f"xT_{p}" for p in PASSES] + [f"exp_{a}" for a in (1, 2, 3)],
    "vector": ["part_hi", "part_rest", "v_staged", "ln_var", "hidden_0", "hidden_1", "hidden_moe", "gate_in",
               "gate_diff", "onehot", "picked", "expert_out", "gather_map", "scatter_map", "entries", "merged",
               "up_done", "fw_ready"]
    + [f"hb_{p}" for p in ("A", "B1", "B2_0", "B2_1", "B2", "B3")] + [f"sixseven_{p}" for p in ("B1", "B3")]
    + [f"{n}_{a}" for n in ("ring_free", "mx_ready", "max_split", "acc_out", "normed") for a in (1, 2, 3)],
    "gpsimd": ["consts", "part_mid", "part_lo", "ln_rstd", "ctx_pad", "o_taken_B1", "o_taken_B2_0", "o_taken_B2_1",
               "o_taken_B3", "kept", "token_row", "ones_again"],
    "sync": ["x_in", "index_in", "bias_in", "weights_in", "parts_out", "v_out", "ctx_in", "ew_in", "fw_in", "out_done"]
    + [f"{n}_{a}" for n in ("v_in", "stacks_in", "max_out", "max_in") for a in (1, 2, 3)],
}


class Chain:

    def __init__(self, eng, sem):
        self.eng, self.sem, self.base, self.k, self.it = eng, sem, 0, 0, None

    def loop(self, it, per):
        self.base, self.k, self.it, self.per = self.base + self.k, 0, it, per

    def end(self, times):
        assert self.k == self.per, (self.k, self.per)
        self.base, self.k, self.it = self.base + times * self.per, 0, None

    def link(self, ins):
        self.note(ins)
        self.join()

    def note(self, ins):
        self.k += 1
        ins.then_inc(self.sem, 1)

    def join(self):
        at = self.base + self.k
        self.eng.wait_ge(self.sem, at if self.it is None else self.it * self.per + at)


KT = -(-CTX // P)
FIRST, RING = 4, 3
ACC = 7
QW = S // 2
WT = QW // P


def steps_of(causal, qp):
    out = []
    for h in range(2):
        qc = 2 * qp + h if causal else h
        kts = range(R * qc + R) if causal else range(KT)
        for kt in kts:
            c0 = max(0, kt - R * qc) * P if causal else 0
            kn = P if causal else min(P, CTX - kt * P)
            out.append((h, kt, c0, kn, kt == kts[-1]))
    return out


def tiles_of(causal, qp):
    out = []
    for q8 in range(WT):
        nk = (WT * qp + q8 + 1) * P if causal else CTX // CH * CH
        for j in range(4):
            for kb in range(-(-nk // CH)):
                n = min(CH, nk - kb * CH)
                out.append((j, 1, q8, kb, n, causal and kb * CH + n == nk))
        if not causal:
            out.append((0, 4, q8, CTX // CH, CTX % CH, False))
    return out


def ring_base(causal, g, qp):
    tiles = [len(tiles_of(causal, w if causal else 0)) + 1 for w in range(2)]
    if g < 0:
        return qp * tiles[0]
    full = [t + 2 for t in tiles]
    if g < NG - 1:
        return qp * full[0] + (sum(tiles) + g * sum(full))
    return qp * 2 + (sum(tiles) + g * sum(full))


def step_base(causal, g, qp):
    if causal:
        per = [len(steps_of(True, w)) for w in range(2)]
        return g * sum(per) + sum(per[:qp])
    n = len(steps_of(False, 0))
    return qp * n + g * 2 * n


def spread(causal, qp):
    steps, tiles = steps_of(causal, qp), tiles_of(causal, qp)
    first = 3
    n = len(steps) - first
    per = [[] for _ in steps]
    for i in range(len(tiles)):
        per[first + i * n // len(tiles)].append(i)
    return [(t[:len(t) * 3 // 10], t[len(t) * 3 // 10:len(t) * 7 // 10], t[len(t) * 7 // 10:]) for t in per]


def build(nc, A, out):
    ctx = ExitStack()
    with ctx:
        def sb(name, shape, dt=F32):
            return ctx.enter_context(nc.sbuf_tensor(name, shape, dt))

        sems = {}

        def sem(name):
            if name not in sems:
                sems[name] = ctx.enter_context(nc.semaphore(name))
            return sems[name]

        x_sb = sb("x_sb", [P, S // P, E])
        xmean = sb("xmean", [P, S // P])
        xrstd = sb("xrstd", [P, S // P])
        o_sb = sb("o_sb", [P, S // P, E])
        hb = sb("hb", [P, R, E])
        xT = sb("xT", [P, 2, CH])
        z = sb("z", [P, R, E])
        z2 = sb("z2", [P, R, E])
        st, mv, ve, rs = ([sb(f"{n}{u}", [P, R, *w]) for u in range(2)]
                          for n, w in (("st", [6]), ("mv", [2]), ("ve", []), ("rs", [])))
        mhalf = sb("mhalf", [P, R])
        identf = sb("identf", [P, P])
        identb = sb("identb", [P, P], BF16)
        mask_kq = sb("mask_kq", [P, P], BF16)
        mask_qk = sb("mask_qk", [P, P], BF16)
        accS = sb("accS", [P, 2, CH])
        rec = sb("rec", [P, R * 4])
        mxb = [sb(f"mxb{w}", [P, 4 * WT, 4]) for w in range(2)]
        mx = sb("mx", [P, 4 * WT])
        mneg = sb("mneg", [4 * WT, P])
        mres = sb("mres", [4 * WT, P])
        mparts = sb("mparts", [4 * WT, 3, P], BF16)
        wt = {n: sb(n, [P, 2, E]) for n in ("wq1", "wk1", "wv1", "wo1", "wq2", "wk2", "wv2", "wo2", "wf",
                                            "wq3", "wk3", "wv3", "wo3", "sw12")}
        sw3 = sb("sw3", [P, E])
        gate_w = sb("gate_w", [P, 2, 16])
        bias_col = {n: sb(n, [P, 2]) for n in ("bq3", "bk3")}
        rows = {}
        for n, w in (("bo1", E), ("g1", E), ("b1", E), ("g2", E), ("b2", E), ("g3", E),
                     ("b3", E), ("bv3", E), ("bo3", E), ("slg", HF), ("slb", HF),
                     ("elg", HF), ("elb", HF), ("gateb", 16), ("expb", NE)):
            rows[n] = sb("row_" + n, [P, w])
        bias_row = {n: wt[w][0:1, k, :] for n, w, k in (("bo2", "wq1", 0), ("bf", "wq1", 1), ("sb12", "wk1", 0),
                                                       ("sb3", "wk1", 1))}
        tg = sb("tg", [P, 4])
        iota8 = sb("iota8", [P, NE])
        tok_id = sb("tok_id", [P, S // P])
        code = sb("code", [P, M + R])
        first_code = sb("first_code", [P, R])
        entry_id = sb("entry_id", [P, R])
        ones = sb("ones", [1, P])
        sc = sb("sc", [P, R, 16])
        sel = sb("sel", [P, R, NE])
        oh = sb("oh", [P, R, NE])
        small = sb("small", [P, 8, R])
        ohT = sb("ohT", [NE, R, P])

        arena = sb("arena", [P, 26624])

        def region(at, shape, dt=F32):
            n = 1
            for d in shape:
                n *= d
            words = n if dt != BF16 else n // 2
            v = arena[:, at:at + words]
            if dt != F32:
                v = v.bitcast(dt)
            if len(shape) == 2:
                v = v.rearrange("p (a b) -> p a b", b=shape[1])
            elif len(shape) == 3:
                v = v.rearrange("p (a b c) -> p a b c", b=shape[1], c=shape[2])
            return v

        stackQ = [region(4096 * h, (4, S), BF16) for h in range(2)]
        stackK = [region(8192 + 4096 * h, (4, S), BF16) for h in range(2)]
        probs = [region(16384 + 1024 * n, (2, CH)) for n in range(4)]
        vg = [region(22528 + 2048 * h, (S // P, 4, 32)) for h in range(2)]
        pt = region(16384, (2, CH))
        pr = region(17408, (2, CH))
        parts = [region(18432 + 512 * n, (2, CH), BF16) for n in range(3)]
        vst = region(19968, (R, H, 32))
        ew12 = region(0, (2, 2 * NE * HF))
        ew3 = region(4096, (NE * E,))
        eb = region(6144, (2 * HF + E,))
        hb_1 = region(24064, (R, E))
        z_1 = region(17408, (R, E))
        z2_1 = region(18432, (R, E))
        HB, XT, Z, Z2 = (hb, hb_1), (xT, accS), (z, z_1), (z2, z2_1)
        SG = [region(25088 + 512 * u, (R, HF)) for u in range(2)]
        shr = region(19968, (S // P, E))
        which = region(8192, (S // P, M))
        where_to = region(8192, (R, S))
        bsel = region(16384, (R, 2 * HF + E))
        hs = region(24064, (R, 2 * HF))
        vals = region(6656, (R, E + 4))
        row_id = region(24064, (M,))
        mtmp = region(24576, (M,))
        idx_i = region(25088, (2, M + R), I32)
        wgu = region(0, (2, 2, FF))
        wd = region(3072, (FF // P, E))
        hT = region(4608, (FF // P, CH))
        sgT = region(7680, (2, CH))
        wint = region(8704, (2, 2, FF), I32)
        dint = region(11776, (FF // P, E), I32)

        ps = ctx.enter_context(nc.psum_tensor("ps", [P, 8, 512], F32))

        scr_qk = {}
        for n in ("q1", "k1", "q2", "k2", "q3", "k3"):
            scr_qk[n] = nc.dram_tensor("scr_" + n, [3, E, S], BF16, kind="Internal").ap()
        scr_v = {n: nc.dram_tensor("scr_" + n, [S, H * 32], F32, kind="Internal").ap() for n in ("v1", "v2", "v3")}
        scr_m = nc.dram_tensor("scr_m", [3, 3, NG * 2, 4 * QW], BF16, kind="Internal").ap()

        weights_early = []

        def w2(name, src):
            weights_early.append((wt[name][:, :, :], src.rearrange("(c p) n -> p c n", p=P)))

        for n in ("wq1", "wk1", "wv1", "wo1", "wq2", "wk2", "wv2", "wo2", "wf", "wq3", "wk3", "wv3", "wo3", "sw12"):
            w2(n, A[n])
        weights_early.append((sw3[:, :], A["sw3"]))
        weights_early.append((gate_w[:, :, 0:NE + 1], A["gate_w"].rearrange("(c p) n -> p c n", p=P)))
        for n in ("bq3", "bk3"):
            weights_early.append((bias_col[n][:, :], A[n]))
        for n in rows:
            w = A[n].shape[0]
            weights_early.append((rows[n][:, 0:w], A[n].partition_broadcast(P)))
        weights_early.append((tg[:, :], A["gates"].partition_broadcast(P)))

        weights_in = sem("weights_in")
        x_in = sem("x_in")
        W_ALL = 16 * len(weights_early)

        dma_jobs = {}
        NORM = dict(A=1)

        SPLITS = {"A": (0, 2), "C": (8, 2), "B1": (16, 1), "B2": (20, 1)}
        VSTORES = {"A": (0, 1), "C": (4, 2)}
        LNS = {"A": (0, 1), "B1": (4, 1), "B2x": (8, 8), "MOE": (24, 1), "B2": (25, 1), "B3": (29, 1)}

        def split_n(p, c, k):
            base, per = SPLITS[p]
            return c * per + (base + k)

        def v_n(p, c, k):
            base, per = VSTORES[p]
            return c * per + (base + k)

        def ln_n(p, c, k):
            base, per = LNS[p]
            return c * per + (base + k)

        proj_t, part_hi, part_rest, part_mid, part_lo, parts_out = (
            sem(n) for n in ("proj_t", "part_hi", "part_rest", "part_mid", "part_lo", "parts_out"))
        v_staged, v_out = sem("v_staged"), sem("v_out")
        ln_var, ln_rstd = sem("ln_var"), sem("ln_rstd")
        consts = sem("consts")
        N_CONST = 16

        def apart(eng):
            eng.nop(nofuse=True)

        def chunk_banks(u):
            return ps[:, 4 + 2 * u:6 + 2 * u, :].rearrange("p b (r e) -> p (b r) e", e=E)

        block = ctx.enter_context(nc.Block())

        TR = {"A": 1, "C": 1, "B1": 2, "B2_0": 4, "B2_1": 4, "B2": 1, "B3": 2}

        @block.sync
        def _(sp):
            for name in SIGNALS["sync"]:
                sp.sem_inc(sem(name), START)
            for t in range(NC):
                sp.dma_start(x_sb[:, 4 * t:4 * t + 4, :],
                             A["x"][0, t * CH:(t + 1) * CH, :].rearrange("(r p) e -> p r e", p=P)).then_inc(x_in, 16)
            sp.dma_start(idx_i[:, 0, 0:M], A["index_b"].partition_broadcast(P)).then_inc(sem("index_in"), 16)
            sp.dma_start(idx_i[:, 1, 0:M], A["index_t"].partition_broadcast(P)).then_inc(sem("index_in"), 16)
            sp.dma_start(idx_i[:, :, M:M + R], A["index_col"]).then_inc(sem("index_in"), 16)
            for dst, src in weights_early:
                sp.dma_start(dst, src).then_inc(weights_in, 16)

            def store_parts(p, c, k, name):
                n = split_n(p, c, k)
                dst = [scr_qk[name][i, :, ds(c * CH, CH)].rearrange("(o p) q -> p o q", p=P) for i in range(3)]
                sp.wait_ge(part_hi, START + n + 1)
                apart(sp)
                sp.dma_start(dst[0], parts[0]).then_inc(parts_out, 16)
                sp.wait_ge(part_lo, START + n + 1)
                apart(sp)
                sp.dma_start(dst[1], parts[1]).then_inc(parts_out, 16)
                apart(sp)
                sp.dma_start(dst[2], parts[2]).then_inc(parts_out, 16)

            def store_v(p, c, k, name):
                sp.wait_ge(v_staged, START + v_n(p, c, k) + 1)
                apart(sp)
                sp.dma_start(scr_v[name][ds(c * CH, CH), :].rearrange("(r p) n -> p r n", p=P),
                             vst.rearrange("p r h d -> p r (h d)")).then_inc(v_out, 16)

            with sp.Fori(0, NC) as c:
                store_parts("A", c, 0, "k1")
                store_parts("A", c, 1, "q1")
                store_v("A", c, 0, "v1")

            sp.wait_ge(sem("mm_A"), START + 12)
            for n, dst in bias_row.items():
                sp.dma_start(dst, A[n].unsqueeze(0)).then_inc(sem("bias_in"), 16)
            ctx_in = sem("ctx_in")
            with sp.Fori(0, 3) as c:
                sp.wait_ge(sem("tr_C"), START + c)
                apart(sp)
                sp.dma_start(hb[:, :, :], A["ctx"][0, ds(c * CH, CH), :].rearrange("(r p) e -> p r e", p=P))\
                  .then_inc(ctx_in, 16)
                store_parts("C", c, 0, "k2")
                store_parts("C", c, 1, "k3")
                store_v("C", c, 0, "v2")
                store_v("C", c, 1, "v3")
            sp.wait_ge(sem("ctx_pad"), START + 1)
            sp.dma_start(hb[0:CTX - 3 * CH, 0, :], A["ctx"][0, 3 * CH:CTX, :]).then_inc(ctx_in, 16)
            store_parts("C", 3, 0, "k2")
            store_parts("C", 3, 1, "k3")
            store_v("C", 3, 0, "v2")
            store_v("C", 3, 1, "v3")

            def attention_loads(a, parts_needed, v_needed):
                sp.wait_ge(parts_out, START + parts_needed)
                sp.wait_ge(v_out, START + v_needed)
                causal = a == 1
                for g in range(NG):
                    half = g % 2
                    if g >= 2:
                        sp.wait_ge(sem(f"acc_out_{a}"), START + 4 * (g - 1))
                    for blk in range(6):
                        for stack, parts_of, nm in ((stackQ, Q_PARTS, "q"), (stackK, K_PARTS, "k")):
                            sp.dma_start(stack[half][D * blk:D * blk + D, :, :],
                                         scr_qk[f"{nm}{a}"][parts_of[blk], g * 64:g * 64 + 64, :]
                                         .rearrange("(h d) q -> d h q", d=D))\
                              .then_inc(sem(f"stacks_in_{a}"), 16)
                    sp.dma_start(vg[half].rearrange("p k h d -> p k (h d)"),
                                 scr_v[f"v{a}"][:, g * 128:g * 128 + 128].rearrange("(k p) n -> p k n", p=P))\
                      .then_inc(sem(f"v_in_{a}"), 16)
                    sp.wait_ge(sem(f"stacks_in_{a}"), START + 192 * (g + 1))
                    sp.wait_ge(sem(f"v_in_{a}"), START + 16 * (g + 1))

                    def move_maxima(qp):
                        w = qp + 2 * g
                        sp.wait_ge(sem(f"max_split_{a}"), START + w + 1)
                        apart(sp)
                        for part in range(3):
                            sp.dma_start(scr_m[a - 1, part, ds(w, 1), :].rearrange("o (w q) -> (o w) q", q=P),
                                         mparts[:, part, :]).then_inc(sem(f"max_out_{a}"), 16)
                        sp.wait_ge(sem(f"max_out_{a}"), START + w * 48 + 48)
                        apart(sp)
                        sp.dma_start(stackQ[half][QROWS:QROWS + 3, :, ds(qp * QW, QW)],
                                     scr_m[a - 1, :, ds(w, 1), :].rearrange("t o (h q) -> t (o h) q", q=QW))\
                          .then_inc(sem(f"max_in_{a}"), 16)
                        sp.wait_ge(sem(f"max_in_{a}"), START + w * 16 + 16)
                        apart(sp)

                    if causal:
                        move_maxima(0)
                        move_maxima(1)
                    else:
                        with sp.Fori(0, 2) as qp:
                            move_maxima(qp)

            attention_loads(1, 48 * 16, 16 * 12)
            with sp.Fori(0, NC) as c:
                store_parts("B1", c, 0, "q2")
            attention_loads(2, 48 * 20, 16 * 12)
            sp.wait_ge(sem("normed_2"), START + 1)
            ew_in = sem("ew_in")
            sp.dma_start(ew12, A["ew12"].rearrange("(c p) n -> p c n", p=P)).then_inc(ew_in, 16)
            sp.dma_start(ew3, A["ew3"]).then_inc(ew_in, 16)
            sp.dma_start(eb[0:NE, :], A["eb"]).then_inc(ew_in, 16)
            with sp.Fori(0, NC) as c:
                store_parts("B2", c, 0, "q3")
            attention_loads(3, 48 * 24, 16 * 12)
            sp.wait_ge(sem("normed_3"), START + 1)
            fw_in = sem("fw_in")
            sp.dma_start(wint[:, 0, :, :], A["w_gate"].rearrange("(c p) n -> p c n", p=P)).then_inc(fw_in, 16)
            sp.dma_start(wint[:, 1, :, :], A["w_up"].rearrange("(c p) n -> p c n", p=P)).then_inc(fw_in, 16)
            sp.dma_start(dint, A["w_down"].rearrange("(c p) n -> p c n", p=P)).then_inc(fw_in, 16)
            with sp.Fori(0, NC) as c:
                sp.wait_ge(sem("sixseven_B3"), START + c * 2 + 2)
                apart(sp)
                sp.dma_start(out[0, ds(c * CH, CH), :].rearrange("(r p) e -> p r e", p=P),
                             x_sb[:, ds(c * 4, 4), :]).then_inc(sem("out_done"), 16)
            sp.wait_ge(sem("out_done"), START + 16 * NC)

        @block.gpsimd
        def _(pool):
            for name in SIGNALS["gpsimd"]:
                pool.sem_inc(sem(name), START)
            pool.memset(identf[:, :], 0.0).then_inc(consts, 1)
            pool.memset(identb[:, :], 0.0).then_inc(consts, 1)
            pool.memset(mask_kq[:, :], 0.0).then_inc(consts, 1)
            pool.memset(mask_qk[:, :], 0.0).then_inc(consts, 1)
            pool.wait_ge(consts, START + 4)
            pool.affine_select(out=identf[:, :], in_=identf[:, :], compare_op=ALU.not_equal, fill=1.0, base=0,
                               pattern=[[-1, P]], channel_multiplier=1).then_inc(consts, 1)
            pool.affine_select(out=identb[:, :], in_=identb[:, :], compare_op=ALU.not_equal, fill=1.0, base=0,
                               pattern=[[-1, P]], channel_multiplier=1).then_inc(consts, 1)
            pool.affine_select(out=mask_kq[:, :], in_=mask_kq[:, :], compare_op=ALU.is_ge, fill=MASKED, base=0,
                               pattern=[[1, P]], channel_multiplier=-1).then_inc(consts, 1)
            pool.affine_select(out=mask_qk[:, :], in_=mask_qk[:, :], compare_op=ALU.is_ge, fill=MASKED, base=0,
                               pattern=[[-1, P]], channel_multiplier=1).then_inc(consts, 1)
            pool.memset(mhalf[:, :], -0.5).then_inc(consts, 1)
            pool.memset(vst, 0.0).then_inc(consts, 1)
            pool.wait_ge(consts, START + 10)
            pool.memset(vst[:, :, :, D:D + 1], 1.0).then_inc(consts, 1)
            pool.iota(iota8[:, :], [[1, NE]], base=-NE, channel_multiplier=0,
                      allow_small_or_imprecise_dtypes=True).then_inc(consts, 1)
            pool.iota(tok_id[:, :], [[P, S // P]], base=1, channel_multiplier=1,
                      allow_small_or_imprecise_dtypes=True).then_inc(consts, 1)

            pool.memset(ones[:, :], 1.0).then_inc(consts, 1)
            pool.iota(row_id, [[1, M]], base=-M, channel_multiplier=0,
                      allow_small_or_imprecise_dtypes=True).then_inc(consts, 1)
            pool.iota(entry_id[:, :], [[P, R]], base=-M, channel_multiplier=1,
                      allow_small_or_imprecise_dtypes=True).then_inc(consts, 1)

            def rstd(p, c, k, u=0):
                n = ln_n(p, c, k)
                pool.wait_ge(ln_var, START + n + 1)
                pool.tensor_tensor(rs[u][:, :], ve[u][:, :], mhalf[:, :], ALU.pow).then_inc(ln_rstd, 1)

            def split(p, c, k):
                n = split_n(p, c, k)
                pool.wait_ge(part_rest, START + n + 1)
                pool.wait_ge(parts_out, START + n * 48)
                apart(pool)
                pool.tensor_copy(parts[1], pr).then_inc(part_mid, 1)
                pool.wait_ge(part_mid, START + n + 1)
                pool.tensor_tensor(parts[2], pr, parts[1], ALU.subtract).then_inc(part_lo, 1)

            with pool.Fori(0, NC) as c:
                rstd("A", c, 0)
                split("A", c, 0)
                split("A", c, 1)
            with pool.Fori(0, 3) as c:
                split("C", c, 0)
                split("C", c, 1)
            pool.wait_ge(sem("tr_C"), START + 3)
            pool.memset(hb[:, :, :], 0.0).then_inc(sem("ctx_pad"), 1)
            split("C", 3, 0)
            split("C", 3, 1)

            def take_o(a, p, c):
                pool.wait_ge(sem(f"tr_{p}"), START + c * TR[p])
                apart(pool)
                pool.tensor_copy(hb[:, :, :], o_sb[:, ds(c * 4, 4), :]).then_inc(sem(f"o_taken_{p}"), 1)

            pool.wait_ge(sem("normed_1"), START + 1)
            with pool.Fori(0, NC) as c:
                take_o(1, "B1", c)
                rstd("B1", c, 0)
                split("B1", c, 0)
            pool.wait_ge(sem("normed_2"), START + 1)
            with pool.Fori(0, NC // 2) as c:
                for u in range(2):
                    p = f"B2_{u}"
                    pool.wait_ge(sem(f"tr_{p}"), START + c * 4)
                    if u == 0:
                        pool.wait_ge(sem("kept"), START + c * 2)
                    apart(pool)
                    pool.tensor_copy(HB[u][:, :, :], o_sb[:, ds(c * 8 + 4 * u, 4), :]).then_inc(sem(f"o_taken_{p}"), 1)
                for k in range(3):
                    for u in range(2):
                        rstd("B2x", c, 2 * k + u, u)
                for u in range(2):
                    pool.wait_ge(sem(f"hb_B2_{u}"), START + c * 2 + 2)
                    pool.wait_ge(sem(f"o_taken_B2_{u}"), START + c + 1)
                    apart(pool)
                    pool.tensor_copy(o_sb[:, ds(c * 8 + 4 * u, 4), :], HB[u][:, :, :]).then_inc(sem("kept"), 1)
                for u in range(2):
                    rstd("B2x", c, 6 + u, u)
            pool.wait_ge(sem("mm_MOE"), START + 1)
            pool.iota(where_to, [[0, R], [1, S]], base=1, channel_multiplier=0,
                      allow_small_or_imprecise_dtypes=True).then_inc(sem("token_row"), 1)
            rstd("MOE", 0, 0)
            with pool.Fori(0, NC) as c:
                rstd("B2", c, 0)
                split("B2", c, 0)
            pool.wait_ge(sem("scattered"), START + NC)
            pool.wait_ge(part_lo, START + 24)
            for half in range(2):
                pool.memset(stackK[half][QROWS:QROWS + 3, :, :], 1.0).then_inc(sem("ones_again"), 1)
                pool.wait_ge(sem("ones_again"), START + half + 1)
            pool.wait_ge(sem("normed_3"), START + 1)
            with pool.Fori(0, NC) as c:
                take_o(3, "B3", c)
                rstd("B3", c, 0)

        @block.scalar
        def _(act):
            for name in SIGNALS["scalar"]:
                act.sem_inc(sem(name), START)
            def evac_T(p, c, k, mm_before, bank=0, dst=None):
                act.wait_ge(sem(f"tr_{p}"), START + c * TR[p] + k + 1)
                act.wait_ge(sem(f"mm_{p}"), START + mm_before)
                act.activation(xT[:, :, :] if dst is None else dst, ps[:, bank:bank + 2, :],
                               ACT.Copy).then_inc(sem(f"xT_{p}"), 1)

            def take_proj(p, c, k, bank, mm_at, bias=None):
                n = split_n(p, c, k)
                act.wait_ge(sem(f"mm_{p}"), START + mm_at)
                act.wait_ge(part_rest, START + n)
                if bias is None:
                    act.activation(pt, ps[:, bank:bank + 2, :], ACT.Copy).then_inc(proj_t, 1)
                else:
                    act.activation(pt[:, 0, :], ps[:, bank, :], ACT.Identity, bias=bias[:, 0:1])
                    act.activation(pt[:, 1, :], ps[:, bank + 1, :], ACT.Identity, bias=bias[:, 1:2])\
                       .then_inc(proj_t, 1)

            act.wait_ge(weights_in, START + W_ALL)
            act.activation(tg[:, :], tg[:, :], ACT.Tanh).then_inc(sem("tanh_done"), 1)
            with act.Fori(0, NC) as c:
                evac_T("A", c, 0, c * 3)
                take_proj("A", c, 0, 2, c * 3 + 1)
                take_proj("A", c, 1, 4, c * 3 + 2)
            with act.Fori(0, NC) as c:
                evac_T("C", c, 0, c * 4)
                take_proj("C", c, 0, 2, c * 4 + 1)
                take_proj("C", c, 1, 4, c * 4 + 2, bias_col["bk3"])

            def attend(a, causal, scale):
                def window(g, qp):
                    base = step_base(causal, g, qp)
                    for t, (_, _, c0, kn, _) in enumerate(steps_of(causal, qp if causal else 0)):
                        for pair in range(2):
                            act.wait_ge(sem(f"scores_{a}"), START + base * 2 + (2 * t + pair + 1))
                            if pair == 0:
                                act.wait_ge(sem(f"pv_{a}"), START + base + (t - 1))
                            act.activation(probs[2 * (t % 2) + pair][0:kn, :, c0:CH],
                                           ps[0:kn, 2 * pair:2 * pair + 2, c0:CH], ACT.Exp,
                                           scale=scale).then_inc(sem(f"exp_{a}"), 1)

                for g in range(NG):
                    if causal:
                        window(g, 0)
                        window(g, 1)
                    else:
                        with act.Fori(0, 2) as qp:
                            window(g, qp)

            attend(1, True, float(S) ** -0.5)
            with act.Fori(0, NC) as c:
                evac_T("B1", c, 0, c * 2)
                evac_T("B1", c, 1, c * 2 + 1)
                take_proj("B1", c, 0, 2, c * 2 + 2)
            attend(2, False, float(CTX) ** -0.5)
            def flat(t):
                return t[:, :, :].rearrange("p r e -> p (r e)")

            with act.Fori(0, NC // 2) as c:
                for k in range(2):
                    for u in range(2):
                        evac_T(f"B2_{u}", c, k, c * 4 + k, 2 * u, XT[u][:, :, :])
                    for u in range(2):
                        act.wait_ge(sem(f"mm_B2_{u}"), START + c * 4 + (k + 1))
                        act.activation(Z[u][:, :, :], chunk_banks(u), ACT.Relu).then_inc(sem(f"relu_{u}"), 1)
                for u in range(2):
                    evac_T(f"B2_{u}", c, 2, c * 4 + 2, 2 * u, XT[u][:, :, :])
                for u in range(2):
                    act.wait_ge(sem(f"mm_B2_{u}"), START + c * 4 + 3)
                    act.activation(SG[u], chunk_banks(u)[:, :, 0:HF], ACT.Silu).then_inc(sem(f"silu_{u}"), 1)
                for u in range(2):
                    act.wait_ge(sem(f"tr_B2_{u}"), START + c * 4 + 4)
                    act.activation(flat(Z2[u])[:, 0:CH], ps[:, 2 * u, :], ACT.Copy).then_inc(sem(f"xT_B2_{u}"), 1)
                for u in range(2):
                    act.wait_ge(sem(f"mm_B2_{u}"), START + c * 4 + 4)
                    apart(act)
                    act.activation(shr[:, ds(c * 8 + 4 * u, 4), :], chunk_banks(u), ACT.Copy)\
                       .then_inc(sem(f"shared_{u}"), 1)
            act.wait_ge(sem("mm_MOE"), START + 1)
            act.activation(xT[:, :, :], ps[:, 0:2, :], ACT.Copy).then_inc(sem("xT_MOE"), 1)
            act.wait_ge(sem("gate_in"), START + 1)
            act.activation(sc[:, :, 0:NE + 1], sc[:, :, 0:NE + 1], ACT.Sigmoid).then_inc(sem("gates_out"), 1)
            act.wait_ge(sem("tr_MOE"), START + 1)
            act.activation(ohT[:, :, :].rearrange("e r p -> e (r p)"), ps[0:NE, 4, :], ACT.Copy)\
               .then_inc(sem("onehot_t"), 1)
            act.wait_ge(sem("gate_diff"), START + 1)
            act.activation(small[:, 3, :], small[:, 2, :], ACT.Sigmoid).then_inc(sem("gates_out"), 1)
            act.activation(small[:, 4, :], small[:, 2, :], ACT.Sigmoid, scale=-1.0).then_inc(sem("gates_out"), 1)
            act.wait_ge(sem("mm_MOE"), START + 4)
            act.activation(bsel[:, 0:3, :], ps[:, 5:8, :], ACT.Copy).then_inc(sem("bias_moe"), 1)
            act.activation(bsel[:, 3, :], ps[:, 4, :], ACT.Copy).then_inc(sem("bias_moe"), 1)
            act.wait_ge(sem("picked"), START + 4)
            act.activation(SG[0], hs[:, :, 0:HF], ACT.Silu).then_inc(sem("silu_moe"), 1)
            act.wait_ge(sem("tr_MOE"), START + 2)
            act.activation(flat(z2)[:, 0:CH], ps[:, 0, :], ACT.Copy).then_inc(sem("xT_MOE"), 1)
            with act.Fori(0, NC) as c:
                evac_T("B2", c, 0, c)
                take_proj("B2", c, 0, 2, c + 1, bias_col["bq3"])
            attend(3, False, float(D) ** -0.5)
            with act.Fori(0, NC) as c:
                m = c * 8
                evac_T("B3", c, 0, m)
                evac_T("B3", c, 1, m + 1)
                for f in range(FF // P):
                    act.wait_ge(sem("mm_B3"), START + m + 2 + f)
                    if f >= 2:
                        act.wait_ge(sem("up_done"), START + c * 6 + (f - 1))
                    else:
                        act.wait_ge(sem("up_done"), START + c * 6)
                    act.activation(sgT[:, f % 2, :], ps[:, 2 + 2 * (f % 2), :], ACT.Silu).then_inc(sem("silu_3"), 1)

        @block.tensor
        def _(pe):
            for name in SIGNALS["tensor"]:
                pe.sem_inc(sem(name), START)
            pe.wait_ge(weights_in, START + W_ALL)
            pe.wait_ge(consts, START + N_CONST)

            def transposes(p, c, k, src, ready, value, bank=0):
                pe.wait_ge(ready, START + value)
                pe.wait_ge(sem(f"xT_{p}"), START + c * TR[p] + k)
                for cc in range(2):
                    for r in range(R):
                        last = pe.transpose(ps[:, bank + cc, r * P:(r + 1) * P], src[:, r, cc * P:(cc + 1) * P],
                                            identf[:, :])
                last.then_inc(sem(f"tr_{p}"), 1)

            def feature_major(p, w, bank, xt_at, n_out=2, free=None):
                pe.wait_ge(sem(f"xT_{p}"), START + xt_at)
                if free is not None:
                    pe.wait_ge(free[0], START + free[1])
                for oc in range(n_out):
                    for cc in range(2):
                        last = pe.matmul(ps[:, bank + oc, :], w[:, cc, oc * P:(oc + 1) * P], xT[:, cc, :],
                                         start=(cc == 0), stop=(cc == 1))
                last.then_inc(sem(f"mm_{p}"), 1)

            def token_major(p, w, bank, xt_at, free=None, xt=None, bias=None):
                xt = xT if xt is None else xt
                pe.wait_ge(sem(f"xT_{p}"), START + xt_at)
                if free is not None:
                    pe.wait_ge(free[0], START + free[1])
                for r in range(R):
                    dst = ps[:, bank + r // 2, (r % 2) * E:(r % 2) * E + E]
                    for cc in range(2):
                        last = pe.matmul(dst, xt[:, cc, r * P:(r + 1) * P], w[:, cc, :], start=(cc == 0),
                                         stop=(cc == 1 and bias is None))
                    if bias is not None:
                        last = pe.matmul(dst, ones[:, :], bias, start=False, stop=True)
                last.then_inc(sem(f"mm_{p}"), 1)

            with pe.Fori(0, NC) as c:
                transposes("A", c, 0, hb, sem("hb_A"), c + 1)
                feature_major("A", wt["wk1"], 2, c + 1, free=(proj_t, c * 2))
                feature_major("A", wt["wq1"], 4, c + 1, free=(proj_t, c * 2))
                token_major("A", wt["wv1"], 6, c + 1, free=(v_staged, c))
            with pe.Fori(0, NC) as c:
                transposes("C", c, 0, hb, sem("ctx_in"), c * 16 + 16)
                feature_major("C", wt["wk2"], 2, c + 1, free=(proj_t, c * 2 + 8))
                feature_major("C", wt["wk3"], 4, c + 1, free=(proj_t, c * 2 + 8))
                token_major("C", wt["wv2"], 6, c + 1, free=(v_staged, c * 2 + 4))
                token_major("C", wt["wv3"], 6, c + 1, free=(v_staged, c * 2 + 5))

            def attend(a, causal, before):
                scores, exps, pv = sem(f"scores_{a}"), sem(f"exp_{a}"), sem(f"pv_{a}")
                ring_full, ring_free = sem(f"ring_full_{a}"), sem(f"ring_free_{a}")
                for s, v in before:
                    pe.wait_ge(s, START + v)

                def enter(g, qp, k):
                    pe.wait_ge(ring_free, START + ring_base(causal, g, qp) + (k - RING + 1 if k else 0))
                    return FIRST + k % RING

                def row_tile(g, qp, b, tile):
                    j0, nj, q8, kb, n, masked = tile
                    sq, sk = stackQ[g % 2], stackK[g % 2]
                    for j in range(j0, j0 + nj):
                        at = (j - j0) * n
                        mm = pe.matmul(ps[:, b, at:at + n], sq[0:QROWS, j, ds(qp * QW + q8 * P, P)],
                                       sk[0:QROWS, j, kb * CH:kb * CH + n], start=True, stop=not masked)
                    if masked:
                        mm = pe.matmul(ps[:, b, n - P:n], identb[:, :], mask_qk[:, :], start=False, stop=True)
                    mm.then_inc(ring_full, 1)

                def turn_maxima(b, before):
                    pe.wait_ge(sem(f"mx_ready_{a}"), START + before + 1)
                    apart(pe)
                    pe.transpose(ps[0:4 * WT, b, 0:P], mx[:, :], identf[:, :]).then_inc(ring_full, 1)

                def maxima_alone(qp):
                    tiles = tiles_of(causal, qp if causal else 0)
                    for k, tile in enumerate(tiles):
                        row_tile(0, qp, enter(-1, qp, k), tile)
                    turn_maxima(enter(-1, qp, len(tiles)), qp)

                def window(g, qp):
                    half = g % 2
                    sq, sk = stackQ[half], stackK[half]
                    w0 = qp if causal else 0
                    steps, tiles = steps_of(causal, w0), tiles_of(causal, w0)
                    where = spread(causal, w0)
                    base = step_base(causal, g, qp)
                    pe.wait_ge(sem(f"max_in_{a}"), START + qp * 16 + (32 * g + 16))
                    pe.wait_ge(sem(f"v_in_{a}"), START + 16 * (g + 1))

                    def values(t):
                        h, kt, c0, kn, last_kt = steps[t]
                        pe.wait_ge(exps, START + base * 2 + (2 * t + 2))
                        if kt == 0:
                            pe.wait_ge(sem(f"acc_out_{a}"), START + qp * 2 + (4 * g + h))
                        for j in range(4):
                            mm = pe.matmul(ps[32 * j:32 * j + 32, ACC, c0:CH], vg[half][0:kn, kt, j, :],
                                           probs[2 * (t % 2) + j // 2][0:kn, j % 2, c0:CH],
                                           start=(kt == 0), stop=last_kt, tile_position=(0, 32 * j))
                        mm.then_inc(pv, 1)

                    def turn(h, b):
                        pe.wait_ge(sem(f"acc_out_{a}"), START + qp * 2 + (4 * g + h + 1))
                        for r in range(R):
                            mm = pe.transpose(ps[:, b, r * P:(r + 1) * P], accS[:, h, r * P:(r + 1) * P],
                                              identf[:, :])
                        mm.then_inc(ring_full, 1)

                    k = [0]
                    for t, (h, kt, c0, kn, _) in enumerate(steps):
                        diag = causal and kt >= R * (2 * w0 + h)
                        todo = where[t] if g + 1 < NG else ((), (), ())

                        def row_tiles(slot):
                            for idx in todo[slot]:
                                if idx == 0:
                                    pe.wait_ge(sem(f"stacks_in_{a}"), START + 192 * (g + 2))
                                b = enter(g, qp, k[0])
                                k[0] += 1
                                row_tile(g + 1, qp, b, tiles[idx])

                        for pair in range(2):
                            pe.wait_ge(exps, START + base * 2 + (2 * t + pair - 1))
                            for jj in range(2):
                                j = 2 * pair + jj
                                mm = pe.matmul(ps[0:kn, j, c0:CH], sk[0:QROWS + 3, j, kt * P:kt * P + kn],
                                               sq[0:QROWS + 3, j, ds(qp * QW + (h * CH + c0), CH - c0)],
                                               start=True, stop=not diag)
                                if diag:
                                    mm = pe.matmul(ps[:, j, c0:c0 + P], identb[:, :], mask_kq[:, :],
                                                   start=False, stop=True)
                            mm.then_inc(scores, 1)
                            row_tiles(pair)
                        if t >= 1:
                            values(t - 1)
                        if h == 1 and kt == 1:
                            turn(0, enter(g, qp, k[0]))
                            k[0] += 1
                        row_tiles(2)
                    values(len(steps) - 1)
                    turn(1, enter(g, qp, k[0]))
                    if g + 1 < NG:
                        turn_maxima(enter(g, qp, k[0] + 1), qp + 2 * (g + 1))

                pe.wait_ge(sem(f"stacks_in_{a}"), START + 192)
                if causal:
                    maxima_alone(0)
                    maxima_alone(1)
                else:
                    with pe.Fori(0, 2) as qp:
                        maxima_alone(qp)
                for g in range(NG):
                    if causal:
                        window(g, 0)
                        window(g, 1)
                    else:
                        with pe.Fori(0, 2) as qp:
                            window(g, qp)

            attend(1, True, ((proj_t, 16), (v_staged, 12)))

            def o_proj(p, w, c, per_tr, per_mm):
                transposes(p, c, 0, hb, sem(f"o_taken_{p}"), c + 1)
                token_major(p, w, 6, c * per_tr + 1, free=(sem(f"sixseven_{p}"), c * SIX[p]))

            SIX = {"B1": 1, "B3": 2}
            pe.wait_ge(sem("normed_1"), START + 1)
            with pe.Fori(0, NC) as c:
                o_proj("B1", wt["wo1"], c, 2, 2)
                transposes("B1", c, 1, hb, sem("hb_B1"), c + 1)
                feature_major("B1", wt["wq2"], 2, c * 2 + 2, free=(proj_t, c + 16))
            attend(2, False, ((proj_t, 20), (sem("sixseven_B1"), 4)))
            pe.wait_ge(sem("normed_2"), START + 1)
            pe.wait_ge(sem("bias_in"), START + 64)
            with pe.Fori(0, NC // 2) as c:
                for u in range(2):
                    transposes(f"B2_{u}", c, 0, HB[u], sem(f"o_taken_B2_{u}"), c + 1, 2 * u)
                for u in range(2):
                    token_major(f"B2_{u}", wt["wo2"], 4 + 2 * u, c * 4 + 1, (sem(f"shared_{u}"), c), XT[u], bias_row["bo2"])
                for u in range(2):
                    transposes(f"B2_{u}", c, 1, HB[u], sem(f"hb_B2_{u}"), c * 2 + 1, 2 * u)
                for u in range(2):
                    token_major(f"B2_{u}", wt["wf"], 4 + 2 * u, c * 4 + 2, (sem(f"relu_{u}"), c * 2 + 1), XT[u],
                                bias_row["bf"])
                for u in range(2):
                    transposes(f"B2_{u}", c, 2, HB[u], sem(f"hb_B2_{u}"), c * 2 + 2, 2 * u)
                for u in range(2):
                    token_major(f"B2_{u}", wt["sw12"], 4 + 2 * u, c * 4 + 3, (sem(f"relu_{u}"), c * 2 + 2), XT[u],
                                bias_row["sb12"])
                for u in range(2):
                    pe.wait_ge(sem(f"hidden_{u}"), START + c + 1)
                    for r in range(R):
                        mm = pe.transpose(ps[:, 2 * u, r * P:(r + 1) * P], Z[u][:, r, 0:HF], identf[:, :])
                    mm.then_inc(sem(f"tr_B2_{u}"), 1)
                for u in range(2):
                    pe.wait_ge(sem(f"xT_B2_{u}"), START + c * 4 + 4)
                    for r in range(R):
                        dst = ps[:, 4 + 2 * u + r // 2, (r % 2) * E:(r % 2) * E + E]
                        pe.matmul(dst, Z2[u][:, :, :].rearrange("p r e -> p (r e)")[:, r * P:(r + 1) * P], sw3[:, :],
                                  start=True, stop=False)
                        mm = pe.matmul(dst, ones[:, :], bias_row["sb3"], start=False, stop=True)
                    mm.then_inc(sem(f"mm_B2_{u}"), 1)
            pe.wait_ge(sem("kept"), START + NC)
            pe.wait_ge(sem("gather_map"), START + 1)
            for half in range(2):
                for t in range(S // P):
                    mm = pe.matmul(ps[:, half, :], o_sb[:, t, half * P:(half + 1) * P], which[:, t, :],
                                   start=(t == 0), stop=(t == S // P - 1))
            mm.then_inc(sem("mm_MOE"), 1)
            pe.wait_ge(sem("xT_MOE"), START + 1)
            for u in range(2):
                pe.wait_ge(sem(f"shared_{u}"), START + NC // 2)
            for r in range(R):
                for cc in range(2):
                    mm = pe.matmul(ps[:, 4, r * 16:r * 16 + NE + 1], xT[:, cc, r * P:(r + 1) * P],
                                   gate_w[:, cc, 0:NE + 1], start=(cc == 0), stop=(cc == 1))
            mm.then_inc(sem("mm_MOE"), 1)
            pe.wait_ge(sem("ew_in"), START + 48)

            def experts_up(r):
                for n in range(4):
                    for cc in range(2):
                        mm = pe.matmul(ps[:, 4 * (r % 2) + n, :], xT[:, cc, r * P:(r + 1) * P],
                                       ew12[:, cc, n * 512:(n + 1) * 512], start=(cc == 0), stop=(cc == 1))
                mm.then_inc(sem("mm_MOE"), 1)

            experts_up(0)
            pe.wait_ge(sem("onehot"), START + 1)
            for r in range(R):
                mm = pe.transpose(ps[0:NE, 4, r * P:(r + 1) * P], oh[:, r, :], identf[:, :])
            mm.then_inc(sem("tr_MOE"), 1)
            pe.wait_ge(sem("onehot_t"), START + 1)
            for r in range(R):
                mm = pe.matmul(ps[:, 5 + r if r < 3 else 4, :], ohT[:, r, :], eb[0:NE, :], start=True, stop=True)
            mm.then_inc(sem("mm_MOE"), 1)
            pe.wait_ge(sem("bias_moe"), START + 2)
            experts_up(1)
            pe.wait_ge(sem("picked"), START + 1)
            experts_up(2)
            pe.wait_ge(sem("picked"), START + 2)
            experts_up(3)
            pe.wait_ge(sem("hidden_moe"), START + 1)
            for r in range(R):
                mm = pe.transpose(ps[:, 0, r * P:(r + 1) * P], z[:, r, 0:HF], identf[:, :])
            mm.then_inc(sem("tr_MOE"), 1)
            pe.wait_ge(sem("xT_MOE"), START + 2)
            for r in range(R):
                if r >= 2:
                    pe.wait_ge(sem("expert_out"), START + r - 1)
                for n in range(4):
                    mm = pe.matmul(ps[:, 4 * (r % 2) + n, :],
                                   z2[:, :, :].rearrange("p r e -> p (r e)")[:, r * P:(r + 1) * P],
                                   ew3[:, n * 512:(n + 1) * 512], start=True, stop=True)
                mm.then_inc(sem("mm_MOE"), 1)
            pe.wait_ge(sem("entries"), START + 1)
            pe.wait_ge(sem("scatter_map"), START + 1)
            for c in range(NC):
                if c >= 2:
                    pe.wait_ge(sem("merged"), START + c - 1)
                for r in range(R):
                    for m in range(R):
                        mm = pe.matmul(ps[:, 4 * (c % 2) + r, 0:E + 1], where_to[:, m, (R * c + r) * P:(R * c + r + 1) * P],
                                       vals[:, m, 0:E + 1], start=(m == 0), stop=(m == R - 1))
                mm.then_inc(sem("scattered"), 1)
            pe.wait_ge(sem("merged"), START + NC)
            with pe.Fori(0, NC) as c:
                transposes("B2", c, 0, hb, sem("hb_B2"), c + 1)
                feature_major("B2", wt["wq3"], 2, c + 1, free=(proj_t, c + 20))
            attend(3, False, ((proj_t, 24), (sem("ones_again"), 2)))
            pe.wait_ge(sem("normed_3"), START + 1)
            with pe.Fori(0, NC) as c:
                o_proj("B3", wt["wo3"], c, 2, 8)
                transposes("B3", c, 1, hb, sem("hb_B3"), c + 1)
                pe.wait_ge(sem("xT_B3"), START + c * 2 + 2)
                pe.wait_ge(sem("fw_ready"), START + 3)
                for f in range(FF // P):
                    b = 2 + 2 * (f % 2)
                    pe.wait_ge(sem("up_done"), START + c * 6 + max(0, f - 1))
                    for u in range(2):
                        for cc in range(2):
                            mm = pe.matmul(ps[:, b + u, :], wgu[:, u, cc, f * P:(f + 1) * P], xT[:, cc, :],
                                           start=(cc == 0), stop=(cc == 1))
                    mm.then_inc(sem("mm_B3"), 1)
                pe.wait_ge(sem("up_done"), START + c * 6 + 6)
                pe.wait_ge(sem("sixseven_B3"), START + c * 2 + 1)
                for r in range(R):
                    for f in range(FF // P):
                        mm = pe.matmul(ps[:, 6 + r // 2, (r % 2) * E:(r % 2) * E + E], hT[:, f, r * P:(r + 1) * P],
                                       wd[:, f, :], start=(f == 0), stop=(f == FF // P - 1))
                mm.then_inc(sem("mm_B3"), 1)

        @block.vector
        def _(dve):
            for name in SIGNALS["vector"]:
                dve.sem_inc(sem(name), START)
            ch = Chain(dve, sem("vector_chain"))
            link, note, join = ch.link, ch.note, ch.join

            def ln_stats(src, eps, u=0):
                apart(dve)
                for r in range(R):
                    note(dve.bn_stats(st[u][:, r, :], src[:, r, :]))
                join()
                apart(dve)
                for r in range(R):
                    note(dve.bn_aggr(mv[u][:, r, :], st[u][:, r, :]))
                join()
                dve.tensor_scalar(ve[u][:, :], mv[u][:, :, 1], eps, None, ALU.add).then_inc(ln_var, 1)

            def ln_apply(n, src, dst, g=None, b=None, signal=None, u=0):
                w = src.shape[-1]
                dve.wait_ge(ln_rstd, START + n + 1)
                for r in range(R):
                    ins = dve.tensor_scalar(dst[:, r, :], src[:, r, :], mv[u][:, r, 0:1], rs[u][:, r:r + 1],
                                            ALU.subtract, ALU.mult)
                    if g is None and r == R - 1 and signal is not None:
                        ins.then_inc(signal, 1)
                    else:
                        note(ins)
                if g is not None:
                    join()
                    link(dve.tensor_tensor(dst, dst, wide(g, w), ALU.mult))
                    ins = dve.tensor_tensor(dst, dst, wide(b, w), ALU.add)
                    if signal is not None:
                        ins.then_inc(signal, 1)
                    else:
                        link(ins)
                elif signal is None:
                    join()

            def layernorm(p, c, k, src, dst, eps, g=None, b=None, signal=None):
                ln_stats(src, eps)
                ln_apply(ln_n(p, c, k), src, dst, g, b, signal)

            def wide(row, w):
                return row[:, 0:w].unsqueeze(1).to_broadcast([P, R, w])

            def chunk6():
                return ps[:, 6:8, :].rearrange("p b (r e) -> p (b r) e", e=E)

            def split(p, c, k):
                n = split_n(p, c, k)
                dve.wait_ge(proj_t, START + n + 1)
                dve.wait_ge(parts_out, START + n * 48)
                dve.tensor_copy(parts[0], pt).then_inc(part_hi, 1)
                dve.wait_ge(part_hi, START + n + 1)
                dve.wait_ge(part_lo, START + n)
                dve.tensor_tensor(pr, pt, parts[0], ALU.subtract).then_inc(part_rest, 1)

            def stage_v(p, c, k, mm_at, bias=None):
                dve.wait_ge(sem(f"mm_{p}"), START + mm_at)
                dve.wait_ge(v_out, START + v_n(p, c, k) * 16)
                src = chunk6().rearrange("p r (h d) -> p r h d", d=D)
                if bias is None:
                    dve.tensor_copy(vst[:, :, :, 0:D], src).then_inc(v_staged, 1)
                else:
                    link(dve.tensor_tensor(z[:, :, :], chunk6(), wide(bias, E), ALU.add))
                    dve.tensor_copy(vst[:, :, :, 0:D], z[:, :, :].rearrange("p r (h d) -> p r h d", d=D))\
                       .then_inc(v_staged, 1)

            for w in range(2):
                link(dve.memset(mxb[w][:, :, :], MASKED))
            for half in range(2):
                link(dve.memset(stackK[half][QROWS:QROWS + 3, :, :], 1.0))
            dve.wait_ge(consts, START + N_CONST)
            dve.wait_ge(sem("index_in"), START + 48)
            idx_b, tmp = region(16384, (M + R,)), region(17408, (M + R,))
            link(dve.tensor_copy(code[:, :], idx_i[:, 1, :]))
            link(dve.tensor_scalar(tmp, code[:, :], 0.0, float(S), ALU.is_lt, ALU.mult))
            link(dve.tensor_tensor(code[:, :], code[:, :], tmp, ALU.add))
            link(dve.tensor_copy(idx_b, idx_i[:, 0, :]))
            link(dve.tensor_scalar(tmp, idx_b, 0.0, None, ALU.is_equal))
            link(dve.tensor_scalar(idx_b, idx_b, -1.0, None, ALU.is_equal))
            link(dve.tensor_tensor(tmp, tmp, idx_b, ALU.add))
            link(dve.scalar_tensor_tensor(out=code[:, :], in0=code[:, :], scalar=1.0, in1=tmp,
                                          op0=ALU.add, op1=ALU.mult))
            for r in range(R):
                link(dve.tensor_scalar(mtmp, code[:, 0:M], code[:, M + r:M + r + 1], None, ALU.is_equal))
                link(dve.tensor_tensor(mtmp, mtmp, row_id, ALU.mult))
                link(dve.tensor_reduce(first_code[:, r:r + 1], mtmp, AX.X, ALU.min))
            link(dve.tensor_tensor(first_code[:, :], first_code[:, :], entry_id[:, :], ALU.is_equal))
            link(dve.tensor_tensor(first_code[:, :], first_code[:, :], code[:, M:M + R], ALU.mult))
            dve.wait_ge(x_in, START + 64)
            with dve.Fori(0, NC) as c:
                ch.loop(c, 13)
                dve.wait_ge(sem("tr_A"), START + c)
                layernorm("A", c, 0, x_sb[:, ds(c * 4, 4), :], hb[:, :, :], 1e-5, signal=sem("hb_A"))
                note(dve.tensor_copy(xmean[:, ds(c * 4, 4)], mv[0][:, :, 0]))
                note(dve.tensor_copy(xrstd[:, ds(c * 4, 4)], rs[0][:, :]))
                split("A", c, 0)
                split("A", c, 1)
                stage_v("A", c, 0, c * 3 + 3)
            ch.end(NC)
            with dve.Fori(0, NC) as c:
                ch.loop(c, 1)
                split("C", c, 0)
                split("C", c, 1)
                stage_v("C", c, 0, c * 4 + 3)
                stage_v("C", c, 1, c * 4 + 4, rows["bv3"])
            ch.end(NC)

            def attend(a, causal):
                ring_full, ring_free = sem(f"ring_full_{a}"), sem(f"ring_free_{a}")

                def entry(g, qp, k):
                    dve.wait_ge(ring_full, START + ring_base(causal, g, qp) + (k + 1))
                    return FIRST + k % RING

                def row_max(qp, b, tile):
                    j0, nj, q8, kb, n, _ = tile
                    dst = mxb[qp if causal else 0][:, :, kb].rearrange("p (j q) -> p j q", j=4)[:, j0:j0 + nj, q8]
                    dve.tensor_reduce(dst, ps[:, b, 0:nj * n].rearrange("p (j n) -> p j n", j=nj),
                                      AX.X, ALU.max).then_inc(ring_free, 1)

                def last_max(qp, uses):
                    dve.wait_ge(ring_free, START + uses)
                    dve.tensor_reduce(mx[:, :], mxb[qp if causal else 0][:, :, :], AX.X, ALU.max)\
                       .then_inc(sem(f"mx_ready_{a}"), 1)

                def split_maxima(before, b, uses):
                    dve.wait_ge(sem(f"max_out_{a}"), START + before * 48)
                    dve.wait_ge(sem(f"max_split_{a}"), START + before)
                    dve.tensor_scalar(mneg[:, :], ps[0:4 * WT, b, 0:P], -1.0, None, ALU.mult).then_inc(ring_free, 1)
                    dve.wait_ge(ring_free, START + uses)
                    link(dve.tensor_copy(mparts[:, 0, :], mneg[:, :]))
                    link(dve.tensor_tensor(mres[:, :], mneg[:, :], mparts[:, 0, :], ALU.subtract))
                    link(dve.tensor_copy(mparts[:, 1, :], mres[:, :]))
                    dve.tensor_tensor(mparts[:, 2, :], mres[:, :], mparts[:, 1, :], ALU.subtract)\
                       .then_inc(sem(f"max_split_{a}"), 1)

                def window(g, qp):
                    w0 = qp if causal else 0
                    steps, tiles = steps_of(causal, w0), tiles_of(causal, w0)
                    where = spread(causal, w0)
                    base = step_base(causal, g, qp)
                    end0 = sum(1 for s in steps if s[0] == 0)

                    def take_acc(h):
                        dve.wait_ge(sem(f"pv_{a}"), START + base + (end0 if h == 0 else len(steps)))
                        dve.tensor_copy(accS[:, h, :], ps[:, ACC, :]).then_inc(sem(f"acc_out_{a}"), 1)

                    def norm_acc(h, b):
                        acc = ps[:, b, :].rearrange("p (r j d) -> p r j d", r=R, d=32)
                        rec4 = rec[:, :].rearrange("p (r j) -> p r j", r=R)
                        link(dve.reciprocal(rec4, acc[:, :, :, D]))
                        dve.tensor_tensor(
                            o_sb[:, ds(qp * WT + 4 * h, 4), g * 64:g * 64 + 64].rearrange("p r (j d) -> p r j d", d=D),
                            acc[:, :, :, 0:D], rec4.unsqueeze(3).to_broadcast([P, R, 4, D]),
                            ALU.mult).then_inc(ring_free, 1)

                    k = 0
                    for t, (h, kt, c0, kn, _) in enumerate(steps):
                        todo = where[t] if g + 1 < NG else ((), (), ())
                        for idx in (*todo[0], *todo[1]):
                            row_max(qp, entry(g, qp, k), tiles[idx])
                            k += 1
                        if h == 1 and kt == 0:
                            take_acc(0)
                        if h == 1 and kt == 1:
                            norm_acc(0, entry(g, qp, k))
                            k += 1
                        for idx in todo[2]:
                            row_max(qp, entry(g, qp, k), tiles[idx])
                            k += 1
                    take_acc(1)
                    if g + 1 < NG:
                        last_max(qp, ring_base(causal, g, qp) + k)
                    norm_acc(1, entry(g, qp, k))
                    if g + 1 < NG:
                        split_maxima(qp + 2 * (g + 1), entry(g, qp, k + 1), ring_base(causal, g, qp) + (k + 2))

                def maxima_alone(qp):
                    tiles = tiles_of(causal, qp if causal else 0)
                    for k, tile in enumerate(tiles):
                        row_max(qp, entry(-1, qp, k), tile)
                    last_max(qp, ring_base(causal, -1, qp) + len(tiles))
                    split_maxima(qp, entry(-1, qp, len(tiles)), ring_base(causal, -1, qp) + (len(tiles) + 1))

                if causal:
                    maxima_alone(0)
                    maxima_alone(1)
                else:
                    with dve.Fori(0, 2) as qp:
                        ch.loop(qp, 3)
                        maxima_alone(qp)
                    ch.end(2)
                for g in range(NG):
                    if causal:
                        window(g, 0)
                        window(g, 1)
                    else:
                        with dve.Fori(0, 2) as qp:
                            ch.loop(qp, 5 if g + 1 < NG else 2)
                            window(g, qp)
                        ch.end(2)
                dve.wait_ge(ring_free, START + ring_base(causal, NG - 1, 1) + 2)
                dve.memset(rec[:, 0:1], 0.0).then_inc(sem(f"normed_{a}"), 1)

            attend(1, True)
            dve.wait_ge(weights_in, START + W_ALL)
            dve.wait_ge(sem("tanh_done"), START + 1)
            with dve.Fori(0, NC) as c:
                ch.loop(c, 18)
                dve.wait_ge(sem("mm_B1"), START + c * 2 + 1)
                dve.tensor_tensor(z[:, :, :], chunk6(), wide(rows["bo1"], E), ALU.add).then_inc(sem("sixseven_B1"), 1)
                dve.wait_ge(sem("sixseven_B1"), START + c + 1)
                dve.wait_ge(sem("tr_B1"), START + c * 2 + 1)
                for r in range(R):
                    note(dve.tensor_scalar(hb[:, r, :], x_sb[:, ds(c * 4 + r, 1), :].rearrange("p o e -> p (o e)"),
                                           xmean[:, ds(c * 4 + r, 1)], xrstd[:, ds(c * 4 + r, 1)],
                                           ALU.subtract, ALU.mult))
                join()
                link(dve.scalar_tensor_tensor(out=z2[:, :, :], in0=z[:, :, :], scalar=0.0, in1=hb[:, :, :],
                                              op0=ALU.max, op1=ALU.add))
                layernorm("B1", c, 0, z2[:, :, :], hb[:, :, :], 1e-6, rows["g1"], rows["b1"], signal=sem("hb_B1"))
                split("B1", c, 0)
            ch.end(NC)
            attend(2, False)

            dve.wait_ge(sem("normed_2"), START + 1)
            for t in range(S // P):
                ins = dve.tensor_scalar(which[:, t, :], code[:, 0:M], tok_id[:, t:t + 1], None, ALU.is_equal)
                if t < S // P - 1:
                    note(ins)
            ins.then_inc(sem("gather_map"), 1)

            with dve.Fori(0, NC // 2) as c:
                ch.loop(c, 108)
                lanes = [(u, Z[u][:, :, :], Z2[u][:, :, :], HB[u][:, :, :], x_sb[:, ds(c * 8 + 4 * u, 4), :],
                          Z[u][:, :, 0:HF]) for u in range(2)]
                n = c * 8 + LNS["B2x"][0]
                for u, za, zb, h, xc, hid in lanes:
                    dve.wait_ge(sem(f"relu_{u}"), START + c * 2 + 1)
                    ln_stats(za, 0.25e-6, u)
                for u, za, zb, h, xc, hid in lanes:
                    dve.wait_ge(sem(f"tr_B2_{u}"), START + c * 4 + 1)
                    ln_apply(n + u, za, h, rows["g2"], rows["b2"], sem(f"hb_B2_{u}"), u)
                for u, za, zb, h, xc, hid in lanes:
                    dve.wait_ge(sem(f"relu_{u}"), START + c * 2 + 2)
                    link(dve.tensor_tensor(zb, za, h, ALU.add))
                    ln_stats(zb, 1e-6, u)
                for u, za, zb, h, xc, hid in lanes:
                    ln_apply(n + (2 + u), zb, zb, rows["g3"], rows["b3"], None, u)
                    link(dve.scalar_tensor_tensor(out=xc, in0=zb, scalar=tg[:, 0:1], in1=xc, op0=ALU.mult, op1=ALU.add))
                    ln_stats(xc, 1e-5, u)
                for u, za, zb, h, xc, hid in lanes:
                    dve.wait_ge(sem(f"tr_B2_{u}"), START + c * 4 + 2)
                    ln_apply(n + (4 + u), xc, h, None, None, sem(f"hb_B2_{u}"), u)
                for u, za, zb, h, xc, hid in lanes:
                    dve.wait_ge(sem(f"silu_{u}"), START + c + 1)
                    link(dve.tensor_tensor(hid, SG[u], chunk_banks(u)[:, :, HF:E], ALU.mult))
                    ln_stats(hid, 1e-5, u)
                for u, za, zb, h, xc, hid in lanes:
                    ln_apply(n + (6 + u), hid, hid, rows["slg"], rows["slb"], sem(f"hidden_{u}"), u)
            ch.end(NC // 2)
            hid = z[:, :, 0:HF]
            dve.wait_ge(sem("mm_MOE"), START + 2)
            logits = ps[:, 4, 0:R * 16].rearrange("p (r n) -> p r n", r=R)[:, :, 0:NE + 1]
            dve.tensor_tensor(sc[:, :, 0:NE + 1], logits, wide(rows["gateb"], NE + 1), ALU.add)\
               .then_inc(sem("gate_in"), 1)
            dve.wait_ge(sem("gates_out"), START + 1)
            io = iota8[:, :].unsqueeze(1).to_broadcast([P, R, NE])
            link(dve.tensor_tensor(sel[:, :, :], sc[:, :, 0:NE], wide(rows["expb"], NE), ALU.add))
            link(dve.tensor_reduce(small[:, 0, :], sel[:, :, :], AX.X, ALU.max))
            link(dve.tensor_tensor(oh[:, :, :], sel[:, :, :],
                                   small[:, 0, :].unsqueeze(2).to_broadcast([P, R, NE]), ALU.is_ge))
            link(dve.tensor_tensor(sel[:, :, :], oh[:, :, :], io, ALU.mult))
            link(dve.tensor_reduce(small[:, 1, :], sel[:, :, :], AX.X, ALU.min))
            dve.tensor_tensor(oh[:, :, :], io, small[:, 1, :].unsqueeze(2).to_broadcast([P, R, NE]),
                              ALU.is_equal).then_inc(sem("onehot"), 1)
            dve.wait_ge(sem("onehot"), START + 1)
            link(dve.tensor_tensor(sel[:, :, :], oh[:, :, :], sc[:, :, 0:NE], ALU.mult))
            link(dve.tensor_reduce(small[:, 5, :], sel[:, :, :], AX.X, ALU.add))
            dve.tensor_tensor(small[:, 2, :], sc[:, :, NE], small[:, 5, :], ALU.subtract)\
               .then_inc(sem("gate_diff"), 1)
            dve.wait_ge(sem("token_row"), START + 1)
            for m in range(R):
                ins = dve.tensor_scalar(where_to[:, m, :], where_to[:, m, :], first_code[:, m:m + 1], None, ALU.is_equal)
                if m < R - 1:
                    note(ins)
            ins.then_inc(sem("scatter_map"), 1)
            dve.wait_ge(sem("gates_out"), START + 3)
            link(dve.tensor_scalar(vals[:, :, E], small[:, 3, :], -1.0, None, ALU.add))
            dve.wait_ge(sem("bias_moe"), START + 2)
            for r in range(R):
                dve.wait_ge(sem("mm_MOE"), START + (3, 5, 6, 7)[r])
                up = ps[:, 4 * (r % 2):4 * (r % 2) + 4, :].rearrange("p (u b) (e h) -> p u (b e) h", u=2, h=HF)
                acc = hs[:, r, :].rearrange("p (u h) -> p u h", u=2)
                for e in range(NE):
                    start = bsel[:, r, 0:2 * HF].rearrange("p (u h) -> p u h", u=2)
                    ins = dve.scalar_tensor_tensor(out=acc, in0=up[:, :, e, :], scalar=oh[:, r, e:e + 1],
                                                   in1=acc if e else start, op0=ALU.mult, op1=ALU.add)
                    if e < NE - 1:
                        link(ins)
                ins.then_inc(sem("picked"), 1)
            dve.wait_ge(sem("silu_moe"), START + 1)
            link(dve.tensor_tensor(hid, SG[0], hs[:, :, HF:2 * HF], ALU.mult))
            layernorm("MOE", 0, 0, hid, hid, 1e-5, rows["elg"], rows["elb"], signal=sem("hidden_moe"))
            for r in range(R):
                dve.wait_ge(sem("mm_MOE"), START + 8 + r)
                down = ps[:, 4 * (r % 2):4 * (r % 2) + 4, :].rearrange("p b (e n) -> p (b e) n", n=E)
                for e in range(NE):
                    ins = dve.scalar_tensor_tensor(out=vals[:, r, 0:E], in0=down[:, e, :], scalar=oh[:, r, e:e + 1],
                                                   in1=vals[:, r, 0:E] if e else bsel[:, r, 2 * HF:2 * HF + E],
                                                   op0=ALU.mult, op1=ALU.add)
                    if e < NE - 1:
                        link(ins)
                ins.then_inc(sem("expert_out"), 1)
            dve.wait_ge(sem("expert_out"), START + R)
            for r in range(R):
                ins = dve.tensor_scalar(vals[:, r, 0:E], vals[:, r, 0:E], small[:, 4, r:r + 1], None, ALU.mult)
                if r < R - 1:
                    note(ins)
            ins.then_inc(sem("entries"), 1)
            for c in range(NC):
                xc = x_sb[:, 4 * c:4 * c + 4, :]
                b = 4 * (c % 2)
                dve.wait_ge(sem("scattered"), START + c + 1)
                link(dve.tensor_scalar(small[:, 6, :], ps[:, b:b + 4, E], 1.0, None, ALU.add))
                for r in range(R):
                    ins = dve.scalar_tensor_tensor(out=z[:, r, :], in0=shr[:, R * c + r, :], scalar=small[:, 6, r:r + 1],
                                                   in1=ps[:, b + r, 0:E], op0=ALU.mult, op1=ALU.add)
                    if r < R - 1:
                        note(ins)
                ins.then_inc(sem("merged"), 1)
                dve.wait_ge(sem("merged"), START + c + 1)
                link(dve.scalar_tensor_tensor(out=xc, in0=z[:, :, :], scalar=tg[:, 2:3], in1=xc,
                                              op0=ALU.mult, op1=ALU.add))
            with dve.Fori(0, NC) as c:
                ch.loop(c, 11)
                dve.wait_ge(sem("tr_B2"), START + c)
                layernorm("B2", c, 0, x_sb[:, ds(c * 4, 4), :], hb[:, :, :], 1e-5, signal=sem("hb_B2"))
                split("B2", c, 0)
            ch.end(NC)
            attend(3, False)
            dve.wait_ge(sem("fw_in"), START + 48)
            for u in range(2):
                dve.tensor_scalar(wgu[:, u, :, :], wint[:, u, :, :], 1.0 / 127.0, None, ALU.mult)\
                   .then_inc(sem("fw_ready"), 1)
            dve.tensor_scalar(wd, dint, 1.0 / 127.0, None, ALU.mult).then_inc(sem("fw_ready"), 1)
            six3 = sem("sixseven_B3")
            with dve.Fori(0, NC) as c:
                ch.loop(c, 12)
                m = c * 8
                xc = x_sb[:, ds(c * 4, 4), :]
                dve.wait_ge(sem("mm_B3"), START + m + 1)
                dve.tensor_tensor(z[:, :, :], chunk6(), wide(rows["bo3"], E), ALU.add).then_inc(six3, 1)
                dve.wait_ge(six3, START + c * 2 + 1)
                link(dve.scalar_tensor_tensor(out=xc, in0=z[:, :, :], scalar=tg[:, 1:2], in1=xc,
                                              op0=ALU.mult, op1=ALU.add))
                dve.wait_ge(sem("tr_B3"), START + c * 2 + 1)
                layernorm("B3", c, 0, xc, hb[:, :, :], 1e-5, signal=sem("hb_B3"))
                for f in range(FF // P):
                    dve.wait_ge(sem("mm_B3"), START + m + (2 + f))
                    dve.wait_ge(sem("silu_3"), START + c * 6 + (f + 1))
                    dve.tensor_tensor(hT[:, f, :], sgT[:, f % 2, :], ps[:, 3 + 2 * (f % 2), :], ALU.mult)\
                       .then_inc(sem("up_done"), 1)
                dve.wait_ge(sem("mm_B3"), START + m + 8)
                dve.scalar_tensor_tensor(out=xc, in0=chunk6(), scalar=tg[:, 3:4], in1=xc, op0=ALU.mult, op1=ALU.add)\
                   .then_inc(six3, 1)
            ch.end(NC)


_NAMES = {
    "wk1": "L0_xattn_Wk1", "wv1": "L0_xattn_Wv1", "wq1": "L0_xattn_Wq1", "wk2": "L0_xattn_Wk2",
    "wv2": "L0_xattn_Wv2", "wq2": "L0_xattn_Wq2", "wo1": "L0_xattn_Wo1", "wo2": "L0_xattn_Wo2",
    "wf": "L0_xattn_Wf", "bo1": "L0_xattn_bo1", "bo2": "L0_xattn_bo2", "bf": "L0_xattn_bf",
    "g1": "L0_xattn_g1", "b1": "L0_xattn_b1", "g2": "L0_xattn_g2", "b2": "L0_xattn_b2", "g3": "L0_xattn_g3",
    "b3": "L0_xattn_b3", "sb3": "L0_ffn_sb3", "slg": "L0_ffn_s_ln_g", "slb": "L0_ffn_s_ln_b",
    "elg": "L0_ffn_sel_ln_g", "elb": "L0_ffn_sel_ln_b", "expb": "L0_ffn_exp_bias",
    "index_b": "L0_ffn_index_b", "index_t": "L0_ffn_index_t",
    "wq3": "L1_xattn_Wq", "bq3": "L1_xattn_bq", "wk3": "L1_xattn_Wk", "bk3": "L1_xattn_bk",
    "wv3": "L1_xattn_Wv", "bv3": "L1_xattn_bv", "wo3": "L1_xattn_Wo", "bo3": "L1_xattn_bo",
    "x": "x", "ctx": "ctx_1024",
}


def lay_out(inputs):
    import numpy as np
    a = {k: np.asarray(inputs[v]) for k, v in _NAMES.items()}
    for n in ("wk1", "wv1", "wq1", "wk2", "wv2", "wq2"):
        a[n] = a[n].transpose(1, 0, 2).reshape(E, E)
    for n in ("bq3", "bk3"):
        a[n] = a[n].reshape(2, P).T
    f = {k: np.asarray(inputs["L0_ffn_" + k]) for k in
         ("sw1", "sw2", "sw3", "sb1", "sb2", "sg_w", "sg_b", "eg_w", "eg_b", "ew1", "ew2", "ew3", "eb1", "eb2", "eb3")}
    a["sw12"] = np.concatenate([f["sw1"].T, f["sw2"].T], axis=1)
    a["sb12"] = np.concatenate([f["sb1"], f["sb2"]])
    a["sw3"] = f["sw3"].T
    a["gate_w"] = np.concatenate([f["eg_w"].T, f["sg_w"].T], axis=1)
    a["gateb"] = np.concatenate([f["eg_b"], f["sg_b"]])
    a["ew12"] = np.concatenate([f["ew1"].reshape(NE * HF, E).T, f["ew2"].reshape(NE * HF, E).T], axis=1)
    a["ew3"] = f["ew3"].transpose(2, 0, 1).reshape(HF, NE * E)
    a["eb"] = np.concatenate([f["eb1"], f["eb2"], f["eb3"]], axis=1)
    a["index_col"] = np.stack([a["index_b"], a["index_t"]]).reshape(2, R, P).transpose(2, 0, 1)
    a["gates"] = np.concatenate([np.asarray(inputs["g_xattn"]), np.asarray(inputs["g_ffn"])])
    a["w_gate"] = np.asarray(inputs["L1_ffn_w_gate"]).T
    a["w_up"] = np.asarray(inputs["L1_ffn_w_up"]).T
    a["w_down"] = np.asarray(inputs["L1_ffn_w_down"]).T
    return {k: np.ascontiguousarray(v) for k, v in a.items()}


def kernel(**inputs):
    import concourse.bacc as _bacc
    from concourse import mybir as _mybir
    from concourse.bass_utils import run_bass_kernel_spmd as _run

    nc = _bacc.Bacc("TRN2", target_bir_lowering=False, num_devices=1)
    arrays, A = {}, {}
    for name, a in lay_out(inputs).items():
        arrays[f"in_{name}"] = a
        A[name] = nc.dram_tensor(f"in_{name}", a.shape, _mybir.dt.from_np(a.dtype), kind="ExternalInput").ap()
    out = nc.dram_tensor("out_0", (1, S, E), _mybir.dt.float32, kind="ExternalOutput").ap()
    build(nc, A, out)
    r = _run(nc, [arrays], core_ids=[0])
    return r.results[0]["out_0"]
```

```python
from contextlib import ExitStack

import concourse.bass as bass
from concourse import mybir

F32 = mybir.dt.float32
BF16 = mybir.dt.bfloat16
I32 = mybir.dt.int32
ALU = mybir.AluOpType
ACT = mybir.ActivationFunctionType
AX = mybir.AxisListType
ds = bass.ds

P = 128
S = 2048
E = 256
H = 16
D = E // H
CTX = 1601
CH = 512
NC = S // CH
R = CH // P
NG = H // 4
HF = 128
NE = 8
M = 512
FF = 768
QROWS = 6 * D
MASKED = -3.0e38
START = 2

Q_PARTS = (0, 0, 1, 1, 0, 2)
K_PARTS = (0, 1, 0, 1, 2, 0)


PASSES = ("A", "C", "B1_0", "B1_1", "B2_0", "B2_1", "MOE", "Q3_0", "Q3_1", "O3_0", "O3_1", "B3")
SIGNALS = {
    "tensor": [f"{n}_{p}" for n in ("tr", "mm") for p in PASSES]
    + [f"{n}_{a}" for n in ("ring_full", "scores", "pv") for a in (1, 2, 3)] + ["scattered"],
    "scalar": ["ones_made", "proj_t", "part_mid", "tanh_done", "gates_out", "silu_moe", "silu_3", "bias_moe", "onehot_t"]
    + [f"{n}_{u}" for n in ("relu1", "relu", "silu", "shared") for u in (0, 1)]
    + [f"xT_{p}" for p in PASSES] + [f"exp_{a}" for a in (1, 2, 3)],
    "vector": ["part_hi", "part_rest", "v_staged", "ln_var", "hidden_0", "hidden_1", "hidden_moe", "gate_in",
               "gate_diff", "onehot", "picked", "expert_out", "gather_map", "scatter_map", "entries", "merged",
               "up_done", "fw_ready"]
    + [f"hb_{p}" for p in ("A", "B1_0", "B1_1", "B2_0", "B2_1", "Q3_0", "Q3_1", "B3")]
    + ["added_0", "added_1", "down_done"]
    + [f"{n}_{a}" for n in ("ring_free", "mx_ready", "max_split", "acc_out", "normed") for a in (1, 2, 3)],
    "gpsimd": ["consts", "part_lo", "ln_rstd", "ctx_pad", "o_taken_B1_0", "o_taken_B1_1", "o_taken_B2_0",
               "o_taken_B2_1", "o_taken_O3_0", "o_taken_O3_1", "kept", "token_row", "ones_again"],
    "sync": ["x_in", "index_in", "bias_in", "weights_in", "later_in", "parts_out_0", "parts_out_1", "v_out_0", "v_out_1", "v_out_2", "ctx_in", "ew_in", "fw_in", "out_done"]
    + [f"{n}_{a}" for n in ("v_in", "stacks_in", "max_out", "max_in") for a in (1, 2, 3)],
}


class Chain:

    def __init__(self, eng, sem):
        self.eng, self.sem, self.base, self.k, self.it = eng, sem, 0, 0, None

    def loop(self, it, per):
        self.base, self.k, self.it, self.per = self.base + self.k, 0, it, per

    def end(self, times):
        assert self.k == self.per, (self.k, self.per)
        self.base, self.k, self.it = self.base + times * self.per, 0, None

    def link(self, ins):
        self.note(ins)
        self.join()

    def note(self, ins):
        self.k += 1
        ins.then_inc(self.sem, 1)

    def join(self):
        at = self.base + self.k
        self.eng.wait_ge(self.sem, at if self.it is None else self.it * self.per + at)


KT = -(-CTX // P)
FIRST, RING = 4, 3
ACC = 7
QW = S // 2
WT = QW // P


def chunk_of(causal, qp, h):
    return ((0, 3), (1, 2))[qp][h] if causal else 2 * qp + h


def steps_of(causal, qp):
    out = []
    for h in range(2):
        qc = chunk_of(causal, qp, h)
        kts = range(R * qc + R) if causal else range(KT)
        for kt in kts:
            c0 = max(0, kt - R * qc) * P if causal else 0
            kn = P if causal else min(P, CTX - kt * P)
            out.append((h, kt, c0, kn, kt == kts[-1]))
    return out


def tiles_of(causal, qp):
    out = []
    for q8 in range(WT):
        nk = (R * chunk_of(causal, qp, q8 // R) + q8 % R + 1) * P if causal else CTX // CH * CH
        for j in range(4):
            for kb in range(-(-nk // CH)):
                n = min(CH, nk - kb * CH)
                out.append((j, 1, q8, kb, n, causal and kb * CH + n == nk))
        if not causal:
            out.append((0, 4, q8, CTX // CH, CTX % CH, False))
    return out


def next_of(g, qp):
    if qp == 0:
        return g, 1
    return (g + 1, 0) if g + 1 < NG else None


def ring_base(causal, g, qp):
    if g < 0:
        return 0
    n = len(tiles_of(causal, 0)) + 1
    for gg in range(NG):
        for w in range(2):
            if (gg, w) == (g, qp):
                return n
            after = next_of(gg, w)
            n += 2 + (len(tiles_of(causal, after[1])) + 1 if after else 0)
    return n


def step_base(causal, g, qp):
    per = [len(steps_of(causal, w)) for w in range(2)]
    return g * sum(per) + sum(per[:qp])


def spread(causal, g, qp):
    steps, after = steps_of(causal, qp), next_of(g, qp)
    tiles = tiles_of(causal, after[1]) if after else []
    last = len(steps) - 4
    per = [[] for _ in steps]
    for i in range(len(tiles)):
        per[i * last // len(tiles)].append(i)
    return [(t[:len(t) * 3 // 10], t[len(t) * 3 // 10:len(t) * 7 // 10], t[len(t) * 7 // 10:]) for t in per], last


def build(nc, A, out):
    ctx = ExitStack()
    with ctx:
        def sb(name, shape, dt=F32):
            return ctx.enter_context(nc.sbuf_tensor(name, shape, dt))

        sems = {}

        def sem(name):
            if name not in sems:
                sems[name] = ctx.enter_context(nc.semaphore(name))
            return sems[name]

        x_sb = sb("x_sb", [P, S // P, E])
        xmean = sb("xmean", [P, S // P])
        xrstd = sb("xrstd", [P, S // P])
        o_sb = sb("o_sb", [P, S // P, E])
        hb = sb("hb", [P, R, E])
        xT = sb("xT", [P, 2, CH])
        z = sb("z", [P, R, E])
        z2 = sb("z2", [P, R, E])
        st, mv, ve, rs = ([sb(f"{n}{u}", [P, R, *w]) for u in range(2)]
                          for n, w in (("st", [6]), ("mv", [2]), ("ve", []), ("rs", [])))
        mhalf = sb("mhalf", [P, R])
        identf = sb("identf", [P, P])
        identb = sb("identb", [P, P], BF16)
        mask_kq = sb("mask_kq", [P, P], BF16)
        mask_qk = sb("mask_qk", [P, P], BF16)
        accS = sb("accS", [P, 2, CH])
        rec = sb("rec", [P, R * 4])
        mxb = [sb(f"mxb{w}", [P, 4 * WT, 4]) for w in range(2)]
        mx = sb("mx", [P, 4 * WT])
        mneg = sb("mneg", [4 * WT, P])
        mres = sb("mres", [4 * WT, P])
        mparts = sb("mparts", [4 * WT, 3, P], BF16)
        wt = {n: sb(n, [P, 2, E]) for n in ("wq1", "wk1", "wv1", "wo1", "wq2", "wk2", "wv2", "wo2", "wf",
                                            "wq3", "wk3", "wv3", "wo3", "sw12")}
        sw3 = sb("sw3", [P, E])
        gate_w = sb("gate_w", [P, 2, 16])
        bias_col = {n: sb(n, [P, 2]) for n in ("bq3", "bk3")}
        rows = {}
        for n, w in (("g1", E), ("b1", E), ("g2", E), ("b2", E), ("g3", E),
                     ("b3", E), ("bv3", E), ("slg", HF), ("slb", HF),
                     ("elg", HF), ("elb", HF), ("gateb", 16), ("expb", NE)):
            rows[n] = sb("row_" + n, [P, w])
        bias_row = {n: wt[w][0:1, k, :] for n, w, k in (("bo2", "wq1", 0), ("bf", "wq1", 1), ("sb12", "wk1", 0),
                                                       ("sb3", "wk1", 1), ("bo1", "wv1", 0), ("bo3", "wv1", 1))}
        tg = sb("tg", [P, 4])
        iota8 = sb("iota8", [P, NE])
        tok_id = sb("tok_id", [P, S // P])
        code = sb("code", [P, M + R])
        first_code = sb("first_code", [P, R])
        entry_id = sb("entry_id", [P, R])
        ones = sb("ones", [1, P])
        sc = sb("sc", [P, R, 16])
        sel = sb("sel", [P, R, NE])
        oh = sb("oh", [P, R, NE])
        small = sb("small", [P, 8, R])
        ohT = sb("ohT", [NE, R, P])

        arena = sb("arena", [P, 26624])

        def region(at, shape, dt=F32):
            n = 1
            for d in shape:
                n *= d
            words = n if dt != BF16 else n // 2
            v = arena[:, at:at + words]
            if dt != F32:
                v = v.bitcast(dt)
            if len(shape) == 2:
                v = v.rearrange("p (a b) -> p a b", b=shape[1])
            elif len(shape) == 3:
                v = v.rearrange("p (a b c) -> p a b c", b=shape[1], c=shape[2])
            return v

        stackQ = [region(4096 * h, (4, S), BF16) for h in range(2)]
        stackK = [region(8192 + 4096 * h, (4, S), BF16) for h in range(2)]
        probs = [region(16384 + 1024 * n, (2, CH)) for n in range(4)]
        vg = [region(22528 + 2048 * h, (S // P, 4, 32)) for h in range(2)]
        pt = [region(at, (2, CH)) for at in (16384, 1024)]
        pr = [region(at, (2, CH)) for at in (17408, 2048)]
        parts = [[region(at + 512 * n, (2, CH), BF16) for n in range(3)] for at in (18432, 3072)]
        vst = [region(at, (R, H, 32)) for at in (19968, 4608, 22016)]
        hc = region(0, (R, E))
        xTc = accS
        ew12 = region(0, (2, 2 * NE * HF))
        ew3 = region(4096, (NE * E,))
        eb = region(6144, (2 * HF + E,))
        hb_1 = region(24064, (R, E))
        z_1 = region(17408, (R, E))
        z2_1 = region(18432, (R, E))
        Z_B1 = (z, region(6656, (R, E)))
        HB, XT, Z, Z2 = (hb, hb_1), (xT, accS), (z, z_1), (z2, z2_1)
        SG = [region(25088 + 512 * u, (R, HF)) for u in range(2)]
        shr = region(19968, (S // P, E))
        which = region(8192, (S // P, M))
        where_to = region(8192, (R, S))
        bsel = region(16384, (R, 2 * HF + E))
        hs = region(24064, (R, 2 * HF))
        vals = region(6656, (R, E + 4))
        row_id = region(24064, (M,))
        mtmp = region(24576, (M,))
        idx_i = region(25088, (2, M + R), I32)
        wgu = region(0, (2, 2, FF))
        wd = region(3072, (FF // P, E))
        hT = region(4608, (FF // P, CH))
        sgT = region(7680, (2, CH))
        wint = region(8704, (2, 2, FF), I32)
        dint = region(11776, (FF // P, E), I32)

        ps = ctx.enter_context(nc.psum_tensor("ps", [P, 8, 512], F32))

        scr_qk = {}
        for n in ("q1", "k1", "q2", "k2", "q3", "k3"):
            scr_qk[n] = nc.dram_tensor("scr_" + n, [3, E, S], BF16, kind="Internal").ap()
        scr_v = {n: nc.dram_tensor("scr_" + n, [S, H * 32], F32, kind="Internal").ap() for n in ("v1", "v2", "v3")}
        scr_m = nc.dram_tensor("scr_m", [3, 3, NG * 2, 4 * QW], BF16, kind="Internal").ap()

        weights_later = []

        def w2(name, src):
            weights_later.append((wt[name][:, :, :], src.rearrange("(c p) n -> p c n", p=P)))

        for n in ("wo1", "wq2", "wo2", "wf", "wq3", "wo3", "sw12"):
            w2(n, A[n])
        weights_later.append((sw3[:, :], A["sw3"]))
        weights_later.append((gate_w[:, :, 0:NE + 1], A["gate_w"].rearrange("(c p) n -> p c n", p=P)))
        weights_later.append((bias_col["bq3"][:, :], A["bq3"]))
        for n in rows:
            if n != "bv3":
                w = A[n].shape[0]
                weights_later.append((rows[n][:, 0:w], A[n].partition_broadcast(P)))
        weights_later.append((tg[:, :], A["gates"].partition_broadcast(P)))

        weights_in = sem("weights_in")
        x_in = sem("x_in")
        first_names = ("wk1", "wq1", "wv1", "wk2", "wk3", "wv2", "wv3")
        weights_first = [(wt[n][:, :, :], A[n].rearrange("(c p) n -> p c n", p=P)) for n in first_names]
        weights_first += [(bias_col["bk3"][:, :], A["bk3"]), (rows["bv3"][:, 0:E], A["bv3"].partition_broadcast(P))]
        W_FIRST, W_LATER = 16 * len(weights_first), 16 * len(weights_later)


        SPLITS = {"AC": (0, 4), "B1": (16, 2), "Q3": (20, 2)}
        LNS = {"A": (0, 1), "B1": (4, 2), "B2x": (8, 8), "MOE": (24, 1), "Q3": (25, 2), "B3": (29, 1)}

        def split_n(p, c, k):
            base, per = SPLITS[p]
            return c * per + (base + k)

        def split_set(p, c, k):
            if p == "AC":
                return k % 2, c * 2 + k // 2
            return k, c + {"B1": 8, "Q3": 10}[p]

        def ln_n(p, c, k):
            base, per = LNS[p]
            return c * per + (base + k)

        proj_t, part_hi, part_rest, part_mid, part_lo = (
            sem(n) for n in ("proj_t", "part_hi", "part_rest", "part_mid", "part_lo"))
        parts_out = [sem(f"parts_out_{w}") for w in range(2)]
        v_staged, v_out = sem("v_staged"), [sem(f"v_out_{w}") for w in range(3)]
        ln_var, ln_rstd = sem("ln_var"), sem("ln_rstd")
        consts = sem("consts")
        N_CONST = 20

        def apart(eng):
            eng.nop(nofuse=True)

        def chunk_banks(u):
            return ps[:, 4 + 2 * u:6 + 2 * u, :].rearrange("p b (r e) -> p (b r) e", e=E)

        block = ctx.enter_context(nc.Block())

        TR = {"A": 1, "C": 1, "B1_0": 2, "B1_1": 2, "B2_0": 4, "B2_1": 4, "Q3_0": 1, "Q3_1": 1, "O3_0": 1, "O3_1": 1, "B3": 1}

        @block.sync
        def _(sp):
            for name in SIGNALS["sync"]:
                sp.sem_inc(sem(name), START)

            def load_ctx(c, last=False):
                sp.wait_ge(sem("tr_C"), START + c)
                if last:
                    sp.wait_ge(sem("ctx_pad"), START + 1)
                apart(sp)
                if last:
                    sp.dma_start(hc[0:CTX - 3 * CH, 0, :], A["ctx"][0, 3 * CH:CTX, :]).then_inc(sem("ctx_in"), 16)
                else:
                    sp.dma_start(hc, A["ctx"][0, ds(c * CH, CH), :].rearrange("(r p) e -> p r e", p=P))\
                      .then_inc(sem("ctx_in"), 16)

            for t in range(NC):
                sp.dma_start(x_sb[:, 4 * t:4 * t + 4, :],
                             A["x"][0, t * CH:(t + 1) * CH, :].rearrange("(r p) e -> p r e", p=P)).then_inc(x_in, 16)
            sp.dma_start(idx_i[:, 0, 0:M], A["index_b"].partition_broadcast(P)).then_inc(sem("index_in"), 16)
            sp.dma_start(idx_i[:, 1, 0:M], A["index_t"].partition_broadcast(P)).then_inc(sem("index_in"), 16)
            sp.dma_start(idx_i[:, :, M:M + R], A["index_col"]).then_inc(sem("index_in"), 16)
            for dst, src in weights_first:
                sp.dma_start(dst, src).then_inc(weights_in, 16)
            load_ctx(0)
            for dst, src in weights_later:
                sp.dma_start(dst, src).then_inc(sem("later_in"), 16)

            def store_parts(p, c, k, name, chunk=None):
                n = split_n(p, c, k)
                w = split_set(p, c, k)[0]
                chunk = c if chunk is None else chunk
                dst = [scr_qk[name][i, :, ds(chunk * CH, CH)].rearrange("(o p) q -> p o q", p=P) for i in range(3)]
                sp.wait_ge(part_hi, START + n + 1)
                apart(sp)
                sp.dma_start(dst[0], parts[w][0]).then_inc(parts_out[w], 16)
                sp.wait_ge(part_mid, START + n + 1)
                apart(sp)
                sp.dma_start(dst[1], parts[w][1]).then_inc(parts_out[w], 16)
                sp.wait_ge(part_lo, START + n + 1)
                apart(sp)
                sp.dma_start(dst[2], parts[w][2]).then_inc(parts_out[w], 16)

            def store_v(c, w):
                sp.wait_ge(v_staged, START + c * 3 + (w + 1))
                apart(sp)
                sp.dma_start(scr_v[f"v{w + 1}"][ds(c * CH, CH), :].rearrange("(r p) n -> p r n", p=P),
                             vst[w].rearrange("p r h d -> p r (h d)")).then_inc(v_out[w], 16)

            def pass_ac(c, last):
                store_parts("AC", c, 0, "k1")
                store_parts("AC", c, 1, "q1")
                store_v(c, 0)
                if not last:
                    load_ctx(c + 1, c == NC - 2 if isinstance(c, int) else False)
                store_parts("AC", c, 2, "k2")
                store_parts("AC", c, 3, "k3")
                store_v(c, 1)
                store_v(c, 2)

            with sp.Fori(0, NC - 2) as c:
                pass_ac(c, False)
            pass_ac(NC - 2, False)
            pass_ac(NC - 1, True)
            sp.wait_ge(sem("mm_A"), START + 12)
            for n, dst in bias_row.items():
                sp.dma_start(dst, A[n].unsqueeze(0)).then_inc(sem("bias_in"), 16)

            def attention_loads(a, parts_needed):
                sp.wait_ge(parts_out[0], START + 48 * parts_needed)
                sp.wait_ge(parts_out[1], START + 48 * parts_needed)
                for w in range(3):
                    sp.wait_ge(v_out[w], START + 16 * NC)
                causal = a == 1

                def load_stacks(g):
                    half = g % 2
                    if g >= 2:
                        sp.wait_ge(sem(f"acc_out_{a}"), START + 4 * (g - 1))
                    for blk in range(6):
                        for stack, parts_of, nm in ((stackQ, Q_PARTS, "q"), (stackK, K_PARTS, "k")):
                            sp.dma_start(stack[half][D * blk:D * blk + D, :, :],
                                         scr_qk[f"{nm}{a}"][parts_of[blk], g * 64:g * 64 + 64, :]
                                         .rearrange("(h d) q -> d h q", d=D))\
                              .then_inc(sem(f"stacks_in_{a}"), 16)
                    sp.dma_start(vg[half].rearrange("p k h d -> p k (h d)"),
                                 scr_v[f"v{a}"][:, g * 128:g * 128 + 128].rearrange("(k p) n -> p k n", p=P))\
                      .then_inc(sem(f"v_in_{a}"), 16)
                    sp.wait_ge(sem(f"stacks_in_{a}"), START + 192 * (g + 1))
                    sp.wait_ge(sem(f"v_in_{a}"), START + 16 * (g + 1))

                def move_maxima(g, qp):
                    w = qp + 2 * g
                    sp.wait_ge(sem(f"max_split_{a}"), START + w + 1)
                    for part in range(3):
                        sp.dma_start(scr_m[a - 1, part, w:w + 1, :].rearrange("o (w q) -> (o w) q", q=P),
                                     mparts[:, part, :]).then_inc(sem(f"max_out_{a}"), 16)
                    sp.wait_ge(sem(f"max_out_{a}"), START + w * 48 + 48)
                    for h in range(2):
                        at = chunk_of(causal, qp, h) * CH
                        sp.dma_start(stackQ[g % 2][QROWS:QROWS + 3, :, at:at + CH],
                                     scr_m[a - 1, :, w:w + 1, :].rearrange("t o (j q) -> t (o j) q", q=QW)
                                     [:, :, h * CH:h * CH + CH]).then_inc(sem(f"max_in_{a}"), 16)
                    sp.wait_ge(sem(f"max_in_{a}"), START + w * 32 + 32)

                load_stacks(0)
                move_maxima(0, 0)
                load_stacks(1)
                for g in range(NG):
                    move_maxima(g, 1)
                    if g + 1 < NG:
                        move_maxima(g + 1, 0)
                    if g + 2 < NG:
                        load_stacks(g + 2)

            attention_loads(1, 8)
            with sp.Fori(0, NC // 2) as c:
                for u in range(2):
                    store_parts("B1", c, u, "q2", c * 2 + u)
            attention_loads(2, 10)
            sp.wait_ge(sem("normed_2"), START + 1)
            ew_in = sem("ew_in")
            sp.dma_start(ew12, A["ew12"].rearrange("(c p) n -> p c n", p=P)).then_inc(ew_in, 16)
            sp.dma_start(ew3, A["ew3"]).then_inc(ew_in, 16)
            sp.dma_start(eb[0:NE, :], A["eb"]).then_inc(ew_in, 16)
            with sp.Fori(0, NC // 2) as c:
                for u in range(2):
                    store_parts("Q3", c, u, "q3", c * 2 + u)
            attention_loads(3, 12)
            sp.wait_ge(sem("normed_3"), START + 1)
            fw_in = sem("fw_in")
            sp.dma_start(wint[:, 0, :, :], A["w_gate"].rearrange("(c p) n -> p c n", p=P)).then_inc(fw_in, 16)
            sp.dma_start(wint[:, 1, :, :], A["w_up"].rearrange("(c p) n -> p c n", p=P)).then_inc(fw_in, 16)
            sp.dma_start(dint, A["w_down"].rearrange("(c p) n -> p c n", p=P)).then_inc(fw_in, 16)
            with sp.Fori(0, NC) as c:
                sp.wait_ge(sem("down_done"), START + c + 1)
                apart(sp)
                sp.dma_start(out[0, ds(c * CH, CH), :].rearrange("(r p) e -> p r e", p=P),
                             x_sb[:, ds(c * 4, 4), :]).then_inc(sem("out_done"), 16)
            sp.wait_ge(sem("out_done"), START + 16 * NC)

        @block.gpsimd
        def _(pool):
            for name in SIGNALS["gpsimd"]:
                pool.sem_inc(sem(name), START)
            pool.memset(identf[:, :], 0.0).then_inc(consts, 1)
            pool.memset(identb[:, :], 0.0).then_inc(consts, 1)
            pool.memset(mask_kq[:, :], 0.0).then_inc(consts, 1)
            pool.memset(mask_qk[:, :], 0.0).then_inc(consts, 1)
            pool.wait_ge(consts, START + 4)
            pool.affine_select(out=identf[:, :], in_=identf[:, :], compare_op=ALU.not_equal, fill=1.0, base=0,
                               pattern=[[-1, P]], channel_multiplier=1).then_inc(consts, 1)
            pool.affine_select(out=identb[:, :], in_=identb[:, :], compare_op=ALU.not_equal, fill=1.0, base=0,
                               pattern=[[-1, P]], channel_multiplier=1).then_inc(consts, 1)
            pool.affine_select(out=mask_kq[:, :], in_=mask_kq[:, :], compare_op=ALU.is_ge, fill=MASKED, base=0,
                               pattern=[[1, P]], channel_multiplier=-1).then_inc(consts, 1)
            pool.affine_select(out=mask_qk[:, :], in_=mask_qk[:, :], compare_op=ALU.is_ge, fill=MASKED, base=0,
                               pattern=[[-1, P]], channel_multiplier=1).then_inc(consts, 1)
            pool.memset(mhalf[:, :], -0.5).then_inc(consts, 1)
            for w in range(3):
                pool.memset(vst[w], 0.0).then_inc(consts, 1)
            pool.wait_ge(consts, START + 12)
            for w in range(3):
                pool.memset(vst[w][:, :, :, D:D + 1], 1.0).then_inc(consts, 1)
            pool.iota(iota8[:, :], [[1, NE]], base=-NE, channel_multiplier=0,
                      allow_small_or_imprecise_dtypes=True).then_inc(consts, 1)
            pool.iota(tok_id[:, :], [[P, S // P]], base=1, channel_multiplier=1,
                      allow_small_or_imprecise_dtypes=True).then_inc(consts, 1)

            pool.memset(ones[:, :], 1.0).then_inc(consts, 1)
            pool.iota(row_id, [[1, M]], base=-M, channel_multiplier=0,
                      allow_small_or_imprecise_dtypes=True).then_inc(consts, 1)
            pool.iota(entry_id[:, :], [[P, R]], base=-M, channel_multiplier=1,
                      allow_small_or_imprecise_dtypes=True).then_inc(consts, 1)

            def rstd(p, c, k, u=0):
                n = ln_n(p, c, k)
                pool.wait_ge(ln_var, START + n + 1)
                pool.tensor_tensor(rs[u][:, :], ve[u][:, :], mhalf[:, :], ALU.pow).then_inc(ln_rstd, 1)

            def split(p, c, k):
                n = split_n(p, c, k)
                w, uses = split_set(p, c, k)
                pool.wait_ge(part_mid, START + n + 1)
                pool.wait_ge(parts_out[w], START + uses * 48)
                apart(pool)
                pool.tensor_tensor(parts[w][2], pr[w], parts[w][1], ALU.subtract).then_inc(part_lo, 1)

            def pass_ac(c, last):
                split("AC", c, 0)
                if not last:
                    rstd("A", c + 1, 0)
                split("AC", c, 1)
                if isinstance(c, int) and c == NC - 2:
                    pool.wait_ge(sem("tr_C"), START + c + 1)
                    pool.memset(hc, 0.0).then_inc(sem("ctx_pad"), 1)
                    pool.wait_ge(sem("ctx_pad"), START + 1)
                split("AC", c, 2)
                split("AC", c, 3)

            rstd("A", 0, 0)
            with pool.Fori(0, NC - 2) as c:
                pass_ac(c, False)
            pass_ac(NC - 2, False)
            pass_ac(NC - 1, True)

            def take_o(p, c, u, per):
                pool.wait_ge(sem(f"tr_{p}_{u}"), START + c * per)
                apart(pool)
                pool.tensor_copy(HB[u][:, :, :], o_sb[:, ds(c * 8 + 4 * u, 4), :])\
                    .then_inc(sem(f"o_taken_{p}_{u}"), 1)

            pool.wait_ge(sem("normed_1"), START + 1)
            with pool.Fori(0, NC // 2) as c:
                for u in range(2):
                    take_o("B1", c, u, 2)
                for u in range(2):
                    rstd("B1", c, u, u)
                for u in range(2):
                    split("B1", c, u)
            pool.wait_ge(sem("normed_2"), START + 1)
            with pool.Fori(0, NC // 2) as c:
                for u in range(2):
                    if u == 0:
                        pool.wait_ge(sem("kept"), START + c * 2)
                    take_o("B2", c, u, 4)
                for k in range(3):
                    for u in range(2):
                        rstd("B2x", c, 2 * k + u, u)
                for u in range(2):
                    pool.wait_ge(sem(f"hb_B2_{u}"), START + c * 2 + 2)
                    pool.wait_ge(sem(f"o_taken_B2_{u}"), START + c + 1)
                    apart(pool)
                    pool.tensor_copy(o_sb[:, ds(c * 8 + 4 * u, 4), :], HB[u][:, :, :]).then_inc(sem("kept"), 1)
                for u in range(2):
                    rstd("B2x", c, 6 + u, u)
            pool.wait_ge(sem("mm_MOE"), START + 1)
            pool.iota(where_to, [[0, R], [1, S]], base=1, channel_multiplier=0,
                      allow_small_or_imprecise_dtypes=True).then_inc(sem("token_row"), 1)
            rstd("MOE", 0, 0)
            with pool.Fori(0, NC // 2) as c:
                for u in range(2):
                    rstd("Q3", c, u, u)
                for u in range(2):
                    split("Q3", c, u)
            pool.wait_ge(sem("scattered"), START + NC)
            pool.wait_ge(part_lo, START + 24)
            for half in range(2):
                pool.memset(stackK[half][QROWS:QROWS + 3, :, :], 1.0).then_inc(sem("ones_again"), 1)
                pool.wait_ge(sem("ones_again"), START + half + 1)
            pool.wait_ge(sem("normed_3"), START + 1)
            with pool.Fori(0, NC // 2) as c:
                for u in range(2):
                    take_o("O3", c, u, 1)
            for u in range(2):
                pool.wait_ge(sem(f"o_taken_O3_{u}"), START + NC // 2)
            with pool.Fori(0, NC) as c:
                rstd("B3", c, 0)

        @block.scalar
        def _(act):
            for name in SIGNALS["scalar"]:
                act.sem_inc(sem(name), START)
            def evac_T(p, c, k, mm_before, bank=0, dst=None):
                act.wait_ge(sem(f"tr_{p}"), START + c * TR[p] + k + 1)
                act.wait_ge(sem(f"mm_{p}"), START + mm_before)
                act.activation(xT[:, :, :] if dst is None else dst, ps[:, bank:bank + 2, :],
                               ACT.Copy).then_inc(sem(f"xT_{p}"), 1)

            def take_proj(p, c, k, bank, mm_at, bias=None, mm=None):
                n = split_n(p, c, k)
                act.wait_ge(sem(f"mm_{mm or p}"), START + mm_at)
                w, _ = split_set(p, c, k)
                act.wait_ge(part_rest, START + n - 1)
                if bias is None:
                    act.activation(pt[w], ps[:, bank:bank + 2, :], ACT.Copy).then_inc(proj_t, 1)
                else:
                    act.activation(pt[w][:, 0, :], ps[:, bank, :], ACT.Identity, bias=bias[:, 0:1])
                    act.activation(pt[w][:, 1, :], ps[:, bank + 1, :], ACT.Identity, bias=bias[:, 1:2])\
                       .then_inc(proj_t, 1)

            def middle(p, c, k):
                n = split_n(p, c, k)
                w, uses = split_set(p, c, k)
                act.wait_ge(part_rest, START + n + 1)
                act.wait_ge(parts_out[w], START + uses * 48)
                act.activation(parts[w][1], pr[w], ACT.Copy).then_inc(part_mid, 1)

            act.wait_ge(consts, START + N_CONST)
            for half in range(2):
                act.activation(stackK[half][QROWS:QROWS + 3, :, :].rearrange("t h q -> t (h q)"),
                               mhalf[QROWS:QROWS + 3, 0:1].to_broadcast([3, 4 * S]), ACT.Copy, scale=-2.0)\
                   .then_inc(sem("ones_made"), 1)
            act.wait_ge(weights_in, START + W_FIRST)
            with act.Fori(0, NC) as c:
                evac_T("A", c, 0, c * 3)
                take_proj("AC", c, 0, 2, mm_at=c * 3 + 1, mm="A")
                evac_T("C", c, 0, c * 4, dst=xTc[:, :, :])
                middle("AC", c, 0)
                take_proj("AC", c, 1, 4, mm_at=c * 3 + 2, mm="A")
                middle("AC", c, 1)
                take_proj("AC", c, 2, 2, mm_at=c * 4 + 1, mm="C")
                middle("AC", c, 2)
                take_proj("AC", c, 3, 4, mm_at=c * 4 + 2, bias=bias_col["bk3"], mm="C")
                middle("AC", c, 3)
            act.wait_ge(sem("later_in"), START + W_LATER)
            act.activation(tg[:, :], tg[:, :], ACT.Tanh).then_inc(sem("tanh_done"), 1)

            def attend(a, causal, scale):
                def window(g, qp):
                    base = step_base(causal, g, qp)
                    for t, (_, _, c0, kn, _) in enumerate(steps_of(causal, qp)):
                        for pair in range(2):
                            act.wait_ge(sem(f"scores_{a}"), START + base * 2 + (2 * t + pair + 1))
                            if pair == 0:
                                act.wait_ge(sem(f"pv_{a}"), START + base + (t - 1))
                            act.activation(probs[2 * (t % 2) + pair][0:kn, :, c0:CH],
                                           ps[0:kn, 2 * pair:2 * pair + 2, c0:CH], ACT.Exp,
                                           scale=scale).then_inc(sem(f"exp_{a}"), 1)

                for g in range(NG):
                    for qp in range(2):
                        window(g, qp)

            attend(1, True, float(S) ** -0.5)
            with act.Fori(0, NC // 2) as c:
                for u in range(2):
                    evac_T(f"B1_{u}", c, 0, c * 2, 2 * u, XT[u][:, :, :])
                for u in range(2):
                    act.wait_ge(sem(f"mm_B1_{u}"), START + c * 2 + 1)
                    act.activation(Z_B1[u][:, :, :], chunk_banks(u), ACT.Relu).then_inc(sem(f"relu1_{u}"), 1)
                for u in range(2):
                    evac_T(f"B1_{u}", c, 1, c * 2 + 1, 2 * u, XT[u][:, :, :])
                for u in range(2):
                    take_proj("B1", c, u, 4 + 2 * u, c * 2 + 2, mm=f"B1_{u}")
                for u in range(2):
                    middle("B1", c, u)
            attend(2, False, float(CTX) ** -0.5)
            def flat(t):
                return t[:, :, :].rearrange("p r e -> p (r e)")

            with act.Fori(0, NC // 2) as c:
                for k in range(2):
                    for u in range(2):
                        evac_T(f"B2_{u}", c, k, c * 4 + k, 2 * u, XT[u][:, :, :])
                    for u in range(2):
                        act.wait_ge(sem(f"mm_B2_{u}"), START + c * 4 + (k + 1))
                        act.activation(Z[u][:, :, :], chunk_banks(u), ACT.Relu).then_inc(sem(f"relu_{u}"), 1)
                for u in range(2):
                    evac_T(f"B2_{u}", c, 2, c * 4 + 2, 2 * u, XT[u][:, :, :])
                for u in range(2):
                    act.wait_ge(sem(f"mm_B2_{u}"), START + c * 4 + 3)
                    act.activation(SG[u], chunk_banks(u)[:, :, 0:HF], ACT.Silu).then_inc(sem(f"silu_{u}"), 1)
                for u in range(2):
                    act.wait_ge(sem(f"tr_B2_{u}"), START + c * 4 + 4)
                    act.activation(flat(Z2[u])[:, 0:CH], ps[:, 2 * u, :], ACT.Copy).then_inc(sem(f"xT_B2_{u}"), 1)
                for u in range(2):
                    act.wait_ge(sem(f"mm_B2_{u}"), START + c * 4 + 4)
                    apart(act)
                    act.activation(shr[:, ds(c * 8 + 4 * u, 4), :], chunk_banks(u), ACT.Copy)\
                       .then_inc(sem(f"shared_{u}"), 1)
            act.wait_ge(sem("mm_MOE"), START + 1)
            act.activation(xT[:, :, :], ps[:, 0:2, :], ACT.Copy).then_inc(sem("xT_MOE"), 1)
            act.wait_ge(sem("gate_in"), START + 1)
            act.activation(sc[:, :, 0:NE + 1], sc[:, :, 0:NE + 1], ACT.Sigmoid).then_inc(sem("gates_out"), 1)
            act.wait_ge(sem("tr_MOE"), START + 1)
            act.activation(ohT[:, :, :].rearrange("e r p -> e (r p)"), ps[0:NE, 4, :], ACT.Copy)\
               .then_inc(sem("onehot_t"), 1)
            act.wait_ge(sem("gate_diff"), START + 1)
            act.activation(small[:, 3, :], small[:, 2, :], ACT.Sigmoid).then_inc(sem("gates_out"), 1)
            act.activation(small[:, 4, :], small[:, 2, :], ACT.Sigmoid, scale=-1.0).then_inc(sem("gates_out"), 1)
            act.wait_ge(sem("mm_MOE"), START + 4)
            act.activation(bsel[:, 0:3, :], ps[:, 5:8, :], ACT.Copy).then_inc(sem("bias_moe"), 1)
            act.activation(bsel[:, 3, :], ps[:, 4, :], ACT.Copy).then_inc(sem("bias_moe"), 1)
            act.wait_ge(sem("picked"), START + 4)
            act.activation(SG[0], hs[:, :, 0:HF], ACT.Silu).then_inc(sem("silu_moe"), 1)
            act.wait_ge(sem("tr_MOE"), START + 2)
            act.activation(flat(z2)[:, 0:CH], ps[:, 0, :], ACT.Copy).then_inc(sem("xT_MOE"), 1)
            with act.Fori(0, NC // 2) as c:
                for u in range(2):
                    evac_T(f"Q3_{u}", c, 0, c, 2 * u, XT[u][:, :, :])
                for u in range(2):
                    take_proj("Q3", c, u, 4 + 2 * u, c + 1, bias_col["bq3"], mm=f"Q3_{u}")
                for u in range(2):
                    middle("Q3", c, u)
            attend(3, False, float(D) ** -0.5)
            with act.Fori(0, NC // 2) as c:
                for u in range(2):
                    evac_T(f"O3_{u}", c, 0, c, 2 * u, XT[u][:, :, :])

            def gates_up(c):
                for f in range(FF // P):
                    act.wait_ge(sem("mm_B3"), START + c * 7 + (f + 1))
                    act.wait_ge(sem("up_done"), START + c * 6 + max(0, f - 1))
                    act.activation(sgT[:, f % 2, :], ps[:, 2 + 2 * (f % 2), :], ACT.Silu).then_inc(sem("silu_3"), 1)

            evac_T("B3", 0, 0, 0)
            with act.Fori(0, NC - 1) as c:
                gates_up(c)
                evac_T("B3", c + 1, 0, c * 7 + 6)
            gates_up(NC - 1)

        @block.tensor
        def _(pe):
            for name in SIGNALS["tensor"]:
                pe.sem_inc(sem(name), START)
            pe.wait_ge(weights_in, START + W_FIRST)
            pe.wait_ge(consts, START + N_CONST)

            def transposes(p, c, k, src, ready, value, bank=0, also=None):
                pe.wait_ge(ready, START + value)
                pe.wait_ge(sem(f"xT_{p}"), START + c * TR[p] + k)
                if also is not None:
                    pe.wait_ge(also[0], START + also[1])
                for cc in range(2):
                    for r in range(R):
                        last = pe.transpose(ps[:, bank + cc, r * P:(r + 1) * P], src[:, r, cc * P:(cc + 1) * P],
                                            identf[:, :])
                last.then_inc(sem(f"tr_{p}"), 1)

            def feature_major(p, w, bank, xt_at, n_out=2, free=None, xt=None):
                xt = xT if xt is None else xt
                pe.wait_ge(sem(f"xT_{p}"), START + xt_at)
                if free is not None:
                    pe.wait_ge(free[0], START + free[1])
                for oc in range(n_out):
                    for cc in range(2):
                        last = pe.matmul(ps[:, bank + oc, :], w[:, cc, oc * P:(oc + 1) * P], xt[:, cc, :],
                                         start=(cc == 0), stop=(cc == 1))
                last.then_inc(sem(f"mm_{p}"), 1)

            def token_major(p, w, bank, xt_at, free=None, xt=None, bias=None):
                xt = xT if xt is None else xt
                pe.wait_ge(sem(f"xT_{p}"), START + xt_at)
                if free is not None:
                    pe.wait_ge(free[0], START + free[1])
                for r in range(R):
                    dst = ps[:, bank + r // 2, (r % 2) * E:(r % 2) * E + E]
                    for cc in range(2):
                        last = pe.matmul(dst, xt[:, cc, r * P:(r + 1) * P], w[:, cc, :], start=(cc == 0),
                                         stop=(cc == 1 and bias is None))
                    if bias is not None:
                        last = pe.matmul(dst, ones[:, :], bias, start=False, stop=True)
                last.then_inc(sem(f"mm_{p}"), 1)

            with pe.Fori(0, NC) as c:
                transposes("A", c, 0, hb, sem("hb_A"), c + 1, also=(sem("xT_C"), c))
                feature_major("A", wt["wk1"], 2, c + 1, free=(proj_t, c * 4 - 1))
                transposes("C", c, 0, hc, sem("ctx_in"), c * 16 + 16, also=(sem("xT_A"), c + 1))
                feature_major("A", wt["wq1"], 4, c + 1, free=(proj_t, c * 4))
                token_major("A", wt["wv1"], 6, c + 1, free=(v_staged, c * 3))
                feature_major("C", wt["wk2"], 2, c + 1, free=(proj_t, c * 4 + 1), xt=xTc)
                feature_major("C", wt["wk3"], 4, c + 1, free=(proj_t, c * 4 + 2), xt=xTc)
                token_major("C", wt["wv2"], 6, c + 1, free=(v_staged, c * 3 + 1), xt=xTc)
                token_major("C", wt["wv3"], 6, c + 1, free=(v_staged, c * 3 + 2), xt=xTc)
            pe.wait_ge(sem("later_in"), START + W_LATER)
            pe.wait_ge(sem("bias_in"), START + 16 * len(bias_row))

            def attend(a, causal, before):
                scores, exps, pv = sem(f"scores_{a}"), sem(f"exp_{a}"), sem(f"pv_{a}")
                ring_full, ring_free = sem(f"ring_full_{a}"), sem(f"ring_free_{a}")
                for s, v in before:
                    pe.wait_ge(s, START + v)

                def enter(g, qp, k):
                    pe.wait_ge(ring_free, START + ring_base(causal, g, qp) + (k - RING + 1 if k else 0))
                    return FIRST + k % RING

                def row_tile(g, qp, b, tile):
                    j0, nj, q8, kb, n, masked = tile
                    sq, sk = stackQ[g % 2], stackK[g % 2]
                    q0 = chunk_of(causal, qp, q8 // R) * CH + q8 % R * P
                    for j in range(j0, j0 + nj):
                        at = (j - j0) * n
                        mm = pe.matmul(ps[:, b, at:at + n], sq[0:QROWS, j, q0:q0 + P],
                                       sk[0:QROWS, j, kb * CH:kb * CH + n], start=True, stop=not masked)
                    if masked:
                        mm = pe.matmul(ps[:, b, n - P:n], identb[:, :], mask_qk[:, :], start=False, stop=True)
                    mm.then_inc(ring_full, 1)

                def turn_maxima(b, before):
                    pe.wait_ge(sem(f"mx_ready_{a}"), START + before + 1)
                    pe.transpose(ps[0:4 * WT, b, 0:P], mx[:, :], identf[:, :]).then_inc(ring_full, 1)

                def maxima_alone():
                    tiles = tiles_of(causal, 0)
                    for k, tile in enumerate(tiles):
                        row_tile(0, 0, enter(-1, 0, k), tile)
                    turn_maxima(enter(-1, 0, len(tiles)), 0)

                def window(g, qp):
                    half = g % 2
                    sq, sk = stackQ[half], stackK[half]
                    steps, after = steps_of(causal, qp), next_of(g, qp)
                    tiles = tiles_of(causal, after[1]) if after else []
                    where, turn_at = spread(causal, g, qp)
                    base = step_base(causal, g, qp)
                    pe.wait_ge(sem(f"max_in_{a}"), START + 32 * (2 * g + qp + 1))
                    pe.wait_ge(sem(f"v_in_{a}"), START + 16 * (g + 1))

                    def values(t):
                        h, kt, c0, kn, last_kt = steps[t]
                        pe.wait_ge(exps, START + base * 2 + (2 * t + 2))
                        if kt == 0:
                            pe.wait_ge(sem(f"acc_out_{a}"), START + qp * 2 + (4 * g + h))
                        for j in range(4):
                            mm = pe.matmul(ps[32 * j:32 * j + 32, ACC, c0:CH], vg[half][0:kn, kt, j, :],
                                           probs[2 * (t % 2) + j // 2][0:kn, j % 2, c0:CH],
                                           start=(kt == 0), stop=last_kt, tile_position=(0, 32 * j))
                        mm.then_inc(pv, 1)

                    def turn(h, b):
                        pe.wait_ge(sem(f"acc_out_{a}"), START + qp * 2 + (4 * g + h + 1))
                        for r in range(R):
                            mm = pe.transpose(ps[:, b, r * P:(r + 1) * P], accS[:, h, r * P:(r + 1) * P],
                                              identf[:, :])
                        mm.then_inc(ring_full, 1)

                    k = [0]
                    for t, (h, kt, c0, kn, _) in enumerate(steps):
                        qc = chunk_of(causal, qp, h)
                        diag = causal and kt >= R * qc

                        def row_tiles(slot):
                            for idx in where[t][slot]:
                                if idx == 0:
                                    pe.wait_ge(sem(f"stacks_in_{a}"), START + 192 * (after[0] + 1))
                                b = enter(g, qp, k[0])
                                k[0] += 1
                                row_tile(*after, b, tiles[idx])

                        for pair in range(2):
                            pe.wait_ge(exps, START + base * 2 + (2 * t + pair - 1))
                            for jj in range(2):
                                j = 2 * pair + jj
                                mm = pe.matmul(ps[0:kn, j, c0:CH], sk[0:QROWS + 3, j, kt * P:kt * P + kn],
                                               sq[0:QROWS + 3, j, qc * CH + c0:qc * CH + CH],
                                               start=True, stop=not diag)
                                if diag:
                                    mm = pe.matmul(ps[:, j, c0:c0 + P], identb[:, :], mask_kq[:, :],
                                                   start=False, stop=True)
                            mm.then_inc(scores, 1)
                            row_tiles(pair)
                        if t >= 1:
                            values(t - 1)
                        if h == 1 and kt == 1:
                            turn(0, enter(g, qp, k[0]))
                            k[0] += 1
                        row_tiles(2)
                        if after and t == turn_at:
                            turn_maxima(enter(g, qp, k[0]), after[1] + 2 * after[0])
                            k[0] += 1
                    values(len(steps) - 1)
                    turn(1, enter(g, qp, k[0]))

                pe.wait_ge(sem(f"stacks_in_{a}"), START + 192)
                maxima_alone()
                for g in range(NG):
                    for qp in range(2):
                        window(g, qp)

            attend(1, True, ((proj_t, 16), (v_staged, 12), (sem("ones_made"), 2)))

            pe.wait_ge(sem("normed_1"), START + 1)
            with pe.Fori(0, NC // 2) as c:
                for u in range(2):
                    transposes(f"B1_{u}", c, 0, HB[u], sem(f"o_taken_B1_{u}"), c + 1, 2 * u)
                for u in range(2):
                    token_major(f"B1_{u}", wt["wo1"], 4 + 2 * u, c * 2 + 1, (proj_t, c * 2 + (15 + u)), XT[u],
                                bias_row["bo1"])
                for u in range(2):
                    transposes(f"B1_{u}", c, 1, HB[u], sem(f"hb_B1_{u}"), c + 1, 2 * u)
                for u in range(2):
                    feature_major(f"B1_{u}", wt["wq2"], 4 + 2 * u, c * 2 + 2, free=(sem(f"relu1_{u}"), c + 1), xt=XT[u])
            attend(2, False, ((proj_t, 20),))
            pe.wait_ge(sem("normed_2"), START + 1)
            with pe.Fori(0, NC // 2) as c:
                for u in range(2):
                    transposes(f"B2_{u}", c, 0, HB[u], sem(f"o_taken_B2_{u}"), c + 1, 2 * u)
                for u in range(2):
                    token_major(f"B2_{u}", wt["wo2"], 4 + 2 * u, c * 4 + 1, (sem(f"shared_{u}"), c), XT[u], bias_row["bo2"])
                for u in range(2):
                    transposes(f"B2_{u}", c, 1, HB[u], sem(f"hb_B2_{u}"), c * 2 + 1, 2 * u)
                for u in range(2):
                    token_major(f"B2_{u}", wt["wf"], 4 + 2 * u, c * 4 + 2, (sem(f"relu_{u}"), c * 2 + 1), XT[u],
                                bias_row["bf"])
                for u in range(2):
                    transposes(f"B2_{u}", c, 2, HB[u], sem(f"hb_B2_{u}"), c * 2 + 2, 2 * u)
                for u in range(2):
                    token_major(f"B2_{u}", wt["sw12"], 4 + 2 * u, c * 4 + 3, (sem(f"relu_{u}"), c * 2 + 2), XT[u],
                                bias_row["sb12"])
                for u in range(2):
                    pe.wait_ge(sem(f"hidden_{u}"), START + c + 1)
                    for r in range(R):
                        mm = pe.transpose(ps[:, 2 * u, r * P:(r + 1) * P], Z[u][:, r, 0:HF], identf[:, :])
                    mm.then_inc(sem(f"tr_B2_{u}"), 1)
                for u in range(2):
                    pe.wait_ge(sem(f"xT_B2_{u}"), START + c * 4 + 4)
                    for r in range(R):
                        dst = ps[:, 4 + 2 * u + r // 2, (r % 2) * E:(r % 2) * E + E]
                        pe.matmul(dst, Z2[u][:, :, :].rearrange("p r e -> p (r e)")[:, r * P:(r + 1) * P], sw3[:, :],
                                  start=True, stop=False)
                        mm = pe.matmul(dst, ones[:, :], bias_row["sb3"], start=False, stop=True)
                    mm.then_inc(sem(f"mm_B2_{u}"), 1)
            pe.wait_ge(sem("kept"), START + NC)
            pe.wait_ge(sem("gather_map"), START + 1)
            for half in range(2):
                for t in range(S // P):
                    mm = pe.matmul(ps[:, half, :], o_sb[:, t, half * P:(half + 1) * P], which[:, t, :],
                                   start=(t == 0), stop=(t == S // P - 1))
            mm.then_inc(sem("mm_MOE"), 1)
            pe.wait_ge(sem("xT_MOE"), START + 1)
            for u in range(2):
                pe.wait_ge(sem(f"shared_{u}"), START + NC // 2)
            for r in range(R):
                for cc in range(2):
                    mm = pe.matmul(ps[:, 4, r * 16:r * 16 + NE + 1], xT[:, cc, r * P:(r + 1) * P],
                                   gate_w[:, cc, 0:NE + 1], start=(cc == 0), stop=(cc == 1))
            mm.then_inc(sem("mm_MOE"), 1)
            pe.wait_ge(sem("ew_in"), START + 48)

            def experts_up(r):
                for n in range(4):
                    for cc in range(2):
                        mm = pe.matmul(ps[:, 4 * (r % 2) + n, :], xT[:, cc, r * P:(r + 1) * P],
                                       ew12[:, cc, n * 512:(n + 1) * 512], start=(cc == 0), stop=(cc == 1))
                mm.then_inc(sem("mm_MOE"), 1)

            experts_up(0)
            pe.wait_ge(sem("onehot"), START + 1)
            for r in range(R):
                mm = pe.transpose(ps[0:NE, 4, r * P:(r + 1) * P], oh[:, r, :], identf[:, :])
            mm.then_inc(sem("tr_MOE"), 1)
            pe.wait_ge(sem("onehot_t"), START + 1)
            for r in range(R):
                mm = pe.matmul(ps[:, 5 + r if r < 3 else 4, :], ohT[:, r, :], eb[0:NE, :], start=True, stop=True)
            mm.then_inc(sem("mm_MOE"), 1)
            pe.wait_ge(sem("bias_moe"), START + 2)
            experts_up(1)
            pe.wait_ge(sem("picked"), START + 1)
            experts_up(2)
            pe.wait_ge(sem("picked"), START + 2)
            experts_up(3)
            pe.wait_ge(sem("hidden_moe"), START + 1)
            for r in range(R):
                mm = pe.transpose(ps[:, 0, r * P:(r + 1) * P], z[:, r, 0:HF], identf[:, :])
            mm.then_inc(sem("tr_MOE"), 1)
            pe.wait_ge(sem("xT_MOE"), START + 2)
            for r in range(R):
                if r >= 2:
                    pe.wait_ge(sem("expert_out"), START + r - 1)
                for n in range(4):
                    mm = pe.matmul(ps[:, 4 * (r % 2) + n, :],
                                   z2[:, :, :].rearrange("p r e -> p (r e)")[:, r * P:(r + 1) * P],
                                   ew3[:, n * 512:(n + 1) * 512], start=True, stop=True)
                mm.then_inc(sem("mm_MOE"), 1)
            pe.wait_ge(sem("entries"), START + 1)
            pe.wait_ge(sem("scatter_map"), START + 1)
            for c in range(NC):
                if c >= 2:
                    pe.wait_ge(sem("merged"), START + c - 1)
                for r in range(R):
                    for m in range(R):
                        mm = pe.matmul(ps[:, 4 * (c % 2) + r, 0:E + 1], where_to[:, m, (R * c + r) * P:(R * c + r + 1) * P],
                                       vals[:, m, 0:E + 1], start=(m == 0), stop=(m == R - 1))
                mm.then_inc(sem("scattered"), 1)
            pe.wait_ge(sem("merged"), START + NC)
            with pe.Fori(0, NC // 2) as c:
                for u in range(2):
                    transposes(f"Q3_{u}", c, 0, HB[u], sem(f"hb_Q3_{u}"), c + 1, 2 * u)
                for u in range(2):
                    feature_major(f"Q3_{u}", wt["wq3"], 4 + 2 * u, c + 1, free=(proj_t, c * 2 + (19 + u)), xt=XT[u])
            attend(3, False, ((proj_t, 24), (sem("ones_again"), 2)))
            pe.wait_ge(sem("normed_3"), START + 1)
            with pe.Fori(0, NC // 2) as c:
                for u in range(2):
                    transposes(f"O3_{u}", c, 0, HB[u], sem(f"o_taken_O3_{u}"), c + 1, 2 * u)
                for u in range(2):
                    token_major(f"O3_{u}", wt["wo3"], 4 + 2 * u, c + 1, (sem(f"added_{u}"), c), XT[u], bias_row["bo3"])

            def feed_forward(c, last):
                pe.wait_ge(sem("xT_B3"), START + c + 1)
                for f in range(FF // P):
                    b = 2 + 2 * (f % 2)
                    pe.wait_ge(sem("up_done"), START + c * 6 + max(0, f - 1))
                    for u in range(2):
                        for cc in range(2):
                            mm = pe.matmul(ps[:, b + u, :], wgu[:, u, cc, f * P:(f + 1) * P], xT[:, cc, :],
                                           start=(cc == 0), stop=(cc == 1))
                    mm.then_inc(sem("mm_B3"), 1)
                if not last:
                    transposes("B3", c + 1, 0, hb, sem("hb_B3"), c + 2)
                pe.wait_ge(sem("up_done"), START + c * 6 + 6)
                pe.wait_ge(sem("down_done"), START + c)
                for r in range(R):
                    for f in range(FF // P):
                        mm = pe.matmul(ps[:, 6 + r // 2, (r % 2) * E:(r % 2) * E + E], hT[:, f, r * P:(r + 1) * P],
                                       wd[:, f, :], start=(f == 0), stop=(f == FF // P - 1))
                mm.then_inc(sem("mm_B3"), 1)

            for u in range(2):
                pe.wait_ge(sem(f"added_{u}"), START + NC // 2)
                pe.wait_ge(sem(f"xT_O3_{u}"), START + NC // 2)
            transposes("B3", 0, 0, hb, sem("hb_B3"), 1)
            pe.wait_ge(sem("fw_ready"), START + 3)
            with pe.Fori(0, NC - 1) as c:
                feed_forward(c, False)
            feed_forward(NC - 1, True)

        @block.vector
        def _(dve):
            for name in SIGNALS["vector"]:
                dve.sem_inc(sem(name), START)
            ch = Chain(dve, sem("vector_chain"))
            link, note, join = ch.link, ch.note, ch.join

            def ln_stats(src, eps, u=0):
                apart(dve)
                for r in range(R):
                    note(dve.bn_stats(st[u][:, r, :], src[:, r, :]))
                join()
                apart(dve)
                for r in range(R):
                    note(dve.bn_aggr(mv[u][:, r, :], st[u][:, r, :]))
                join()
                dve.tensor_scalar(ve[u][:, :], mv[u][:, :, 1], eps, None, ALU.add).then_inc(ln_var, 1)

            def ln_apply(n, src, dst, g=None, b=None, signal=None, u=0):
                w = src.shape[-1]
                dve.wait_ge(ln_rstd, START + n + 1)
                for r in range(R):
                    ins = dve.tensor_scalar(dst[:, r, :], src[:, r, :], mv[u][:, r, 0:1], rs[u][:, r:r + 1],
                                            ALU.subtract, ALU.mult)
                    if g is None and r == R - 1 and signal is not None:
                        ins.then_inc(signal, 1)
                    else:
                        note(ins)
                if g is not None:
                    join()
                    link(dve.tensor_tensor(dst, dst, wide(g, w), ALU.mult))
                    ins = dve.tensor_tensor(dst, dst, wide(b, w), ALU.add)
                    if signal is not None:
                        ins.then_inc(signal, 1)
                    else:
                        link(ins)
                elif signal is None:
                    join()

            def layernorm(p, c, k, src, dst, eps, g=None, b=None, signal=None):
                ln_stats(src, eps)
                ln_apply(ln_n(p, c, k), src, dst, g, b, signal)

            def wide(row, w):
                return row[:, 0:w].unsqueeze(1).to_broadcast([P, R, w])

            def chunk6():
                return ps[:, 6:8, :].rearrange("p b (r e) -> p (b r) e", e=E)

            def split(p, c, k):
                n = split_n(p, c, k)
                w, uses = split_set(p, c, k)
                dve.wait_ge(proj_t, START + n + 1)
                dve.wait_ge(parts_out[w], START + uses * 48)
                dve.tensor_copy(parts[w][0], pt[w]).then_inc(part_hi, 1)
                dve.wait_ge(part_hi, START + n + 1)
                dve.wait_ge(part_lo, START + n - 1)
                dve.tensor_tensor(pr[w], pt[w], parts[w][0], ALU.subtract).then_inc(part_rest, 1)

            def stage_v(c, w, mm, mm_at, bias=None):
                dve.wait_ge(sem(f"mm_{mm}"), START + mm_at)
                dve.wait_ge(v_out[w], START + c * 16)
                src = chunk6().rearrange("p r (h d) -> p r h d", d=D)
                if bias is None:
                    dve.tensor_copy(vst[w][:, :, :, 0:D], src).then_inc(v_staged, 1)
                else:
                    link(dve.tensor_tensor(z[:, :, :], chunk6(), wide(bias, E), ALU.add))
                    dve.tensor_copy(vst[w][:, :, :, 0:D], z[:, :, :].rearrange("p r (h d) -> p r h d", d=D))\
                       .then_inc(v_staged, 1)

            for w in range(2):
                link(dve.memset(mxb[w][:, :, :], MASKED))
            dve.wait_ge(consts, START + N_CONST)
            def norm_x(c):
                dve.wait_ge(sem("tr_A"), START + c)
                layernorm("A", c, 0, x_sb[:, ds(c * 4, 4), :], hb[:, :, :], 1e-5, signal=sem("hb_A"))
                note(dve.tensor_copy(xmean[:, ds(c * 4, 4)], mv[0][:, :, 0]))
                note(dve.tensor_copy(xrstd[:, ds(c * 4, 4)], rs[0][:, :]))

            def pass_ac(c, last):
                split("AC", c, 0)
                if not last:
                    norm_x(c + 1)
                split("AC", c, 1)
                stage_v(c, 0, "A", c * 3 + 3)
                split("AC", c, 2)
                split("AC", c, 3)
                stage_v(c, 1, "C", c * 4 + 3)
                stage_v(c, 2, "C", c * 4 + 4, rows["bv3"])

            dve.wait_ge(x_in, START + 64)
            norm_x(0)
            join()
            dve.wait_ge(sem("index_in"), START + 48)
            idx_b, tmp = region(6656, (M + R,)), region(7424, (M + R,))
            link(dve.tensor_copy(code[:, :], idx_i[:, 1, :]))
            link(dve.tensor_scalar(tmp, code[:, :], 0.0, float(S), ALU.is_lt, ALU.mult))
            link(dve.tensor_tensor(code[:, :], code[:, :], tmp, ALU.add))
            link(dve.tensor_copy(idx_b, idx_i[:, 0, :]))
            link(dve.tensor_scalar(tmp, idx_b, 0.0, None, ALU.is_equal))
            link(dve.tensor_scalar(idx_b, idx_b, -1.0, None, ALU.is_equal))
            link(dve.tensor_tensor(tmp, tmp, idx_b, ALU.add))
            link(dve.scalar_tensor_tensor(out=code[:, :], in0=code[:, :], scalar=1.0, in1=tmp,
                                          op0=ALU.add, op1=ALU.mult))
            for r in range(R):
                link(dve.tensor_scalar(mtmp, code[:, 0:M], code[:, M + r:M + r + 1], None, ALU.is_equal))
                link(dve.tensor_tensor(mtmp, mtmp, row_id, ALU.mult))
                link(dve.tensor_reduce(first_code[:, r:r + 1], mtmp, AX.X, ALU.min))
            link(dve.tensor_tensor(first_code[:, :], first_code[:, :], entry_id[:, :], ALU.is_equal))
            link(dve.tensor_tensor(first_code[:, :], first_code[:, :], code[:, M:M + R], ALU.mult))
            dve.wait_ge(weights_in, START + W_FIRST)
            with dve.Fori(0, NC - 1) as c:
                ch.loop(c, 14)
                pass_ac(c, False)
            ch.end(NC - 1)
            pass_ac(NC - 1, True)

            def attend(a, causal):
                ring_full, ring_free = sem(f"ring_full_{a}"), sem(f"ring_free_{a}")

                def entry(g, qp, k):
                    dve.wait_ge(ring_full, START + ring_base(causal, g, qp) + (k + 1))
                    return FIRST + k % RING

                def row_max(qp, b, tile):
                    j0, nj, q8, kb, n, _ = tile
                    dst = mxb[qp if causal else 0][:, :, kb].rearrange("p (j q) -> p j q", j=4)[:, j0:j0 + nj, q8]
                    dve.tensor_reduce(dst, ps[:, b, 0:nj * n].rearrange("p (j n) -> p j n", j=nj),
                                      AX.X, ALU.max).then_inc(ring_free, 1)

                def last_max(qp, uses):
                    dve.wait_ge(ring_free, START + uses)
                    dve.tensor_reduce(mx[:, :], mxb[qp if causal else 0][:, :, :], AX.X, ALU.max)\
                       .then_inc(sem(f"mx_ready_{a}"), 1)

                def split_maxima(before, b, uses):
                    dve.wait_ge(sem(f"max_out_{a}"), START + before * 48)
                    dve.wait_ge(sem(f"max_split_{a}"), START + before)
                    dve.tensor_scalar(mneg[:, :], ps[0:4 * WT, b, 0:P], -1.0, None, ALU.mult).then_inc(ring_free, 1)
                    dve.wait_ge(ring_free, START + uses)
                    link(dve.tensor_copy(mparts[:, 0, :], mneg[:, :]))
                    link(dve.tensor_tensor(mres[:, :], mneg[:, :], mparts[:, 0, :], ALU.subtract))
                    link(dve.tensor_copy(mparts[:, 1, :], mres[:, :]))
                    dve.tensor_tensor(mparts[:, 2, :], mres[:, :], mparts[:, 1, :], ALU.subtract)\
                       .then_inc(sem(f"max_split_{a}"), 1)

                def window(g, qp):
                    steps, after = steps_of(causal, qp), next_of(g, qp)
                    tiles = tiles_of(causal, after[1]) if after else []
                    where, turn_at = spread(causal, g, qp)
                    base = step_base(causal, g, qp)
                    end0 = sum(1 for s in steps if s[0] == 0)

                    def take_acc(h):
                        dve.wait_ge(sem(f"pv_{a}"), START + base + (end0 if h == 0 else len(steps)))
                        dve.tensor_copy(accS[:, h, :], ps[:, ACC, :]).then_inc(sem(f"acc_out_{a}"), 1)

                    def norm_acc(h, b):
                        qc = chunk_of(causal, qp, h)
                        acc = ps[:, b, :].rearrange("p (r j d) -> p r j d", r=R, d=32)
                        rec4 = rec[:, :].rearrange("p (r j) -> p r j", r=R)
                        link(dve.reciprocal(rec4, acc[:, :, :, D]))
                        dve.tensor_tensor(
                            o_sb[:, qc * R:qc * R + R, g * 64:g * 64 + 64].rearrange("p r (j d) -> p r j d", d=D),
                            acc[:, :, :, 0:D], rec4.unsqueeze(3).to_broadcast([P, R, 4, D]),
                            ALU.mult).then_inc(ring_free, 1)

                    k = 0
                    for t, (h, kt, c0, kn, _) in enumerate(steps):
                        todo = where[t]
                        for idx in (*todo[0], *todo[1]):
                            row_max(after[1], entry(g, qp, k), tiles[idx])
                            k += 1
                        if h == 1 and kt == 0:
                            take_acc(0)
                        if h == 1 and kt == 1:
                            norm_acc(0, entry(g, qp, k))
                            k += 1
                        for idx in todo[2]:
                            row_max(after[1], entry(g, qp, k), tiles[idx])
                            k += 1
                        if after and t == turn_at - 1:
                            last_max(after[1], ring_base(causal, g, qp) + k)
                        if after and t == turn_at:
                            split_maxima(after[1] + 2 * after[0], entry(g, qp, k), ring_base(causal, g, qp) + (k + 1))
                            k += 1
                    take_acc(1)
                    norm_acc(1, entry(g, qp, k))

                def maxima_alone():
                    tiles = tiles_of(causal, 0)
                    for k, tile in enumerate(tiles):
                        row_max(0, entry(-1, 0, k), tile)
                    last_max(0, ring_base(causal, -1, 0) + len(tiles))
                    split_maxima(0, entry(-1, 0, len(tiles)), ring_base(causal, -1, 0) + (len(tiles) + 1))

                maxima_alone()
                for g in range(NG):
                    for qp in range(2):
                        window(g, qp)
                dve.wait_ge(ring_free, START + ring_base(causal, NG - 1, 1) + 2)
                dve.memset(rec[:, 0:1], 0.0).then_inc(sem(f"normed_{a}"), 1)

            attend(1, True)
            dve.wait_ge(sem("later_in"), START + W_LATER)
            dve.wait_ge(sem("tanh_done"), START + 1)
            with dve.Fori(0, NC // 2) as c:
                ch.loop(c, 36)
                for u in range(2):
                    dve.wait_ge(sem(f"tr_B1_{u}"), START + c * 2 + 1)
                    at = c * 8 + 4 * u
                    for r in range(R):
                        note(dve.tensor_scalar(HB[u][:, r, :], x_sb[:, ds(at + r, 1), :].rearrange("p o e -> p (o e)"),
                                               xmean[:, ds(at + r, 1)], xrstd[:, ds(at + r, 1)],
                                               ALU.subtract, ALU.mult))
                    join()
                    dve.wait_ge(sem(f"relu1_{u}"), START + c + 1)
                    link(dve.tensor_tensor(Z_B1[u][:, :, :], Z_B1[u][:, :, :], HB[u][:, :, :], ALU.add))
                    ln_stats(Z_B1[u][:, :, :], 1e-6, u)
                for u in range(2):
                    ln_apply(ln_n("B1", c, u), Z_B1[u][:, :, :], HB[u][:, :, :], rows["g1"], rows["b1"],
                             sem(f"hb_B1_{u}"), u)
                for u in range(2):
                    split("B1", c, u)
            ch.end(NC // 2)
            attend(2, False)

            dve.wait_ge(sem("normed_2"), START + 1)
            for t in range(S // P):
                ins = dve.tensor_scalar(which[:, t, :], code[:, 0:M], tok_id[:, t:t + 1], None, ALU.is_equal)
                if t < S // P - 1:
                    note(ins)
            ins.then_inc(sem("gather_map"), 1)

            with dve.Fori(0, NC // 2) as c:
                ch.loop(c, 108)
                lanes = [(u, Z[u][:, :, :], Z2[u][:, :, :], HB[u][:, :, :], x_sb[:, ds(c * 8 + 4 * u, 4), :],
                          Z[u][:, :, 0:HF]) for u in range(2)]
                n = c * 8 + LNS["B2x"][0]
                for u, za, zb, h, xc, hid in lanes:
                    dve.wait_ge(sem(f"relu_{u}"), START + c * 2 + 1)
                    ln_stats(za, 0.25e-6, u)
                for u, za, zb, h, xc, hid in lanes:
                    dve.wait_ge(sem(f"tr_B2_{u}"), START + c * 4 + 1)
                    ln_apply(n + u, za, h, rows["g2"], rows["b2"], sem(f"hb_B2_{u}"), u)
                for u, za, zb, h, xc, hid in lanes:
                    dve.wait_ge(sem(f"relu_{u}"), START + c * 2 + 2)
                    link(dve.tensor_tensor(zb, za, h, ALU.add))
                    ln_stats(zb, 1e-6, u)
                for u, za, zb, h, xc, hid in lanes:
                    ln_apply(n + (2 + u), zb, zb, rows["g3"], rows["b3"], None, u)
                    link(dve.scalar_tensor_tensor(out=xc, in0=zb, scalar=tg[:, 0:1], in1=xc, op0=ALU.mult, op1=ALU.add))
                    ln_stats(xc, 1e-5, u)
                for u, za, zb, h, xc, hid in lanes:
                    dve.wait_ge(sem(f"tr_B2_{u}"), START + c * 4 + 2)
                    ln_apply(n + (4 + u), xc, h, None, None, sem(f"hb_B2_{u}"), u)
                for u, za, zb, h, xc, hid in lanes:
                    dve.wait_ge(sem(f"silu_{u}"), START + c + 1)
                    link(dve.tensor_tensor(hid, SG[u], chunk_banks(u)[:, :, HF:E], ALU.mult))
                    ln_stats(hid, 1e-5, u)
                for u, za, zb, h, xc, hid in lanes:
                    ln_apply(n + (6 + u), hid, hid, rows["slg"], rows["slb"], sem(f"hidden_{u}"), u)
            ch.end(NC // 2)
            hid = z[:, :, 0:HF]
            dve.wait_ge(sem("mm_MOE"), START + 2)
            logits = ps[:, 4, 0:R * 16].rearrange("p (r n) -> p r n", r=R)[:, :, 0:NE + 1]
            dve.tensor_tensor(sc[:, :, 0:NE + 1], logits, wide(rows["gateb"], NE + 1), ALU.add)\
               .then_inc(sem("gate_in"), 1)
            dve.wait_ge(sem("gates_out"), START + 1)
            io = iota8[:, :].unsqueeze(1).to_broadcast([P, R, NE])
            link(dve.tensor_tensor(sel[:, :, :], sc[:, :, 0:NE], wide(rows["expb"], NE), ALU.add))
            link(dve.tensor_reduce(small[:, 0, :], sel[:, :, :], AX.X, ALU.max))
            link(dve.tensor_tensor(oh[:, :, :], sel[:, :, :],
                                   small[:, 0, :].unsqueeze(2).to_broadcast([P, R, NE]), ALU.is_ge))
            link(dve.tensor_tensor(sel[:, :, :], oh[:, :, :], io, ALU.mult))
            link(dve.tensor_reduce(small[:, 1, :], sel[:, :, :], AX.X, ALU.min))
            dve.tensor_tensor(oh[:, :, :], io, small[:, 1, :].unsqueeze(2).to_broadcast([P, R, NE]),
                              ALU.is_equal).then_inc(sem("onehot"), 1)
            dve.wait_ge(sem("onehot"), START + 1)
            link(dve.tensor_tensor(sel[:, :, :], oh[:, :, :], sc[:, :, 0:NE], ALU.mult))
            link(dve.tensor_reduce(small[:, 5, :], sel[:, :, :], AX.X, ALU.add))
            dve.tensor_tensor(small[:, 2, :], sc[:, :, NE], small[:, 5, :], ALU.subtract)\
               .then_inc(sem("gate_diff"), 1)
            dve.wait_ge(sem("token_row"), START + 1)
            for m in range(R):
                ins = dve.tensor_scalar(where_to[:, m, :], where_to[:, m, :], first_code[:, m:m + 1], None, ALU.is_equal)
                if m < R - 1:
                    note(ins)
            ins.then_inc(sem("scatter_map"), 1)
            dve.wait_ge(sem("gates_out"), START + 3)
            link(dve.tensor_scalar(vals[:, :, E], small[:, 3, :], -1.0, None, ALU.add))
            dve.wait_ge(sem("bias_moe"), START + 2)
            for r in range(R):
                dve.wait_ge(sem("mm_MOE"), START + (3, 5, 6, 7)[r])
                up = ps[:, 4 * (r % 2):4 * (r % 2) + 4, :].rearrange("p (u b) (e h) -> p u (b e) h", u=2, h=HF)
                acc = hs[:, r, :].rearrange("p (u h) -> p u h", u=2)
                for e in range(NE):
                    start = bsel[:, r, 0:2 * HF].rearrange("p (u h) -> p u h", u=2)
                    ins = dve.scalar_tensor_tensor(out=acc, in0=up[:, :, e, :], scalar=oh[:, r, e:e + 1],
                                                   in1=acc if e else start, op0=ALU.mult, op1=ALU.add)
                    if e < NE - 1:
                        link(ins)
                ins.then_inc(sem("picked"), 1)
            dve.wait_ge(sem("silu_moe"), START + 1)
            link(dve.tensor_tensor(hid, SG[0], hs[:, :, HF:2 * HF], ALU.mult))
            layernorm("MOE", 0, 0, hid, hid, 1e-5, rows["elg"], rows["elb"], signal=sem("hidden_moe"))
            for r in range(R):
                dve.wait_ge(sem("mm_MOE"), START + 8 + r)
                down = ps[:, 4 * (r % 2):4 * (r % 2) + 4, :].rearrange("p b (e n) -> p (b e) n", n=E)
                for e in range(NE):
                    ins = dve.scalar_tensor_tensor(out=vals[:, r, 0:E], in0=down[:, e, :], scalar=oh[:, r, e:e + 1],
                                                   in1=vals[:, r, 0:E] if e else bsel[:, r, 2 * HF:2 * HF + E],
                                                   op0=ALU.mult, op1=ALU.add)
                    if e < NE - 1:
                        link(ins)
                ins.then_inc(sem("expert_out"), 1)
            dve.wait_ge(sem("expert_out"), START + R)
            for r in range(R):
                ins = dve.tensor_scalar(vals[:, r, 0:E], vals[:, r, 0:E], small[:, 4, r:r + 1], None, ALU.mult)
                if r < R - 1:
                    note(ins)
            ins.then_inc(sem("entries"), 1)
            for c in range(NC):
                xc = x_sb[:, 4 * c:4 * c + 4, :]
                b = 4 * (c % 2)
                dve.wait_ge(sem("scattered"), START + c + 1)
                link(dve.tensor_scalar(small[:, 6, :], ps[:, b:b + 4, E], 1.0, None, ALU.add))
                for r in range(R):
                    ins = dve.scalar_tensor_tensor(out=z[:, r, :], in0=shr[:, R * c + r, :], scalar=small[:, 6, r:r + 1],
                                                   in1=ps[:, b + r, 0:E], op0=ALU.mult, op1=ALU.add)
                    if r < R - 1:
                        note(ins)
                ins.then_inc(sem("merged"), 1)
                dve.wait_ge(sem("merged"), START + c + 1)
                link(dve.scalar_tensor_tensor(out=xc, in0=z[:, :, :], scalar=tg[:, 2:3], in1=xc,
                                              op0=ALU.mult, op1=ALU.add))
            with dve.Fori(0, NC // 2) as c:
                ch.loop(c, 22)
                for u in range(2):
                    ln_stats(x_sb[:, ds(c * 8 + 4 * u, 4), :], 1e-5, u)
                for u in range(2):
                    dve.wait_ge(sem(f"tr_Q3_{u}"), START + c)
                    ln_apply(ln_n("Q3", c, u), x_sb[:, ds(c * 8 + 4 * u, 4), :], HB[u][:, :, :],
                             signal=sem(f"hb_Q3_{u}"), u=u)
                for u in range(2):
                    split("Q3", c, u)
            ch.end(NC // 2)
            attend(3, False)
            with dve.Fori(0, NC // 2) as c:
                for u in range(2):
                    dve.wait_ge(sem(f"mm_O3_{u}"), START + c + 1)
                    xc = x_sb[:, ds(c * 8 + 4 * u, 4), :]
                    dve.scalar_tensor_tensor(out=xc, in0=chunk_banks(u), scalar=tg[:, 1:2], in1=xc,
                                             op0=ALU.mult, op1=ALU.add).then_inc(sem(f"added_{u}"), 1)
            for u in range(2):
                dve.wait_ge(sem(f"added_{u}"), START + NC // 2)

            ln_stats(x_sb[:, 0:4, :], 1e-5)
            ln_apply(ln_n("B3", 0, 0), x_sb[:, 0:4, :], hb[:, :, :], signal=sem("hb_B3"))
            dve.wait_ge(sem("fw_in"), START + 48)
            for u in range(2):
                dve.tensor_scalar(wgu[:, u, :, :], wint[:, u, :, :], 1.0 / 127.0, None, ALU.mult)\
                   .then_inc(sem("fw_ready"), 1)
            dve.tensor_scalar(wd, dint, 1.0 / 127.0, None, ALU.mult).then_inc(sem("fw_ready"), 1)

            def feed_forward(c, last):
                for f in range(FF // P):
                    dve.wait_ge(sem("mm_B3"), START + c * 7 + (f + 1))
                    dve.wait_ge(sem("silu_3"), START + c * 6 + (f + 1))
                    dve.tensor_tensor(hT[:, f, :], sgT[:, f % 2, :], ps[:, 3 + 2 * (f % 2), :], ALU.mult)\
                       .then_inc(sem("up_done"), 1)
                    if f == 1 and not last:
                        ln_stats(x_sb[:, ds(c * 4 + 4, 4), :], 1e-5)
                    if f == 3 and not last:
                        dve.wait_ge(sem("tr_B3"), START + c + 1)
                        ln_apply(ln_n("B3", c + 1, 0), x_sb[:, ds(c * 4 + 4, 4), :], hb[:, :, :],
                                 signal=sem("hb_B3"))
                dve.wait_ge(sem("mm_B3"), START + c * 7 + 7)
                xc = x_sb[:, ds(c * 4, 4), :]
                dve.scalar_tensor_tensor(out=xc, in0=chunk6(), scalar=tg[:, 3:4], in1=xc, op0=ALU.mult, op1=ALU.add)\
                   .then_inc(sem("down_done"), 1)

            with dve.Fori(0, NC - 1) as c:
                ch.loop(c, 11)
                feed_forward(c, False)
            ch.end(NC - 1)
            feed_forward(NC - 1, True)


_NAMES = {
    "wk1": "L0_xattn_Wk1", "wv1": "L0_xattn_Wv1", "wq1": "L0_xattn_Wq1", "wk2": "L0_xattn_Wk2",
    "wv2": "L0_xattn_Wv2", "wq2": "L0_xattn_Wq2", "wo1": "L0_xattn_Wo1", "wo2": "L0_xattn_Wo2",
    "wf": "L0_xattn_Wf", "bo1": "L0_xattn_bo1", "bo2": "L0_xattn_bo2", "bf": "L0_xattn_bf",
    "g1": "L0_xattn_g1", "b1": "L0_xattn_b1", "g2": "L0_xattn_g2", "b2": "L0_xattn_b2", "g3": "L0_xattn_g3",
    "b3": "L0_xattn_b3", "sb3": "L0_ffn_sb3", "slg": "L0_ffn_s_ln_g", "slb": "L0_ffn_s_ln_b",
    "elg": "L0_ffn_sel_ln_g", "elb": "L0_ffn_sel_ln_b", "expb": "L0_ffn_exp_bias",
    "index_b": "L0_ffn_index_b", "index_t": "L0_ffn_index_t",
    "wq3": "L1_xattn_Wq", "bq3": "L1_xattn_bq", "wk3": "L1_xattn_Wk", "bk3": "L1_xattn_bk",
    "wv3": "L1_xattn_Wv", "bv3": "L1_xattn_bv", "wo3": "L1_xattn_Wo", "bo3": "L1_xattn_bo",
    "x": "x", "ctx": "ctx_1024",
}


def lay_out(inputs):
    import numpy as np
    a = {k: np.asarray(inputs[v]) for k, v in _NAMES.items()}
    for n in ("wk1", "wv1", "wq1", "wk2", "wv2", "wq2"):
        a[n] = a[n].transpose(1, 0, 2).reshape(E, E)
    for n in ("bq3", "bk3"):
        a[n] = a[n].reshape(2, P).T
    f = {k: np.asarray(inputs["L0_ffn_" + k]) for k in
         ("sw1", "sw2", "sw3", "sb1", "sb2", "sg_w", "sg_b", "eg_w", "eg_b", "ew1", "ew2", "ew3", "eb1", "eb2", "eb3")}
    a["sw12"] = np.concatenate([f["sw1"].T, f["sw2"].T], axis=1)
    a["sb12"] = np.concatenate([f["sb1"], f["sb2"]])
    a["sw3"] = f["sw3"].T
    a["gate_w"] = np.concatenate([f["eg_w"].T, f["sg_w"].T], axis=1)
    a["gateb"] = np.concatenate([f["eg_b"], f["sg_b"]])
    a["ew12"] = np.concatenate([f["ew1"].reshape(NE * HF, E).T, f["ew2"].reshape(NE * HF, E).T], axis=1)
    a["ew3"] = f["ew3"].transpose(2, 0, 1).reshape(HF, NE * E)
    a["eb"] = np.concatenate([f["eb1"], f["eb2"], f["eb3"]], axis=1)
    a["index_col"] = np.stack([a["index_b"], a["index_t"]]).reshape(2, R, P).transpose(2, 0, 1)
    a["gates"] = np.concatenate([np.asarray(inputs["g_xattn"]), np.asarray(inputs["g_ffn"])])
    a["w_gate"] = np.asarray(inputs["L1_ffn_w_gate"]).T
    a["w_up"] = np.asarray(inputs["L1_ffn_w_up"]).T
    a["w_down"] = np.asarray(inputs["L1_ffn_w_down"]).T
    return {k: np.ascontiguousarray(v) for k, v in a.items()}


def kernel(**inputs):
    import concourse.bacc as _bacc
    from concourse import mybir as _mybir
    from concourse.bass_utils import run_bass_kernel_spmd as _run

    nc = _bacc.Bacc("TRN2", target_bir_lowering=False, num_devices=1)
    arrays, A = {}, {}
    for name, a in lay_out(inputs).items():
        arrays[f"in_{name}"] = a
        A[name] = nc.dram_tensor(f"in_{name}", a.shape, _mybir.dt.from_np(a.dtype), kind="ExternalInput").ap()
    out = nc.dram_tensor("out_0", (1, S, E), _mybir.dt.float32, kind="ExternalOutput").ap()
    build(nc, A, out)
    r = _run(nc, [arrays], core_ids=[0])
    return r.results[0]["out_0"]
```
